# Optimizing a Trainium2 kernel written in Bass

```python
import numpy as np
import jax
import jax.numpy as jnp

def _softmax(x, axis=-1):
    return jax.nn.softmax(x, axis=axis)

def _gelu(x):
    return jax.nn.gelu(x, approximate=True)

def _silu(x):
    return jax.nn.silu(x)

def _sigmoid(x):
    return jax.nn.sigmoid(x)

def _layernorm(x, axis=-1, eps=1e-05):
    m = jnp.mean(x, axis=axis, keepdims=True)
    v = jnp.var(x, axis=axis, keepdims=True)
    return (x - m) / jnp.sqrt(v + eps)

def _scatter_add(tgt, idx, src, axis=0):
    return tgt.at[idx].add(src)

def _segment_sum(src, seg, n):
    return jax.ops.segment_sum(src, seg, n)
kernel_name = 'mk_seq_postln_d2_jaxref_r8_0ca6f2'

def setup_inputs(seed: int=0):
    np.random.seed(seed)
    _w = jnp.asarray

    def _L0_attn_setup():
        import jax, jax.numpy as jnp
        import numpy as np
        import math
        EMBED_DIM = 128
        NUM_HEADS = 16
        HEAD_DIM = EMBED_DIM // NUM_HEADS
        key = jax.random.key(seed)
        ks = jax.random.split(key, 5)
        B, S, D = (2, 256, EMBED_DIM)
        s = 1.0 / math.sqrt(D)
        x = jax.random.normal(ks[0], (B, S, D), dtype=jnp.float32)
        W_qkv = jax.random.normal(ks[1], (3 * D, D), dtype=jnp.float32) * s
        b_qkv = jax.random.normal(ks[2], (3 * D,), dtype=jnp.float32) * 0.01
        W_out = jax.random.normal(ks[3], (D, D), dtype=jnp.float32) * s
        b_out = jax.random.normal(ks[4], (D,), dtype=jnp.float32) * 0.01
        return {'x': x, 'W_qkv': W_qkv, 'b_qkv': b_qkv, 'W_out': W_out, 'b_out': b_out}
    _L0_attn_in = _L0_attn_setup()

    def _L0_ffn_setup():
        import jax, jax.numpy as jnp
        import numpy as np
        BLOCK = 16
        _GRID = jnp.array([0.0, 0.5, 1.0, 1.5, 2.0, 3.0, 4.0, 6.0], dtype=jnp.float32)
        _MID = jnp.array([0.25, 0.75, 1.25, 1.75, 2.5, 3.5, 5.0], dtype=jnp.float32)

        def fp4_quant_dequant(x):
            shape = x.shape
            xb = x.reshape(shape[:-1] + (shape[-1] // BLOCK, BLOCK))
            scale = jnp.max(jnp.abs(xb), axis=-1, keepdims=True) / 6.0
            scale = jnp.maximum(scale, jnp.float32(1e-12))
            xn = xb / scale
            idx = jnp.searchsorted(_MID, jnp.abs(xn))
            q = _GRID[idx] * jnp.sign(xn) * scale
            return q.reshape(shape)

        def fp4_linear(x, w):
            xq = fp4_quant_dequant(x)
            wq = fp4_quant_dequant(w)
            return jnp.einsum('bsk,nk->bsn', xq, wq)
        key = jax.random.key(seed)
        k1, k2, k3, k4 = jax.random.split(key, 4)
        H, I = (128, 352)
        x = jax.random.normal(k1, (4, 512, H), dtype=jnp.float32)
        w_gate = jax.random.normal(k2, (I, H), dtype=jnp.float32) * 0.02
        w_up = jax.random.normal(k3, (I, H), dtype=jnp.float32) * 0.02
        w_down = jax.random.normal(k4, (H, I), dtype=jnp.float32) * 0.02
        return {'x': x, 'w_gate': w_gate, 'w_up': w_up, 'w_down': w_down}
    _L0_ffn_in = _L0_ffn_setup()

    def _L1_attn_setup():
        import jax, jax.numpy as jnp
        import numpy as np
        DIM = 128
        NUM_HEADS = 16
        HEAD_DIM = DIM // NUM_HEADS
        SCALE = HEAD_DIM ** (-0.5)
        key = jax.random.key(seed)
        k_x, k_wq, k_bq, k_wp, k_bp = jax.random.split(key, 5)
        x = jax.random.normal(k_x, (2, 256, DIM), dtype=jnp.float32)
        W_qkv = jax.random.normal(k_wq, (3 * DIM, DIM), dtype=jnp.float32) * DIM ** (-0.5)
        b_qkv = jax.random.normal(k_bq, (3 * DIM,), dtype=jnp.float32) * 0.02
        W_proj = jax.random.normal(k_wp, (DIM, DIM), dtype=jnp.float32) * DIM ** (-0.5)
        b_proj = jax.random.normal(k_bp, (DIM,), dtype=jnp.float32) * 0.02
        return {'x': x, 'W_qkv': W_qkv, 'b_qkv': b_qkv, 'W_proj': W_proj, 'b_proj': b_proj}
    _L1_attn_in = _L1_attn_setup()

    def _L1_ffn_setup():
        import jax, jax.numpy as jnp
        import numpy as np
        DIM = 128
        DEPTH = 2
        HEADS = 8
        DIM_HEAD = 64
        WINDOW = 64
        INNER = HEADS * DIM_HEAD
        HID = int(DIM * 4 * 2 / 3)
        B, N = (2, 1024)
        QK_SCALE = 8.0

        def shift_token(t):
            t1, t2 = jnp.split(t, 2, axis=-1)
            t2 = jnp.pad(t2, ((0, 0), (1, 0), (0, 0)))[:, :-1]
            return jnp.concatenate([t1, t2], axis=-1)

        def l2norm(t):
            return t / jnp.clip(jnp.linalg.norm(t, axis=-1, keepdims=True), 1e-12)

        def rotate_half(x):
            x1, x2 = jnp.split(x, 2, axis=-1)
            return jnp.concatenate([-x2, x1], axis=-1)

        def rotary_xpos(q, k):
            n = q.shape[-2]
            half_idx = jnp.arange(0, DIM_HEAD, 2, dtype=jnp.float32)
            inv_freq = 1.0 / 10000.0 ** (half_idx / DIM_HEAD)
            t = jnp.arange(n, dtype=jnp.float32)
            freqs = t[:, None] * inv_freq[None, :]
            freqs = jnp.concatenate([freqs, freqs], axis=-1)
            base = (half_idx + 0.4 * DIM_HEAD) / (1.4 * DIM_HEAD)
            power = (t - n // 2) / float(WINDOW // 2)
            scale = base[None, :] ** power[:, None]
            scale = jnp.concatenate([scale, scale], axis=-1)
            cos, sin = (jnp.cos(freqs), jnp.sin(freqs))
            q = q * cos * scale + rotate_half(q) * sin * scale
            k = k * cos / scale + rotate_half(k) * sin / scale
            return (q, k)

        def local_attention(q, k, v):
            b, h, n, d = q.shape
            w = n // WINDOW
            bq = q.reshape(b, h, w, WINDOW, d) * QK_SCALE
            bk = k.reshape(b, h, w, WINDOW, d)
            bv = v.reshape(b, h, w, WINDOW, d)

            def look_around(t):
                p = jnp.pad(t, ((0, 0), (0, 0), (1, 0), (0, 0), (0, 0)))
                return jnp.concatenate([p[:, :, :w], p[:, :, 1:]], axis=3)
            bk, bv = (look_around(bk), look_around(bv))
            bt = jnp.arange(n).reshape(w, WINDOW)
            btp = jnp.pad(bt, ((1, 0), (0, 0)), constant_values=-1)
            btk = jnp.concatenate([btp[:w], btp[1:]], axis=1)
            sim = jnp.einsum('bhwid,bhwjd->bhwij', bq, bk)
            i = bt[:, :, None]
            j = btk[:, None, :]
            mask = (i < j) | (i > j + WINDOW) | (j == -1)
            sim = jnp.where(mask, -jnp.finfo(sim.dtype).max, sim)
            attn = jax.nn.softmax(sim, axis=-1)
            out = jnp.einsum('bhwij,bhwjd->bhwid', attn, bv)
            return out.reshape(b, h, n, d)

        def _layer(x, wqkv, qs, ksc, wo, lg, lb, w1, b1, w2, b2):
            b, n, _ = x.shape
            h = shift_token(x)
            qkv = h @ wqkv
            q, k, v = jnp.split(qkv, 3, axis=-1)
            to_heads = lambda t: t.reshape(b, n, HEADS, DIM_HEAD).transpose(0, 2, 1, 3)
            q, k, v = (to_heads(q), to_heads(k), to_heads(v))
            q = l2norm(q) * qs
            k = l2norm(k) * ksc
            q, k = rotary_xpos(q, k)
            o = local_attention(q, k, v)
            o = o.transpose(0, 2, 1, 3).reshape(b, n, INNER)
            x = x + o @ wo
            h = shift_token(x)
            mu = h.mean(-1, keepdims=True)
            var = h.var(-1, keepdims=True)
            h = (h - mu) / jnp.sqrt(var + 1e-05) * lg + lb
            h = h @ w1 + b1
            a, g = jnp.split(h, 2, axis=-1)
            h = a * jax.nn.gelu(g, approximate=False)
            x = x + h @ w2 + b2
            return x
        key = jax.random.key(seed)
        ks = jax.random.split(key, 6)
        return {'x': jax.random.normal(ks[0], (B, N, DIM), jnp.float32), 'wqkv': jax.random.normal(ks[1], (DEPTH, DIM, 3 * INNER), jnp.float32) * 0.02, 'q_scale': jnp.ones((DEPTH, DIM_HEAD), jnp.float32), 'k_scale': jnp.ones((DEPTH, DIM_HEAD), jnp.float32), 'wo': jax.random.normal(ks[2], (DEPTH, INNER, DIM), jnp.float32) * 0.02, 'ln_g': jnp.ones((DEPTH, DIM), jnp.float32), 'ln_b': jnp.zeros((DEPTH, DIM), jnp.float32), 'w1': jax.random.normal(ks[3], (DEPTH, DIM, 2 * HID), jnp.float32) * 0.02, 'b1': jnp.zeros((DEPTH, 2 * HID), jnp.float32), 'w2': jax.random.normal(ks[4], (DEPTH, HID, DIM), jnp.float32) * 0.02, 'b2': jnp.zeros((DEPTH, DIM), jnp.float32)}
    _L1_ffn_in = _L1_ffn_setup()
    _d = {'L0_attn_x': _L0_attn_in['x'], 'L0_attn_W_qkv': _L0_attn_in['W_qkv'], 'L0_attn_b_qkv': _L0_attn_in['b_qkv'], 'L0_attn_W_out': _L0_attn_in['W_out'], 'L0_attn_b_out': _L0_attn_in['b_out'], 'L0_ffn_w_gate': _L0_ffn_in['w_gate'], 'L0_ffn_w_up': _L0_ffn_in['w_up'], 'L0_ffn_w_down': _L0_ffn_in['w_down'], 'L1_attn_W_qkv': _L1_attn_in['W_qkv'], 'L1_attn_b_qkv': _L1_attn_in['b_qkv'], 'L1_attn_W_proj': _L1_attn_in['W_proj'], 'L1_attn_b_proj': _L1_attn_in['b_proj'], 'L1_ffn_wqkv': _L1_ffn_in['wqkv'], 'L1_ffn_q_scale': _L1_ffn_in['q_scale'], 'L1_ffn_k_scale': _L1_ffn_in['k_scale'], 'L1_ffn_wo': _L1_ffn_in['wo'], 'L1_ffn_ln_g': _L1_ffn_in['ln_g'], 'L1_ffn_ln_b': _L1_ffn_in['ln_b'], 'L1_ffn_w1': _L1_ffn_in['w1'], 'L1_ffn_b1': _L1_ffn_in['b1'], 'L1_ffn_w2': _L1_ffn_in['w2'], 'L1_ffn_b2': _L1_ffn_in['b2']}
    _x0 = _d['L0_attn_x']
    _d['L0_attn_x'] = jax.random.normal(jax.random.fold_in(jax.random.key(seed), 1), (8, 512, 128), dtype=_x0.dtype)
    del _x0
    return _d

def reference(L0_attn_x, L0_attn_W_qkv, L0_attn_b_qkv, L0_attn_W_out, L0_attn_b_out, L0_ffn_w_gate, L0_ffn_w_up, L0_ffn_w_down, L1_attn_W_qkv, L1_attn_b_qkv, L1_attn_W_proj, L1_attn_b_proj, L1_ffn_wqkv, L1_ffn_q_scale, L1_ffn_k_scale, L1_ffn_wo, L1_ffn_ln_g, L1_ffn_ln_b, L1_ffn_w1, L1_ffn_b1, L1_ffn_w2, L1_ffn_b2):

    def _L0_attn_ref(x, W_qkv, b_qkv, W_out, b_out):
        import jax, jax.numpy as jnp
        import numpy as np
        import math
        EMBED_DIM = 128
        NUM_HEADS = 16
        HEAD_DIM = EMBED_DIM // NUM_HEADS
        B, S, D = x.shape
        H, Hd = (NUM_HEADS, HEAD_DIM)
        slopes = jnp.power(2.0, 8.0 * jnp.arange(0, -H, -1, dtype=jnp.float32) / H)
        qkv = x @ W_qkv.T + b_qkv
        qkv = qkv.reshape(B, S, 3, H, Hd).transpose(2, 0, 3, 1, 4)
        q, k, v = (qkv[0], qkv[1], qkv[2])
        scores = jnp.einsum('bhqd,bhkd->bhqk', q, k) / math.sqrt(Hd)
        pos = jnp.arange(S)
        rel = jnp.abs(pos[None, :] - pos[:, None]).astype(jnp.float32)
        bias = -slopes[:, None, None] * rel
        probs = jax.nn.softmax(scores + bias[None], axis=-1)
        out = jnp.einsum('bhqk,bhkd->bhqd', probs, v)
        out = out.transpose(0, 2, 1, 3).reshape(B, S, D)
        return out @ W_out.T + b_out

    def _L0_ffn_ref(x, w_gate, w_up, w_down):
        import jax, jax.numpy as jnp
        import numpy as np
        BLOCK = 16
        _GRID = jnp.array([0.0, 0.5, 1.0, 1.5, 2.0, 3.0, 4.0, 6.0], dtype=jnp.float32)
        _MID = jnp.array([0.25, 0.75, 1.25, 1.75, 2.5, 3.5, 5.0], dtype=jnp.float32)

        def fp4_quant_dequant(x):
            shape = x.shape
            xb = x.reshape(shape[:-1] + (shape[-1] // BLOCK, BLOCK))
            scale = jnp.max(jnp.abs(xb), axis=-1, keepdims=True) / 6.0
            scale = jnp.maximum(scale, jnp.float32(1e-12))
            xn = xb / scale
            idx = jnp.searchsorted(_MID, jnp.abs(xn))
            q = _GRID[idx] * jnp.sign(xn) * scale
            return q.reshape(shape)

        def fp4_linear(x, w):
            xq = fp4_quant_dequant(x)
            wq = fp4_quant_dequant(w)
            return jnp.einsum('bsk,nk->bsn', xq, wq)
        gate = fp4_linear(x, w_gate)
        y = fp4_linear(x, w_up)
        h = jax.nn.silu(gate) * y
        return fp4_linear(h, w_down)

    def _L1_attn_ref(x, W_qkv, b_qkv, W_proj, b_proj):
        import jax, jax.numpy as jnp
        import numpy as np
        DIM = 128
        NUM_HEADS = 16
        HEAD_DIM = DIM // NUM_HEADS
        SCALE = HEAD_DIM ** (-0.5)
        B, N, C = x.shape
        qkv = x @ W_qkv.T + b_qkv
        q, k, v = jnp.split(qkv, 3, axis=-1)

        def heads(t):
            return t.reshape(B, N, NUM_HEADS, HEAD_DIM).transpose(0, 2, 1, 3)
        q, k, v = (heads(q), heads(k), heads(v))
        attn = jnp.einsum('bhnd,bhmd->bhnm', q, k) * SCALE
        attn = jax.nn.softmax(attn, axis=-1)
        out = jnp.einsum('bhnm,bhmd->bhnd', attn, v)
        out = out.transpose(0, 2, 1, 3).reshape(B, N, C)
        return out @ W_proj.T + b_proj

    def _L1_ffn_ref(x, wqkv, q_scale, k_scale, wo, ln_g, ln_b, w1, b1, w2, b2):
        import jax, jax.numpy as jnp
        import numpy as np
        DIM = 128
        DEPTH = 2
        HEADS = 8
        DIM_HEAD = 64
        WINDOW = 64
        INNER = HEADS * DIM_HEAD
        HID = int(DIM * 4 * 2 / 3)
        B, N = (2, 1024)
        QK_SCALE = 8.0

        def shift_token(t):
            t1, t2 = jnp.split(t, 2, axis=-1)
            t2 = jnp.pad(t2, ((0, 0), (1, 0), (0, 0)))[:, :-1]
            return jnp.concatenate([t1, t2], axis=-1)

        def l2norm(t):
            return t / jnp.clip(jnp.linalg.norm(t, axis=-1, keepdims=True), 1e-12)

        def rotate_half(x):
            x1, x2 = jnp.split(x, 2, axis=-1)
            return jnp.concatenate([-x2, x1], axis=-1)

        def rotary_xpos(q, k):
            n = q.shape[-2]
            half_idx = jnp.arange(0, DIM_HEAD, 2, dtype=jnp.float32)
            inv_freq = 1.0 / 10000.0 ** (half_idx / DIM_HEAD)
            t = jnp.arange(n, dtype=jnp.float32)
            freqs = t[:, None] * inv_freq[None, :]
            freqs = jnp.concatenate([freqs, freqs], axis=-1)
            base = (half_idx + 0.4 * DIM_HEAD) / (1.4 * DIM_HEAD)
            power = (t - n // 2) / float(WINDOW // 2)
            scale = base[None, :] ** power[:, None]
            scale = jnp.concatenate([scale, scale], axis=-1)
            cos, sin = (jnp.cos(freqs), jnp.sin(freqs))
            q = q * cos * scale + rotate_half(q) * sin * scale
            k = k * cos / scale + rotate_half(k) * sin / scale
            return (q, k)

        def local_attention(q, k, v):
            b, h, n, d = q.shape
            w = n // WINDOW
            bq = q.reshape(b, h, w, WINDOW, d) * QK_SCALE
            bk = k.reshape(b, h, w, WINDOW, d)
            bv = v.reshape(b, h, w, WINDOW, d)

            def look_around(t):
                p = jnp.pad(t, ((0, 0), (0, 0), (1, 0), (0, 0), (0, 0)))
                return jnp.concatenate([p[:, :, :w], p[:, :, 1:]], axis=3)
            bk, bv = (look_around(bk), look_around(bv))
            bt = jnp.arange(n).reshape(w, WINDOW)
            btp = jnp.pad(bt, ((1, 0), (0, 0)), constant_values=-1)
            btk = jnp.concatenate([btp[:w], btp[1:]], axis=1)
            sim = jnp.einsum('bhwid,bhwjd->bhwij', bq, bk)
            i = bt[:, :, None]
            j = btk[:, None, :]
            mask = (i < j) | (i > j + WINDOW) | (j == -1)
            sim = jnp.where(mask, -jnp.finfo(sim.dtype).max, sim)
            attn = jax.nn.softmax(sim, axis=-1)
            out = jnp.einsum('bhwij,bhwjd->bhwid', attn, bv)
            return out.reshape(b, h, n, d)

        def _layer(x, wqkv, qs, ksc, wo, lg, lb, w1, b1, w2, b2):
            b, n, _ = x.shape
            h = shift_token(x)
            qkv = h @ wqkv
            q, k, v = jnp.split(qkv, 3, axis=-1)
            to_heads = lambda t: t.reshape(b, n, HEADS, DIM_HEAD).transpose(0, 2, 1, 3)
            q, k, v = (to_heads(q), to_heads(k), to_heads(v))
            q = l2norm(q) * qs
            k = l2norm(k) * ksc
            q, k = rotary_xpos(q, k)
            o = local_attention(q, k, v)
            o = o.transpose(0, 2, 1, 3).reshape(b, n, INNER)
            x = x + o @ wo
            h = shift_token(x)
            mu = h.mean(-1, keepdims=True)
            var = h.var(-1, keepdims=True)
            h = (h - mu) / jnp.sqrt(var + 1e-05) * lg + lb
            h = h @ w1 + b1
            a, g = jnp.split(h, 2, axis=-1)
            h = a * jax.nn.gelu(g, approximate=False)
            x = x + h @ w2 + b2
            return x
        for l in range(DEPTH):
            x = _layer(x, wqkv[l], q_scale[l], k_scale[l], wo[l], ln_g[l], ln_b[l], w1[l], b1[l], w2[l], b2[l])
        return x
    x = L0_attn_x
    x = _layernorm(x + _L0_attn_ref(x, L0_attn_W_qkv, L0_attn_b_qkv, L0_attn_W_out, L0_attn_b_out), axis=-1)
    x = _layernorm(x + _L0_ffn_ref(x, L0_ffn_w_gate, L0_ffn_w_up, L0_ffn_w_down), axis=-1)
    x = _layernorm(x + _L1_attn_ref(x, L1_attn_W_qkv, L1_attn_b_qkv, L1_attn_W_proj, L1_attn_b_proj), axis=-1)
    x = _layernorm(x + _L1_ffn_ref(x, L1_ffn_wqkv, L1_ffn_q_scale, L1_ffn_k_scale, L1_ffn_wo, L1_ffn_ln_g, L1_ffn_ln_b, L1_ffn_w1, L1_ffn_b1, L1_ffn_w2, L1_ffn_b2), axis=-1)
    return x

_drawn_inputs = setup_inputs


def setup_inputs(seed=0):
    import zlib

    import numpy as np

    out = dict(_drawn_inputs(seed))
    spreads = {'L1_ffn_q_scale': (1.0, 0.6),
     'L1_ffn_k_scale': (1.0, 0.6),
     'L1_ffn_ln_g': (1.0, 0.6),
     'L1_ffn_ln_b': (0.0, 0.8),
     'L1_ffn_b1': (0.0, 0.8),
     'L1_ffn_b2': (0.0, 0.531)}
    factors = {'L0_attn_b_qkv': 3.945,
     'L0_attn_b_out': 4.334,
     'L0_ffn_w_gate': 5.707,
     'L0_ffn_w_up': 5.554,
     'L0_ffn_w_down': 5.59,
     'L1_attn_b_proj': 2.858,
     'L1_ffn_wqkv': 3.085,
     'L1_ffn_wo': 3.101,
     'L1_ffn_w1': 6.599,
     'L1_ffn_w2': 6.471}
    for name, (base, spread) in spreads.items():
        noise = np.random.default_rng([zlib.crc32(name.encode()), seed]).standard_normal(out[name].shape)
        drawn = base * np.exp(spread * noise) if base else spread * noise
        out[name] = jnp.asarray(drawn.astype(out[name].dtype))
    for name, factor in factors.items():
        out[name] = (out[name] * factor).astype(out[name].dtype)
    return out
```

```python
from contextlib import ExitStack

import concourse.bass as bass
from concourse import mybir

F32 = mybir.dt.float32
BF16 = mybir.dt.bfloat16
ALU = mybir.AluOpType
ACT = mybir.ActivationFunctionType
AX = mybir.AxisListType.X

P = 128
SEQS, S, D = 8, 512, 128
T = S // P
H, HD = 16, 8
PAIRS, QUADS = H // 2, H // 4
SLOTS = 64
INTER = 352
ICH = [(0, 128), (128, 128), (256, 96)]
FB = 16
LAYERS, LH, LD = 2, 8, 64
WIN = 64
BAND = P + WIN
HID = 341
HCH = [(0, 128), (128, 128), (256, 85)]
EPS = 1e-5
Q_PART = [0, 0, 1, 1, 0, 2]
K_PART = [0, 1, 0, 1, 2, 0]
M_SLOT = 8 * len(Q_PART)


def psum_order():
    items = []
    for a in range(2):
        items += [(a, "xT")] + [(a, "qkv", i) for i in range(2)] + [(a, "qkT", g) for g in range(QUADS)]
        for kind, i in attention_order():
            items += [(a, kind) + i]
        items += [(a, "aT"), (a, "proj")]
        if a == 0:
            items += [("f", "xqT")] + [("f", "gu", t) for t in range(T)]
            items += [("f", "hT", c) for c in range(3)] + [("f", "down")]
    for l in range(LAYERS):
        items += [("l", l, "xT")]
        items += [("l", l) + i for i in LOCAL_FRONT]
        items += [("l", l, "s1", t, q) for t in range(T) for q in range(2)]
        items += [("l", l, "mT")]
        for t in range(T):
            items += [("l", l, "s2", t, q) for q in range(2)]
            if t:
                items += [("l", l, "pv", t - 1)]
        items += [("l", l, "pv", T - 1)]
        items += [("l", l, "oT", i) for i in range(2)] + [("l", l, "wo")]
        items += [("l", l, "x2T"), ("l", l, "hB"), ("l", l, "hT")]
        items += [("l", l, "w1", c) for c in range(3)] + [("l", l, "w2")]
    return items


LOCAL_FRONT = [("qk", 0), ("qk", 1), ("qk", 2), ("rT", 0), ("qk", 3), ("rT", 1), ("v", 0), ("v", 1), ("rT", 2), ("rT", 3)]


def attention_order():
    units = [(i, pr) for i in range(T) for pr in range(2)]
    out = [("s1", (0,) + u) for u in units]
    for g in range(QUADS):
        ahead = [("s1", (g + 1,) + u) for u in units] if g + 1 < QUADS else []
        out += ahead[:3] + [("mT", (g,))]
        rest = ahead[3:]
        for n, u in enumerate(units):
            out += [("s2", (g,) + u)] + rest[:1]
            rest = rest[1:]
            if n == 2 and g:
                out += [("oT", (g - 1,))]
    out += [("oT", (QUADS - 1,))]
    return out


def build(nc, ins, out, rounds=SEQS, probe=None):
    ctx = ExitStack()
    with ctx:
        def sb(name, shape, dt=F32):
            return ctx.enter_context(nc.sbuf_tensor(name, shape, dt))

        def sem(name):
            return ctx.enter_context(nc.semaphore(name))

        ring = [ctx.enter_context(nc.psum_tensor(f"ring{i}", [P, 1024], F32)) for i in range(3)]
        pv_bank = [ctx.enter_context(nc.psum_tensor(f"pv_bank{i}", [P, 512], F32)) for i in range(2)]
        ORDER = psum_order()
        PRO = 3
        N_ITEMS = len(ORDER)
        assert N_ITEMS % 3 == 0 and len(set(ORDER)) == N_ITEMS
        INDEX = {name: i for i, name in enumerate(ORDER)}

        def slot(*name):
            return ring[INDEX[name] % 3]

        ident = sb("ident", [P, P])
        identb = sb("identb", [P, P], BF16)
        alibi_q = sb("alibi_q", [P, PAIRS, S], BF16)
        alibi_k = sb("alibi_k", [P, PAIRS, S], BF16)
        alibi_d = sb("alibi_d", [P, H, 3, P], BF16)
        band_q = sb("band_q", [P, BAND], BF16)
        band_k = sb("band_k", [P, BAND], BF16)
        ones_m = sb("ones_m", [P, P], BF16)
        wqkvT = sb("wqkvT", [P, 2, 3 * D])
        woT = sb("woT", [P, 2, D])
        bqkv = sb("bqkv", [P, 2, 3 * D])
        bo = sb("bo", [P, 2, D])
        wguT = sb("wguT", [P, 2, INTER])
        wdT = sb("wdT", [P, 3, D])
        wl_qkv = sb("wl_qkv", [P, LAYERS, 3 * LH * LD])
        wl_o = sb("wl_o", [P, LAYERS, 4, D])
        w1 = sb("w1", [P, LAYERS, 2 * HID])
        w2 = sb("w2", [P, LAYERS, 3, D])
        b1 = sb("b1", [P, LAYERS, 2, 3])
        b2 = sb("b2", [P, LAYERS, D])
        ln_g = sb("ln_g", [P, LAYERS])
        ln_b = sb("ln_b", [P, LAYERS])
        rot_c = sb("rot_c", [P, LAYERS, T, 2, LD])
        rot_s = sb("rot_s", [P, LAYERS, T, 2, LD])
        neg_half = sb("neg_half", [P, 16])
        zeros = sb("zeros", [P, 64])

        x = sb("x", [P, T, D])
        y = sb("y", [P, T, D])
        xT = sb("xT", [P, S])
        stats = sb("stats", [P, T, 6])
        mv = sb("mv", [P, T, 2])
        rstd = sb("rstd", [P, T])
        big = sb("big", [P, 10 * 1024])
        qk = big[:, 0:1024].rearrange("p (t s c) -> p t s c", t=T, s=2)
        part0 = sb("part0", [P, T, 2, D], BF16)
        part1 = sb("part1", [P, T, 2, D], BF16)
        part2 = sb("part2", [P, T, 2, D], BF16)
        aug = sb("aug", [P, 2, T, H, SLOTS], BF16)
        v_aug = sb("v_aug", [P, T, H, 32])
        qkT = big[:, 1024:5120].bitcast(BF16).rearrange("p (g b c s) -> p g b c s", g=QUADS, b=2, c=2)
        qmT = big[:, 5120:6144].bitcast(BF16).rearrange("p (g b s) -> p g b s", g=2, b=2)
        neg_max = sb("neg_max", [P, QUADS, T, 4])
        max_r1 = sb("max_r1", [P, T, 4])
        max_r2 = sb("max_r2", [P, T, 4])
        prob = big[:, 6144:10240].rearrange("p (n m s) -> p n m s", n=4, m=2)
        oT = sb("oT", [P, 2, S])
        rsum = sb("rsum", [P, T * 4])
        att = sb("att", [P, T, D])
        attT = sb("attT", [P, S])
        n4 = T * INTER
        h4 = big[:, 0:n4]
        a4 = big[:, n4:2 * n4]
        s4 = big[:, 2 * n4:3 * n4]
        c4 = big[:, 3 * n4:4 * n4]
        d4 = big[:, 4 * n4:5 * n4]
        hqT = big[:, 5 * n4:5 * n4 + 3 * S].rearrange("p (c s) -> p c s", c=3)
        silu = big[:, 5 * n4 + 3 * S:5 * n4 + 3 * S + 2 * INTER].rearrange("p (c s) -> p c s", c=2)
        lqk = big[:, 0:2048].rearrange("p (b s h d) -> p b s h d", b=2, s=2, h=LH)
        lsq = big[:, 2048:4096].rearrange("p (b s h d) -> p b s h d", b=2, s=2, h=LH)
        lrs = big[:, 4096:6144].rearrange("p (b s h d) -> p b s h d", b=2, s=2, h=LH)
        lqkT = big[:, 6144:10240].rearrange("p (c s) -> p c s", c=8)
        lprob = big[:, 0:4096].rearrange("p (b h q) -> p b h q", b=2, h=LH)
        lo = big[:, 4096:6144].rearrange("p (t c) -> p t c", t=T)
        loT = big[:, 6144:8192].rearrange("p (c s) -> p c s", c=4)
        gel = big[:, 0:1536].rearrange("p (c s) -> p c s", c=3)
        hid = big[:, 1536:3072].rearrange("p (c s) -> p c s", c=3)
        hn = big[:, 3072:3584].rearrange("p (t c) -> p t c", t=T)
        amax = sb("amax", [P, T * INTER // FB])
        fscale = sb("fscale", [P, T * INTER // FB])
        finv = sb("finv", [P, T * INTER // FB])
        xq = sb("xq", [P, T, D])
        lv = sb("lv", [P, T, LH, LD + 1])
        lss = sb("lss", [P, T, 16])
        lrn = sb("lrn", [P, T, 16])
        lneg = sb("lneg", [P, T, LH])
        lm_r1 = sb("lm_r1", [P, T * LH])
        lm_r2 = sb("lm_r2", [P, T * LH])
        lm = sb("lm", [P, T, LH, SLOTS], BF16)
        lmT = sb("lmT", [P, 4, S], BF16)
        lrsum = sb("lrsum", [P, T, LH])

        const_in = sem("const_in")
        x_in = sem("x_in")
        out_done = sem("out_done")
        filled = sem("filled")
        freed = [sem(f"freed{i}") for i in range(3)]
        prep_v = sem("prep_v")
        prep_a = sem("prep_a")
        prep_g = sem("prep_g")
        xT_ready = sem("xT_ready")
        qkv_ready = sem("qkv_ready")
        hi_ready = sem("hi_ready")
        r1_ready = sem("r1_ready")
        mid_ready = sem("mid_ready")
        aug_a = sem("aug_a")
        aug_g = sem("aug_g")
        qkT_ready = sem("qkT_ready")
        max_ready = sem("max_ready")
        maxq_ready = sem("maxq_ready")
        qmT_ready = sem("qmT_ready")
        prob_ready = sem("prob_ready")
        pv_done = sem("pv_done")
        oT_ready = sem("oT_ready")
        att_ready = sem("att_ready")
        attT_ready = sem("attT_ready")
        y_var = sem("y_var")
        rstd_ready = sem("rstd_ready")
        x_ready = sem("x_ready")
        fq_x = sem("fq_x")
        fq_s = sem("fq_s")
        fq_g = sem("fq_g")
        fq_q = sem("fq_q")
        fq_q_h = sem("fq_q_h")
        y_ready = sem("y_ready")
        fT_ready = sem("fT_ready")
        silu_ready = sem("silu_ready")
        lsq_ready = sem("lsq_ready")
        lss_ready = sem("lss_ready")
        lrn_ready = sem("lrn_ready")
        lqn_ready = sem("lqn_ready")
        lsin_ready = sem("lsin_ready")
        lrot_ready = sem("lrot_ready")
        lqkT_ready = sem("lqkT_ready")
        lv_ready = sem("lv_ready")
        lneg_ready = sem("lneg_ready")
        lm_ready = sem("lm_ready")
        lmT_ready = sem("lmT_ready")
        lprob_ready = sem("lprob_ready")
        lo_ready = sem("lo_ready")
        loT_ready = sem("loT_ready")
        h_back = sem("h_back")
        hT_ready = sem("hT_ready")
        gel_ready = sem("gel_ready")
        hid_ready = sem("hid_ready")

        block = ctx.enter_context(nc.Block())
        N_CONST = 28 + 28

        @block.sync
        def _(sp):
            def load(dst, src):
                sp.dma_start(dst, src).then_inc(const_in, 16)

            load(x[:, 0:3, :], ins["wqkv0"].rearrange("(c p) d -> p c d", p=P))
            load(y[:, 0:3, :], ins["wqkv1"].rearrange("(c p) d -> p c d", p=P))
            load(x[:, 3, :], ins["wo0"])
            load(y[:, 3, :], ins["wo1"])
            load(ident[:], ins["ident"])
            load(h4[:, 0:256].rearrange("p (c d) -> p c d", c=2), ins["wgate"][0:256, :].rearrange("(c p) d -> p c d", p=P))
            load(h4[0:96, 256:384], ins["wgate"][256:352, :])
            load(h4[:, 384:640].rearrange("p (c d) -> p c d", c=2), ins["wup"][0:256, :].rearrange("(c p) d -> p c d", p=P))
            load(h4[0:96, 640:768], ins["wup"][256:352, :])
            load(h4[:, 768:768 + INTER], ins["wdown"])
            for a in range(2):
                load(bqkv[:, a, :], ins[f"bqkv{a}"].rearrange("(o n) -> o n", o=1).broadcast_to([P, 3 * D]))
                load(bo[:, a, :], ins[f"bo{a}"].rearrange("(o n) -> o n", o=1).broadcast_to([P, D]))
            load(identb[:], ins["identb"])
            load(alibi_q[:], ins["alibi_q"])
            load(alibi_k[:], ins["alibi_k"])
            load(alibi_d[:], ins["alibi_d"])
            load(band_q[:], ins["band_q"])
            load(band_k[:], ins["band_k"])
            load(ones_m[:], ins["ones_m"])
            load(rot_c[:, 0], ins["rot_c"])
            load(rot_s[:, 0], ins["rot_s"])
            load(rot_c[:, 1], ins["rot_c"])
            load(rot_s[:, 1], ins["rot_s"])
            load(wl_qkv[:], ins["wl_qkv"].rearrange("l d n -> d l n"))
            for l in range(LAYERS):
                load(wl_o[:, l], ins["wl_o"][l].rearrange("(c p) n -> p c n", p=P))

        @block.gpsimd
        def _(pool):
            nc.gpsimd.memset(aug[:], 0.0)
            nc.gpsimd.memset(v_aug[:], 0.0)
            nc.gpsimd.memset(lm[:], 0.0)
            nc.gpsimd.memset(neg_half[:], -0.5)
            nc.gpsimd.memset(zeros[:], 0.0)
            nc.gpsimd.memset(lv[:], 1.0)
            pool.drain()
            nc.gpsimd.memset(aug[:, 1, :, :, M_SLOT:M_SLOT + 3], 1.0)
            nc.gpsimd.memset(v_aug[:, :, :, HD:HD + 1], 1.0)
            pool.drain().then_inc(prep_g, 1)
            NB = 6 * 8 + 22
            pool.wait_ge(fq_s, 1)
            nc.gpsimd.tensor_tensor(
                s4[:, 0:NB * FB].rearrange("p (b f) -> p b f", f=FB),
                s4[:, 0:NB * FB].rearrange("p (b f) -> p b f", f=FB),
                fscale[:, 0:NB].unsqueeze(2).broadcast_to([P, NB, FB]), ALU.mult).then_inc(fq_g, 1)

            with pool.Fori(0, rounds) as r:
                def rsqrt(n):
                    pool.wait_ge(y_var, r * 6 + n)
                    nc.gpsimd.tensor_tensor(rstd[:], mv[:, :, 1], neg_half[:, 0:T], ALU.pow).then_inc(rstd_ready, 1)

                def fp4_scale(n, cols):
                    nb = cols // FB
                    pool.wait_ge(fq_s, r * 2 + 1 + n)
                    nc.gpsimd.tensor_tensor(
                        s4[:, 0:cols].rearrange("p (b f) -> p b f", f=FB),
                        s4[:, 0:cols].rearrange("p (b f) -> p b f", f=FB),
                        fscale[:, 0:nb].unsqueeze(2).broadcast_to([P, nb, FB]), ALU.mult).then_inc(fq_g, 1)

                def attention(a):
                    flat = lambda t: t.rearrange("p t s c -> p (t s c)")
                    pool.wait_ge(hi_ready, r * 2 + a + 1)
                    nc.gpsimd.tensor_tensor(flat(qk), flat(qk), flat(part0[:]), ALU.subtract).then_inc(r1_ready, 1)
                    pool.wait_ge(mid_ready, r * 2 + a + 1)
                    nc.gpsimd.tensor_tensor(flat(part2[:]), flat(qk), flat(part1[:]), ALU.subtract)
                    pool.drain()
                    for side, parts in ((0, Q_PART), (1, K_PART)):
                        for n, part in enumerate(parts):
                            if part:
                                nc.gpsimd.tensor_copy(
                                    aug[:, side, :, :, 8 * n:8 * n + 8],
                                    (part1, part2)[part - 1][:, :, side, :].rearrange("p t (h d) -> p t h d", d=HD))
                    pool.drain().then_inc(aug_g, 1)
                    for g in range(QUADS):
                        pool.wait_ge(max_ready, r * 64 + a * 32 + 8 * g + 8)
                        h0 = 4 * g
                        nc.gpsimd.tensor_tensor(aug[:, 0, :, h0:h0 + 4, M_SLOT], neg_max[:, g],
                                                zeros[:, 0:16].rearrange("p (t h) -> p t h", t=T), ALU.add)
                        pool.drain()
                        nc.gpsimd.tensor_tensor(max_r1[:], neg_max[:, g], aug[:, 0, :, h0:h0 + 4, M_SLOT], ALU.subtract)
                        pool.drain()
                        nc.gpsimd.tensor_copy(aug[:, 0, :, h0:h0 + 4, M_SLOT + 1], max_r1[:])
                        pool.drain()
                        nc.gpsimd.tensor_tensor(aug[:, 0, :, h0:h0 + 4, M_SLOT + 2], max_r1[:],
                                                aug[:, 0, :, h0:h0 + 4, M_SLOT + 1], ALU.subtract)
                        pool.drain().then_inc(maxq_ready, 1)
                    pool.wait_ge(qmT_ready, r * 8 + a * 4 + 4)
                    for k in range(3):
                        nc.gpsimd.tensor_tensor(aug[:, 0, :, :, M_SLOT + k], zeros[:].rearrange("p (t h) -> p t h", t=T),
                                                zeros[:].rearrange("p (t h) -> p t h", t=T), ALU.add)
                    pool.drain()
                    rsqrt(1 + 2 * a)

                def layer(l):
                    for t in range(T):
                        pool.wait_ge(lss_ready, r * 8 + l * 4 + t + 1)
                        nc.gpsimd.tensor_tensor(lrn[:, t, :], lss[:, t, :], neg_half[:, 0:16], ALU.pow).then_inc(lrn_ready, 1)
                        pool.wait_ge(lqn_ready, r * 8 + l * 4 + t + 1)
                        for half in range(2):
                            for side in range(2):
                                nc.gpsimd.tensor_tensor(
                                    lsq[:, t % 2, side, :, 32 * half:32 * half + 32],
                                    lqk[:, t % 2, side, :, 32 - 32 * half:64 - 32 * half],
                                    rot_s[:, l, t, side, 32 * half:32 * half + 32].unsqueeze(1).broadcast_to([P, LH, 32]),
                                    ALU.mult)
                        pool.drain().then_inc(lsin_ready, 1)
                    pool.wait_ge(lneg_ready, r * 16 + l * 8 + 8)
                    lmf = lm[:].rearrange("p t h s -> p (t h) s")
                    lnf = lneg[:].rearrange("p t h -> p (t h)")
                    nc.gpsimd.tensor_tensor(lmf[:, :, 0], lnf, zeros[:, 0:T * LH], ALU.add)
                    pool.drain()
                    nc.gpsimd.tensor_tensor(lm_r1[:], lnf, lmf[:, :, 0], ALU.subtract)
                    pool.drain()
                    nc.gpsimd.tensor_copy(lmf[:, :, 1], lm_r1[:])
                    pool.drain()
                    nc.gpsimd.tensor_tensor(lmf[:, :, 2], lm_r1[:], lmf[:, :, 1], ALU.subtract)
                    nc.gpsimd.memset(lprob[:, :, :, BAND:256], 0.0)
                    pool.drain().then_inc(lm_ready, 1)
                    rsqrt(4 + l)

                attention(0)
                fp4_scale(1, T * D)
                fp4_scale(2, T * INTER)
                rsqrt(2)
                attention(1)
                layer(0)
                layer(1)
                rsqrt(6)

        @block.scalar
        def _(act):
            def load(dst, src, **k):
                act.dma_start(dst, src, **k).then_inc(const_in, 16)

            load(w1[:], ins["w1"].rearrange("l d n -> d l n"))
            for c, (c0, cw) in enumerate(HCH):
                load(w2[0:cw, :, c, :], ins["w2"][:, c0:c0 + cw, :].rearrange("l p n -> p l n"))
                for side in range(2):
                    load(b1[0:cw, :, side, c], ins["b1"][:, side * HID + c0:side * HID + c0 + cw].rearrange("l p -> p l"), allow_slow_non_contiguous=True)
            for l in range(LAYERS):
                load(b2[:, l, :], ins["b2"][l:l + 1, :].broadcast_to([P, D]))
                load(ln_g[:, l:l + 1], ins["ln_g"][l:l + 1, :].rearrange("l p -> p l"), allow_slow_non_contiguous=True)
                load(ln_b[:, l:l + 1], ins["ln_b"][l:l + 1, :].rearrange("l p -> p l"), allow_slow_non_contiguous=True)
            for l in range(LAYERS):
                for side, name in ((0, "q_scale"), (1, "k_scale")):
                    load(c4[:, (2 * l + side) * LD:(2 * l + side + 1) * LD], ins[name][l:l + 1, :].broadcast_to([P, LD]))
                    for half in range(2):
                        o = 4 * LD + (2 * l + side) * LD + 32 * half
                        load(c4[:, o:o + 32], ins[name][l:l + 1, 32 - 32 * half:64 - 32 * half].broadcast_to([P, 32]))

            def copy(dst, src, func=ACT.Copy, **k):
                return nc.scalar.activation(dst, src, func, **k)

            NW = (6 * 8 + 22) * FB
            act.wait_ge(filled, 1)
            copy(wqkvT[:, 0, :], ring[0][:, 0:384])
            copy(wqkvT[:, 1, :], ring[0][:, 384:768])
            copy(woT[:].rearrange("p a d -> p (a d)"), ring[0][:, 768:1024]).then_inc(freed[0], 1)
            act.wait_ge(fq_x, 1)
            copy(s4[:, 0:NW], a4[:, 0:NW], ACT.Sign)
            act.drain()
            copy(a4[:, 0:NW], a4[:, 0:NW], ACT.Abs).then_inc(fq_s, 1)
            act.wait_ge(filled, 2)
            copy(wguT[:, 0, :], ring[1][:, 0:INTER])
            copy(wguT[:, 1, :], ring[1][:, 512:512 + INTER]).then_inc(freed[1], 1)
            act.wait_ge(filled, 3)
            copy(wdT[:, 0:2, :].rearrange("p c d -> p (c d)"), ring[2][:, 0:256])
            copy(wdT[0:96, 2, :], ring[2][0:96, 256:384]).then_inc(freed[2], 1)
            act.drain().then_inc(prep_a, 1)
            act.wait_ge(prep_v, 3)
            act.sem_inc(out_done, 16)

            with act.Fori(0, rounds) as r:
                act.wait_ge(out_done, r * 16 + 16)
                act.dma_start(x[:], ins["x"][bass.ds(r, 1)].rearrange("o (t p) d -> p (o t) d", p=P)).then_inc(x_in, 16)

                def take(*name):
                    act.wait_ge(filled, r * N_ITEMS + PRO + INDEX[name] + 1)

                def release(ins_, *name):
                    ins_.then_inc(freed[INDEX[name] % 3], 1)

                def attention(a):
                    take(a, "xT")
                    release(copy(xT[:], slot(a, "xT")[:, 0:S]), a, "xT")
                    act.drain().then_inc(xT_ready, 1)
                    act.wait_ge(qkv_ready, r * 2 + a + 1)
                    copy(part0[:].rearrange("p t s c -> p (t s c)"), qk.rearrange("p t s c -> p (t s c)")).then_inc(hi_ready, 1)
                    act.drain()
                    for side, parts in ((0, Q_PART), (1, K_PART)):
                        for n, part in enumerate(parts):
                            if part == 0:
                                copy(aug[:, side, :, :, 8 * n:8 * n + 8],
                                     part0[:, :, side, :].rearrange("p t (h d) -> p t h d", d=HD))
                    act.wait_ge(r1_ready, r * 2 + a + 1)
                    copy(part1[:].rearrange("p t s c -> p (t s c)"), qk.rearrange("p t s c -> p (t s c)")).then_inc(mid_ready, 1)
                    act.drain().then_inc(aug_a, 1)
                    for g in range(QUADS):
                        take(a, "qkT", g)
                        release(copy(qkT[:, g].rearrange("p a b s -> p (a b s)"),
                                     slot(a, "qkT", g)[:].bitcast(BF16)), a, "qkT", g)
                        act.drain().then_inc(qkT_ready, 1)
                    n = 0
                    for kind, i in attention_order():
                        if kind == "mT":
                            g = i[0]
                            take(a, "mT", g)
                            release(copy(qmT[:, g % 2].rearrange("p b s -> p (b s)"),
                                         slot(a, "mT", g)[:, 0:512].bitcast(BF16)), a, "mT", g)
                            act.drain().then_inc(qmT_ready, 1)
                        elif kind == "s2":
                            take(a, "s2", *i)
                            if n >= 4:
                                act.wait_ge(pv_done, r * 32 + a * 16 + (n - 4) // 2 + 1)
                            release(copy(prob[:, n % 4].rearrange("p m s -> p (m s)"), slot(a, "s2", *i)[:], ACT.Exp), a, "s2", *i)
                            act.drain().then_inc(prob_ready, 1)
                            n += 1
                    take(a, "aT")
                    release(copy(attT[:], slot(a, "aT")[:, 0:S]), a, "aT")
                    act.drain().then_inc(attT_ready, 1)

                def fp4_sizes(n, cols):
                    act.wait_ge(fq_x, r * 2 + 1 + n)
                    copy(s4[:, 0:cols], a4[:, 0:cols], ACT.Sign)
                    act.drain()
                    copy(a4[:, 0:cols], a4[:, 0:cols], ACT.Abs).then_inc(fq_s, 1)

                def ffn4():
                    fp4_sizes(1, T * D)
                    take("f", "xqT")
                    release(copy(xT[:], slot("f", "xqT")[:, 0:S]), "f", "xqT")
                    act.drain().then_inc(fT_ready, 1)
                    for t in range(T):
                        take("f", "gu", t)
                        if t >= 2:
                            act.wait_ge(fq_q_h, r * T + t - 1)
                        copy(silu[:, t % 2, :], slot("f", "gu", t)[:, 0:INTER], ACT.Silu).then_inc(silu_ready, 1)
                    fp4_sizes(2, T * INTER)
                    for c, (c0, cw) in enumerate(ICH):
                        take("f", "hT", c)
                        release(copy(hqT[0:cw, c, :], slot("f", "hT", c)[0:cw, 0:S]), "f", "hT", c)
                    act.drain().then_inc(fT_ready, 1)

                def shifted(dst, src):
                    copy(dst[0:64, :], src[0:64, 0:S])
                    return copy(dst[64:128, 1:S], src[64:128, 0:S - 1])

                def zero_first():
                    copy(xT[64:128, 0:1], ident[64:128, 0:1])

                def layer(l):
                    L = ("l", l)
                    take(*L, "xT")
                    zero_first()
                    release(shifted(xT, slot(*L, "xT")), *L, "xT")
                    act.drain().then_inc(xT_ready, 1)
                    for kind, t in LOCAL_FRONT:
                        take(*L, kind, t)
                        if kind == "qk":
                            if t >= 2:
                                act.wait_ge(lrot_ready, r * 8 + l * 4 + t - 1)
                            copy(lsq[:, t % 2].rearrange("p s h d -> p (s h d)"), slot(*L, "qk", t)[:], ACT.Square).then_inc(lsq_ready, 1)
                        elif kind == "v":
                            release(copy(lv[:, 2 * t:2 * t + 2, :, 0:LD].rearrange("p t h d -> p (t h) d"),
                                         slot(*L, "v", t)[:].rearrange("p (h d) -> p h d", d=LD)), *L, "v", t)
                            if t == 1:
                                act.drain().then_inc(lv_ready, 1)
                        else:
                            release(copy(lqkT[:, :, t * P:(t + 1) * P], slot(*L, "rT", t)[:].rearrange("p (c q) -> p c q", c=8)), *L, "rT", t)
                            act.drain().then_inc(lqkT_ready, 1)
                    take(*L, "mT")
                    release(copy(lmT[:].rearrange("p c s -> p (c s)"), slot(*L, "mT")[:].bitcast(BF16)), *L, "mT")
                    act.drain().then_inc(lmT_ready, 1)
                    for t in range(T):
                        w = BAND if t < T - 1 else P
                        for q in range(2):
                            take(*L, "s2", t, q)
                            if q == 0 and t >= 2:
                                act.wait_ge(filled, r * N_ITEMS + PRO + INDEX[("l", l, "pv", t - 1)] + 1)
                            sl = slot(*L, "s2", t, q)[:].rearrange("p (m w) -> p m w", m=2)[:, :, 0:2 * BAND].rearrange("p m (u w) -> p m u w", u=2)
                            dst = lprob[:, t % 2, 4 * q:4 * q + 4, 0:w].rearrange("p (u m) w -> p m u w", m=2)
                            for m in range(2):
                                last = copy(dst[:, m], sl[:, m, :, 0:w], ACT.Exp)
                            release(last, *L, "s2", t, q)
                        act.drain().then_inc(lprob_ready, 1)
                    for i in range(2):
                        take(*L, "oT", i)
                        release(copy(loT[:, :, 2 * i * P:(2 * i + 2) * P].rearrange("p c (t q) -> p t c q", t=2),
                                     slot(*L, "oT", i)[:].rearrange("p (t c q) -> p t c q", t=2, c=4)), *L, "oT", i)
                    act.drain().then_inc(loT_ready, 1)
                    take(*L, "x2T")
                    zero_first()
                    release(shifted(xT, slot(*L, "x2T")), *L, "x2T")
                    act.drain().then_inc(xT_ready, 1)
                    take(*L, "hT")
                    release(copy(xT[:], slot(*L, "hT")[:, 0:S], ACT.Identity, scale=ln_g[:, l:l + 1], bias=ln_b[:, l:l + 1]), *L, "hT")
                    act.drain().then_inc(hT_ready, 1)
                    for c, (c0, cw) in enumerate(HCH):
                        take(*L, "w1", c)
                        copy(gel[0:cw, c, :], slot(*L, "w1", c)[0:cw, 512:1024], ACT.Gelu, bias=b1[0:cw, l, 1, c:c + 1]).then_inc(gel_ready, 1)

                attention(0)
                ffn4()
                attention(1)
                layer(0)
                layer(1)
                act.wait_ge(x_ready, r * 4 + 4)
                act.dma_start(out[bass.ds(r, 1)].rearrange("o (t p) d -> p (o t) d", p=P), x[:]).then_inc(out_done, 16)
            act.wait_ge(out_done, 16 * (rounds + 1))

        @block.vector
        def _(dve):
            V = nc.vector

            def fp4(n_cols, src, dst):
                a, c, d = a4[:, 0:n_cols], c4[:, 0:n_cols], d4[:, 0:n_cols]
                V.tensor_scalar(c, a, 5.0, 2.0, ALU.is_gt, ALU.mult)
                V.tensor_scalar(d, a, 0.25, None, ALU.is_gt)
                dve.drain()
                V.scalar_tensor_tensor(c, a, 3.5, c, ALU.is_gt, ALU.add)
                V.scalar_tensor_tensor(d, a, 0.75, d, ALU.is_gt, ALU.add)
                dve.drain()
                V.scalar_tensor_tensor(c, a, 2.5, c, ALU.is_gt, ALU.add)
                V.scalar_tensor_tensor(d, a, 1.25, d, ALU.is_gt, ALU.add)
                dve.drain()
                V.scalar_tensor_tensor(d, a, 1.75, d, ALU.is_gt, ALU.add)
                dve.drain()
                V.scalar_tensor_tensor(d, c, 2.0, d, ALU.mult, ALU.add)
                dve.drain()

            def fp4_norm(src, n_cols):
                nb = n_cols // FB
                V.tensor_reduce(amax[:, 0:nb], src.rearrange("p (b f) -> p b f", f=FB), op=ALU.max, axis=AX,
                                apply_absolute_value=True)
                dve.drain()
                V.tensor_scalar(fscale[:, 0:nb], amax[:, 0:nb], 1.0 / 6.0, 1e-12, ALU.mult, ALU.max)
                dve.drain()
                V.reciprocal(finv[:, 0:nb], fscale[:, 0:nb])
                dve.drain()
                V.tensor_tensor(a4[:, 0:n_cols].rearrange("p (b f) -> p b f", f=FB),
                                src.rearrange("p (b f) -> p b f", f=FB),
                                finv[:, 0:nb].unsqueeze(2).broadcast_to([P, nb, FB]), ALU.mult).then_inc(fq_x, 1)

            NW = (6 * 8 + 22) * FB
            V.memset(h4[96:128, 256:384], 0.0)
            V.memset(h4[96:128, 640:768], 0.0)
            dve.drain().then_inc(prep_v, 1)
            dve.wait_ge(const_in, 16 * N_CONST)
            for l in range(LAYERS):
                for side in range(2):
                    for tab, o in ((rot_c, 0), (rot_s, 4 * LD)):
                        o += (2 * l + side) * LD
                        V.tensor_tensor(tab[:, l, :, side, :], tab[:, l, :, side, :],
                                        c4[:, o:o + LD].unsqueeze(1).broadcast_to([P, T, LD]), ALU.mult)
            for a in range(2):
                V.tensor_scalar(bqkv[:, a, 0:D], bqkv[:, a, 0:D], HD ** -0.5, None, ALU.mult)
            dve.drain().then_inc(prep_v, 1)
            fp4_norm(h4[:, 0:NW], NW)
            dve.wait_ge(fq_s, 1)
            fp4(NW, None, None)
            dve.wait_ge(fq_g, 1)
            V.scalar_tensor_tensor(h4[:, 0:NW], d4[:, 0:NW], 0.5, s4[:, 0:NW], ALU.mult, ALU.mult)
            dve.drain().then_inc(fq_q, 1)
            dve.wait_ge(filled, 1)
            dve.drain().then_inc(prep_v, 1)

            with dve.Fori(0, rounds) as r:
                def take(*name):
                    dve.wait_ge(filled, r * N_ITEMS + PRO + INDEX[name] + 1)

                def release(ins_, *name):
                    return ins_.then_inc(freed[INDEX[name] % 3], 1)

                def moments(src, n):
                    for t in range(T):
                        V.bn_stats(stats[:, t, :], src[:, t, :])
                    dve.drain()
                    for t in range(T):
                        V.bn_aggr(mv[:, t, :], stats[:, t, :])
                    dve.drain()
                    V.tensor_scalar(mv[:, :, 1], mv[:, :, 1], EPS, None, ALU.add).then_inc(y_var, 1)
                    dve.wait_ge(rstd_ready, r * 6 + n)

                def normalise(dst, src):
                    for t in range(T):
                        V.tensor_scalar(dst[:, t, :], src[:, t, :], mv[:, t, 0:1], rstd[:, t:t + 1], ALU.subtract, ALU.mult)

                def close_block(name, bias, n, xn):
                    take(*name)
                    out_ = slot(*name)[:, 0:S].rearrange("p (t d) -> p t d", t=T)
                    if bias is not None:
                        V.tensor_tensor(x[:], x[:], bias.unsqueeze(1).broadcast_to([P, T, D]), ALU.add)
                        dve.drain()
                    release(V.tensor_tensor(y[:], out_, x[:], ALU.add), *name)
                    dve.drain()
                    moments(y, n)
                    normalise(x, y)
                    dve.drain().then_inc(x_ready, 1)

                def attention(a):
                    for i in range(2):
                        take(a, "qkv", i)
                        for b in range(2):
                            t = 2 * i + b
                            src = slot(a, "qkv", i)[:, 512 * b:512 * b + 3 * D]
                            V.scalar_tensor_tensor(qk[:, t, 0, :], src[:, 0:D], HD ** -0.5, bqkv[:, a, 0:D], ALU.mult, ALU.add)
                            V.tensor_tensor(qk[:, t, 1, :], src[:, D:2 * D], bqkv[:, a, D:2 * D], ALU.add)
                            last = V.tensor_tensor(v_aug[:, t, :, 0:HD], src[:, 2 * D:3 * D].rearrange("p (h d) -> p h d", d=HD),
                                                   bqkv[:, a, 2 * D:3 * D].rearrange("p (h d) -> p h d", d=HD), ALU.add)
                        release(last, a, "qkv", i)
                    dve.drain().then_inc(qkv_ready, 1)
                    for kind, i in attention_order():
                        if kind == "s1":
                            g, t, pr = i
                            take(a, "s1", *i)
                            release(V.tensor_reduce(neg_max[:, g, t, 2 * pr:2 * pr + 2],
                                                    slot(a, "s1", *i)[:].rearrange("p (m s) -> p m s", m=2),
                                                    op=ALU.max, axis=AX, negate=True), a, "s1", *i)
                            dve.drain().then_inc(max_ready, 1)
                        elif kind == "s2" and i[1] == 0 and i[2] == 1 and i[0] > 0:
                            pv_out(a, i[0] - 1)
                        elif kind == "oT":
                            g, = i
                            if g == QUADS - 1:
                                pv_out(a, g)
                            take(a, "oT", g)
                            o4 = slot(a, "oT", g)[:, 0:S].rearrange("p (n c) -> p n c", c=32)
                            V.reciprocal(rsum[:], o4[:, :, HD])
                            dve.drain()
                            release(V.tensor_tensor(att[:, :, 32 * g:32 * g + 32].rearrange("p t (j d) -> p t j d", j=4),
                                                    o4[:, :, 0:HD].rearrange("p (t j) d -> p t j d", t=T),
                                                    rsum[:].rearrange("p (t j) -> p t j", t=T).unsqueeze(3).broadcast_to([P, T, 4, HD]),
                                                    ALU.mult), a, "oT", g)
                            dve.drain().then_inc(att_ready, 1)
                    close_block((a, "proj"), bo[:, a, :], 1 + 2 * a, None)

                def pv_out(a, g):
                    dve.wait_ge(pv_done, r * 32 + a * 16 + 4 * g + 4)
                    V.tensor_copy(oT[:, g % 2, :], pv_bank[g % 2][:])
                    dve.drain().then_inc(oT_ready, 1)

                def ffn4():
                    xf = x[:].rearrange("p t d -> p (t d)")
                    fp4_norm(xf, T * D)
                    dve.wait_ge(fq_s, r * 2 + 2)
                    fp4(T * D, None, None)
                    dve.wait_ge(fq_g, r * 2 + 2)
                    V.scalar_tensor_tensor(xq[:].rearrange("p t d -> p (t d)"), d4[:, 0:T * D], 0.5, s4[:, 0:T * D], ALU.mult, ALU.mult)
                    dve.drain().then_inc(fq_q, 1)
                    for t in range(T):
                        dve.wait_ge(silu_ready, r * T + t + 1)
                        release(V.tensor_tensor(h4[:, t * INTER:(t + 1) * INTER], silu[:, t % 2, :],
                                                slot("f", "gu", t)[:, 512:512 + INTER], ALU.mult), "f", "gu", t)
                        dve.drain().then_inc(fq_q_h, 1)
                    fp4_norm(h4, n4)
                    dve.wait_ge(fq_s, r * 2 + 3)
                    fp4(n4, None, None)
                    dve.wait_ge(fq_g, r * 2 + 3)
                    V.scalar_tensor_tensor(h4, d4, 0.5, s4, ALU.mult, ALU.mult)
                    dve.drain().then_inc(fq_q, 1)
                    close_block(("f", "down"), None, 2, None)

                def layer(l):
                    L = ("l", l)
                    for t in range(T):
                        dve.wait_ge(lsq_ready, r * 8 + l * 4 + t + 1)
                        V.tensor_reduce(lss[:, t, :], lsq[:, t % 2].rearrange("p s h d -> p (s h) d"), op=ALU.add, axis=AX)
                        dve.drain()
                        V.tensor_scalar(lss[:, t, :], lss[:, t, :], 1e-24, None, ALU.max).then_inc(lss_ready, 1)
                        dve.wait_ge(lrn_ready, r * 8 + l * 4 + t + 1)
                        release(V.tensor_tensor(lqk[:, t % 2].rearrange("p s h d -> p (s h) d"),
                                                slot(*L, "qk", t)[:].rearrange("p (h d) -> p h d", d=LD),
                                                lrn[:, t, :].unsqueeze(2).broadcast_to([P, 16, LD]), ALU.mult), *L, "qk", t)
                        dve.drain().then_inc(lqn_ready, 1)
                        if t >= 2:
                            dve.wait_ge(filled, r * N_ITEMS + PRO + INDEX[("l", l, "rT", t - 2)] + 1)
                        for side in range(2):
                            V.tensor_tensor(lrs[:, t % 2, side], lqk[:, t % 2, side],
                                            rot_c[:, l, t, side, :].unsqueeze(1).broadcast_to([P, LH, LD]), ALU.mult)
                        dve.drain()
                        dve.wait_ge(lsin_ready, r * 8 + l * 4 + t + 1)
                        V.tensor_tensor(lrs[:, t % 2].rearrange("p s h d -> p (s h d)"), lrs[:, t % 2].rearrange("p s h d -> p (s h d)"),
                                        lsq[:, t % 2].rearrange("p s h d -> p (s h d)"), ALU.add)
                        dve.drain().then_inc(lrot_ready, 1)
                    for t in range(T):
                        lo_, w = (0, BAND) if t else (WIN, P)
                        for q in range(2):
                            take(*L, "s1", t, q)
                            sl = slot(*L, "s1", t, q)[:].rearrange("p (m w) -> p m w", m=2)[:, :, 0:2 * BAND].rearrange("p m (u w) -> p m u w", u=2)
                            release(V.tensor_reduce(lneg[:, t, 4 * q:4 * q + 4].rearrange("p (u m) -> p m u", m=2),
                                                    sl[:, :, :, lo_:BAND], op=ALU.max, axis=AX, negate=True), *L, "s1", t, q)
                            dve.drain().then_inc(lneg_ready, 1)
                    for t in range(T):
                        take(*L, "pv", t)
                        o3 = slot(*L, "pv", t)[:].rearrange("p (b c) -> p b c", b=2)[:, :, 0:4 * (LD + 1)].rearrange("p b (h c) -> p b h c", c=LD + 1)
                        V.reciprocal(lrsum[:, t, :].rearrange("p (b h) -> p b h", b=2), o3[:, :, :, LD])
                        dve.drain()
                        release(V.tensor_tensor(lo[:, t, :].rearrange("p (b h d) -> p b h d", b=2, h=4), o3[:, :, :, 0:LD],
                                                lrsum[:, t, :].rearrange("p (b h) -> p b h", b=2).unsqueeze(3).broadcast_to([P, 2, 4, LD]),
                                                ALU.mult), *L, "pv", t)
                    dve.drain().then_inc(lo_ready, 1)
                    take(*L, "wo")
                    base = x if l == 0 else y
                    release(V.tensor_tensor(y[:], slot(*L, "wo")[:, 0:S].rearrange("p (t d) -> p t d", t=T), base[:], ALU.add), *L, "wo")
                    dve.drain().then_inc(y_ready, 1)
                    take(*L, "hB")
                    V.tensor_copy(hn, slot(*L, "hB")[:, 0:S].rearrange("p (t d) -> p t d", t=T)).then_inc(freed[INDEX[(*L, "hB")] % 3], 1)
                    dve.drain()
                    moments(hn, 4 + l)
                    normalise(hn, hn)
                    dve.drain().then_inc(h_back, 1)
                    V.tensor_tensor(y[:], y[:], b2[:, l, :].unsqueeze(1).broadcast_to([P, T, D]), ALU.add)
                    for c, (c0, cw) in enumerate(HCH):
                        dve.wait_ge(gel_ready, r * 6 + l * 3 + c + 1)
                        release(V.scalar_tensor_tensor(hid[0:cw, c, :], slot(*L, "w1", c)[0:cw, 0:S], b1[0:cw, l, 0, c:c + 1],
                                                       gel[0:cw, c, :], ALU.add, ALU.mult), *L, "w1", c)
                    dve.drain().then_inc(hid_ready, 1)
                    take(*L, "w2")
                    release(V.tensor_tensor(y[:], slot(*L, "w2")[:, 0:S].rearrange("p (t d) -> p t d", t=T), y[:], ALU.add), *L, "w2")
                    dve.drain().then_inc(y_ready, 1)

                dve.wait_ge(x_in, r * 16 + 16)
                attention(0)
                ffn4()
                attention(1)
                layer(0)
                layer(1)
                V.tensor_tensor(y[:], y[:], x[:], ALU.add)
                dve.drain()
                moments(y, 6)
                normalise(x, y)
                dve.drain().then_inc(x_ready, 1)

        @block.tensor
        def _(pe):
            mm = nc.tensor.matmul

            def transpose(dst, src, idt=None):
                n = src.shape[0]
                idt = ident if idt is None else idt
                return nc.tensor.transpose(dst, src, idt[0:n, 0:n])

            pe.wait_ge(const_in, 16 * N_CONST)
            for c in range(3):
                transpose(ring[0][:, c * P:(c + 1) * P], x[:, c, :])
                transpose(ring[0][:, (3 + c) * P:(4 + c) * P], y[:, c, :])
            transpose(ring[0][:, 6 * P:7 * P], x[:, 3, :])
            transpose(ring[0][:, 7 * P:8 * P], y[:, 3, :]).then_inc(filled, 1)
            pe.wait_ge(fq_q, 1)
            for s in range(2):
                for c, (c0, cw) in enumerate(ICH):
                    last = transpose(ring[1][:, 512 * s + c0:512 * s + c0 + cw], h4[0:cw, (3 * s + c) * D:(3 * s + c + 1) * D])
            last.then_inc(filled, 1)
            for c, (c0, cw) in enumerate(ICH):
                last = transpose(ring[2][0:cw, c * P:(c + 1) * P], h4[:, 768 + c0:768 + c0 + cw])
            last.then_inc(filled, 1)
            pe.wait_ge(prep_a, 1)
            pe.wait_ge(prep_v, 2)
            pe.wait_ge(prep_g, 1)

            with pe.Fori(0, rounds) as r:
                def claim(*name):
                    i = INDEX[name]
                    pe.wait_ge(freed[i % 3], r * (N_ITEMS // 3) + 1 + i // 3)
                    return ring[i % 3]

                def fill(last):
                    last.then_inc(filled, 1)

                def scores1(a, g, t, pr):
                    o = claim(a, "s1", g, t, pr)
                    for m in range(2):
                        rows, hp, h = slice(64 * m, 64 * m + 64), 2 * g + pr, 4 * g + 2 * pr + m
                        last = mm(o[:, m * S:(m + 1) * S], qkT[rows, g, pr, 0, t * P:(t + 1) * P],
                                  qkT[rows, g, pr, 1, :], start=True, stop=a == 1)
                    if a == 0:
                        for m in range(2):
                            rows, hp = slice(64 * m, 64 * m + 64), 2 * g + pr
                            mm(o[:, m * S:(m + 1) * S], alibi_q[rows, hp, t * P:(t + 1) * P], alibi_k[rows, hp, :], start=False, stop=False)
                        for m in range(2):
                            last = diagonal(o, m, 4 * g + 2 * pr + m, t)
                    fill(last)

                def diagonal(o, m, h, t):
                    parts = 1 if h % 2 == 0 else 3
                    for n in range(parts):
                        last = mm(o[:, m * S + t * P:m * S + (t + 1) * P], identb[:], alibi_d[:, h, n, :], start=False, stop=n == parts - 1)
                    return last

                def scores2(a, g, t, pr):
                    o = claim(a, "s2", g, t, pr)
                    for m in range(2):
                        rows = slice(64 * m, 64 * m + 64)
                        last = mm(o[:, m * S:(m + 1) * S], qkT[rows, g, pr, 1, t * P:(t + 1) * P], qmT[rows, g % 2, pr, :], start=True, stop=a == 1)
                    if a == 0:
                        for m in range(2):
                            rows, hp = slice(64 * m, 64 * m + 64), 2 * g + pr
                            mm(o[:, m * S:(m + 1) * S], alibi_k[rows, hp, t * P:(t + 1) * P], alibi_q[rows, hp, :], start=False, stop=False)
                        for m in range(2):
                            last = diagonal(o, m, 4 * g + 2 * pr + m, t)
                    fill(last)

                def weighted(a, g, t):
                    n = 8 * g + 2 * t
                    pe.wait_ge(prob_ready, r * 64 + a * 32 + n + 2)
                    for j in range(4):
                        last = mm(pv_bank[g % 2][32 * j:32 * j + 32, :], v_aug[:, t, 4 * g + j, :], prob[:, (n + j // 2) % 4, j % 2, :],
                                  start=t == 0, stop=t == T - 1)
                    last.then_inc(pv_done, 1)

                def attention(a):
                    o = claim(a, "xT")
                    pe.wait_ge(*((x_in, r * 16 + 16) if a == 0 else (x_ready, r * 4 + 2)))
                    for t in range(T):
                        last = transpose(o[:, t * P:(t + 1) * P], x[:, t, :])
                    fill(last)
                    pe.wait_ge(xT_ready, r * 6 + 1 + a)
                    for i in range(2):
                        o = claim(a, "qkv", i)
                        for b in range(2):
                            t = 2 * i + b
                            last = mm(o[:, 512 * b:512 * b + 3 * D], xT[:, t * P:(t + 1) * P], wqkvT[:, a, :], start=True, stop=True)
                        fill(last)
                    pe.wait_ge(aug_a, r * 2 + a + 1)
                    pe.wait_ge(aug_g, r * 2 + a + 1)
                    for g in range(QUADS):
                        o = claim(a, "qkT", g)[:].bitcast(BF16)
                        for pr in range(2):
                            for side in range(2):
                                for t in range(T):
                                    c = (2 * pr + side) * S + t * P
                                    h0 = 4 * g + 2 * pr
                                    last = transpose(o[:, c:c + P], aug[:, side, t, h0:h0 + 2, :].rearrange("p h s -> p (h s)"), identb)
                        fill(last)
                    late = None
                    for kind, i in attention_order():
                        if kind == "s1":
                            if i[1:] == (0, 0):
                                pe.wait_ge(qkT_ready, r * 8 + a * 4 + i[0] + 1)
                            scores1(a, *i)
                        elif kind == "mT":
                            g, = i
                            o = claim(a, "mT", g)[:, 0:512].bitcast(BF16)
                            pe.wait_ge(maxq_ready, r * 8 + a * 4 + g + 1)
                            for pr in range(2):
                                for t in range(T):
                                    c, h0 = pr * S + t * P, 4 * g + 2 * pr
                                    last = transpose(o[:, c:c + P], aug[:, 0, t, h0:h0 + 2, :].rearrange("p h s -> p (h s)"), identb)
                            fill(last)
                        elif kind == "s2":
                            g, t, pr = i
                            if t == 0 and pr == 0:
                                pe.wait_ge(qmT_ready, r * 8 + a * 4 + g + 1)
                            scores2(a, *i)
                            if pr == 0 and late is not None:
                                weighted(a, *late)
                                late = None
                            if pr == 1:
                                late = (g, t)
                        elif kind == "oT":
                            g, = i
                            if g == QUADS - 1:
                                weighted(a, *late)
                            o = claim(a, "oT", g)
                            pe.wait_ge(oT_ready, r * 8 + a * 4 + g + 1)
                            for t in range(T):
                                last = transpose(o[:, t * P:(t + 1) * P], oT[:, g % 2, t * P:(t + 1) * P])
                            fill(last)
                    o = claim(a, "aT")
                    pe.wait_ge(att_ready, r * 8 + a * 4 + 4)
                    for t in range(T):
                        last = transpose(o[:, t * P:(t + 1) * P], att[:, t, :])
                    fill(last)
                    o = claim(a, "proj")
                    pe.wait_ge(attT_ready, r * 2 + a + 1)
                    for t in range(T):
                        last = mm(o[:, t * D:(t + 1) * D], attT[:, t * P:(t + 1) * P], woT[:, a, :], start=True, stop=True)
                    fill(last)

                def ffn4():
                    o = claim("f", "xqT")
                    pe.wait_ge(fq_q, r * 2 + 2)
                    for t in range(T):
                        last = transpose(o[:, t * P:(t + 1) * P], xq[:, t, :])
                    fill(last)
                    pe.wait_ge(fT_ready, r * 2 + 1)
                    for t in range(T):
                        o = claim("f", "gu", t)
                        for s in range(2):
                            last = mm(o[:, 512 * s:512 * s + INTER], xT[:, t * P:(t + 1) * P], wguT[:, s, :], start=True, stop=True)
                        fill(last)
                    pe.wait_ge(fq_q, r * 2 + 3)
                    for c, (c0, cw) in enumerate(ICH):
                        o = claim("f", "hT", c)
                        for t in range(T):
                            last = transpose(o[0:cw, t * P:(t + 1) * P], h4[:, t * INTER + c0:t * INTER + c0 + cw])
                        fill(last)
                    o = claim("f", "down")
                    pe.wait_ge(fT_ready, r * 2 + 2)
                    for t in range(T):
                        for c, (c0, cw) in enumerate(ICH):
                            last = mm(o[:, t * D:(t + 1) * D], hqT[0:cw, c, t * P:(t + 1) * P], wdT[0:cw, c, :], start=c == 0, stop=c == 2)
                    fill(last)

                def layer(l):
                    L = ("l", l)
                    o = claim(*L, "xT")
                    if l == 0:
                        pe.wait_ge(x_ready, r * 4 + 3)
                    else:
                        pe.wait_ge(y_ready, r * 4 + 2)
                    src = x if l == 0 else y
                    for t in range(T):
                        last = transpose(o[:, t * P:(t + 1) * P], src[:, t, :])
                    fill(last)
                    pe.wait_ge(xT_ready, r * 6 + 3 + 2 * l)
                    for kind, t in LOCAL_FRONT:
                        o = claim(*L, kind, t)
                        if kind == "qk":
                            for s in range(2):
                                last = mm(o[:, 512 * s:512 * s + 512], xT[:, t * P:(t + 1) * P], wl_qkv[:, l, 512 * s:512 * s + 512], start=True, stop=True)
                        elif kind == "v":
                            for b in range(2):
                                last = mm(o[:, 512 * b:512 * b + 512], xT[:, (2 * t + b) * P:(2 * t + b + 1) * P], wl_qkv[:, l, 1024:1536], start=True, stop=True)
                        else:
                            pe.wait_ge(lrot_ready, r * 8 + l * 4 + t + 1)
                            for c in range(8):
                                last = transpose(o[:, c * P:(c + 1) * P], lrs[:, t % 2, c // 4, 2 * (c % 4):2 * (c % 4) + 2, :].rearrange("p h d -> p (h d)"))
                        fill(last)
                    for t in range(T):
                        pe.wait_ge(lqkT_ready, r * 8 + l * 4 + t + 1)
                        k0 = t * P - WIN if t else 0
                        c0 = 0 if t else WIN
                        for q in range(2):
                            o = claim(*L, "s1", t, q)
                            for u in range(2):
                                for m in range(2):
                                    rows, pr = slice(64 * m, 64 * m + 64), 2 * q + u
                                    dst = o[:, 512 * m + BAND * u + c0:512 * m + BAND * (u + 1)]
                                    mm(dst, lqkT[rows, pr, t * P:(t + 1) * P], lqkT[rows, 4 + pr, k0:(t + 1) * P], start=True, stop=False)
                                for m in range(2):
                                    dst = o[:, 512 * m + BAND * u + c0:512 * m + BAND * (u + 1)]
                                    last = mm(dst, identb[:], band_q[:, c0:BAND], start=False, stop=True)
                            fill(last)
                    o = claim(*L, "mT")[:].bitcast(BF16)
                    pe.wait_ge(lm_ready, r * 2 + l + 1)
                    for c in range(4):
                        for t in range(T):
                            last = transpose(o[:, c * S + t * P:c * S + (t + 1) * P], lm[:, t, 2 * c:2 * c + 2, :].rearrange("p h s -> p (h s)"), identb)
                    fill(last)
                    pe.wait_ge(lmT_ready, r * 2 + l + 1)

                    def sums(t):
                        o = claim(*L, "pv", t)
                        pe.wait_ge(lprob_ready, r * 8 + l * 4 + t + 1)
                        for h in range(LH):
                            dst = o[:, 512 * (h // 4) + (LD + 1) * (h % 4):512 * (h // 4) + (LD + 1) * (h % 4 + 1)]
                            last = mm(dst, lprob[:, t % 2, h, 0:P], lv[:, t, h, :], start=True, stop=t == 0)
                            if t:
                                last = mm(dst, lprob[WIN:P, (t - 1) % 2, h, P:2 * P], lv[WIN:P, t - 1, h, :], start=False, stop=True)
                        fill(last)

                    pe.wait_ge(lv_ready, r * 2 + l + 1)
                    for t in range(T):
                        w = BAND if t < T - 1 else P
                        for q in range(2):
                            o = claim(*L, "s2", t, q)
                            for u in range(2):
                                for m in range(2):
                                    rows, pr = slice(64 * m, 64 * m + 64), 2 * q + u
                                    dst = o[:, 512 * m + BAND * u:512 * m + BAND * u + w]
                                    mm(dst, lqkT[rows, 4 + pr, t * P:(t + 1) * P], lqkT[rows, pr, t * P:t * P + w], start=True, stop=False)
                                for m in range(2):
                                    rows, pr = slice(64 * m, 64 * m + 64), 2 * q + u
                                    dst = o[:, 512 * m + BAND * u:512 * m + BAND * u + w]
                                    mm(dst, ones_m[rows, :], lmT[rows, pr, t * P:t * P + w], start=False, stop=False)
                                for m in range(2):
                                    dst = o[:, 512 * m + BAND * u:512 * m + BAND * u + w]
                                    last = mm(dst, identb[:], band_k[:, 0:w], start=False, stop=True)
                            fill(last)
                        if t:
                            sums(t - 1)
                    sums(T - 1)
                    pe.wait_ge(lo_ready, r * 2 + l + 1)
                    for i in range(2):
                        o = claim(*L, "oT", i)
                        for b in range(2):
                            for c in range(4):
                                last = transpose(o[:, (4 * b + c) * P:(4 * b + c + 1) * P], lo[:, 2 * i + b, c * P:(c + 1) * P])
                        fill(last)
                    o = claim(*L, "wo")
                    pe.wait_ge(loT_ready, r * 2 + l + 1)
                    for t in range(T):
                        for c in range(4):
                            last = mm(o[:, t * D:(t + 1) * D], loT[:, c, t * P:(t + 1) * P], wl_o[:, l, c, :], start=c == 0, stop=c == 3)
                    fill(last)
                    o = claim(*L, "x2T")
                    pe.wait_ge(y_ready, r * 4 + 2 * l + 1)
                    for t in range(T):
                        last = transpose(o[:, t * P:(t + 1) * P], y[:, t, :])
                    fill(last)
                    o = claim(*L, "hB")
                    pe.wait_ge(xT_ready, r * 6 + 4 + 2 * l)
                    for t in range(T):
                        last = transpose(o[:, t * P:(t + 1) * P], xT[:, t * P:(t + 1) * P])
                    fill(last)
                    o = claim(*L, "hT")
                    pe.wait_ge(h_back, r * 2 + l + 1)
                    for t in range(T):
                        last = transpose(o[:, t * P:(t + 1) * P], hn[:, t, :])
                    fill(last)
                    pe.wait_ge(hT_ready, r * 2 + l + 1)
                    for c, (c0, cw) in enumerate(HCH):
                        o = claim(*L, "w1", c)
                        for s in range(2):
                            last = mm(o[0:cw, 512 * s:512 * s + 512], w1[:, l, s * HID + c0:s * HID + c0 + cw], xT[:], start=True, stop=True)
                        fill(last)
                    o = claim(*L, "w2")
                    pe.wait_ge(hid_ready, r * 2 + l + 1)
                    for t in range(T):
                        for c, (c0, cw) in enumerate(HCH):
                            last = mm(o[:, t * D:(t + 1) * D], hid[0:cw, c, t * P:(t + 1) * P], w2[0:cw, l, c, :], start=c == 0, stop=c == 2)
                    fill(last)

                attention(0)
                ffn4()
                attention(1)
                layer(0)
                layer(1)


def constants():
    import numpy as np
    bf = mybir.dt.np(BF16)
    f32 = np.float32

    def parts(v):
        v = np.asarray(v, f32)
        out = []
        for _ in range(3):
            p = v.astype(bf)
            out.append(p)
            v = v - p.astype(f32)
        return out

    slopes = (2.0 ** (8.0 * np.arange(0, -H, -1, dtype=f32) / H)).astype(f32)
    pos = np.arange(S)
    tile, centred = pos // P, (pos - S // 2).astype(f32)
    alibi_q, alibi_k = np.zeros((P, PAIRS, S), f32), np.zeros((P, PAIRS, S), f32)
    alibi_d = np.zeros((P, H, 3, P), bf)
    within = np.arange(P)
    dist = np.abs(within[:, None] - within[None, :]).astype(f32)
    for h in range(H):
        pr, row0 = h // 2, SLOTS * (h % 2)
        for c in range(T):
            sign = np.sign(tile - c).astype(f32)
            here = (tile == c).astype(f32)
            for i, s in enumerate(parts(slopes[h])):
                s = float(s)
                alibi_q[row0 + 6 * c + i, pr], alibi_k[row0 + 6 * c + i, pr] = sign * centred, -s * here
                alibi_q[row0 + 6 * c + 3 + i, pr], alibi_k[row0 + 6 * c + 3 + i, pr] = sign * s, centred * here
        for i, p in enumerate(parts(-slopes[h] * dist)):
            alibi_d[:, h, i, :] = p
    band = np.arange(BAND)
    gap_q = within[:, None] - (band[None, :] - WIN)
    gap_k = band[None, :] - within[:, None]
    mask = lambda gap: np.where((gap >= 0) & (gap <= WIN), 0.0, -1e30).astype(bf)
    ones_m = np.zeros((P, P), bf)
    for m in range(2):
        ones_m[SLOTS * m:SLOTS * m + 3] = 1
    half = np.arange(0, LD, 2, dtype=f32)
    inv = (1.0 / 10000.0 ** (half / LD)).astype(f32)
    t = np.arange(S, dtype=f32)
    freqs = np.tile(t[:, None] * inv[None, :], (1, 2))
    base = ((half + 0.4 * LD) / (1.4 * LD)).astype(f32)
    scale = np.tile(base[None, :] ** ((t - S // 2) / f32(WIN // 2))[:, None], (1, 2)).astype(f32)
    sign = np.where(np.arange(LD) < LD // 2, -1.0, 1.0).astype(f32)
    lay = lambda q, k: np.ascontiguousarray(np.stack([q, k], 1).reshape(T, P, 2, LD).transpose(1, 0, 2, 3).astype(f32))
    cos, sin = np.cos(freqs).astype(f32), np.sin(freqs).astype(f32)
    return {
        "ident": np.eye(P, dtype=f32), "identb": np.eye(P).astype(bf),
        "alibi_q": alibi_q.astype(bf), "alibi_k": alibi_k.astype(bf), "alibi_d": alibi_d,
        "band_q": mask(gap_q), "band_k": mask(gap_k), "ones_m": ones_m,
        "rot_c": lay(cos * scale * 8, cos / scale), "rot_s": lay(sign * sin * scale * 8, sign * sin / scale),
    }


NAMES = {
    "x": "L0_attn_x", "wqkv0": "L0_attn_W_qkv", "bqkv0": "L0_attn_b_qkv", "wo0": "L0_attn_W_out", "bo0": "L0_attn_b_out",
    "wgate": "L0_ffn_w_gate", "wup": "L0_ffn_w_up", "wdown": "L0_ffn_w_down",
    "wqkv1": "L1_attn_W_qkv", "bqkv1": "L1_attn_b_qkv", "wo1": "L1_attn_W_proj", "bo1": "L1_attn_b_proj",
    "wl_qkv": "L1_ffn_wqkv", "q_scale": "L1_ffn_q_scale", "k_scale": "L1_ffn_k_scale", "wl_o": "L1_ffn_wo",
    "ln_g": "L1_ffn_ln_g", "ln_b": "L1_ffn_ln_b", "w1": "L1_ffn_w1", "b1": "L1_ffn_b1", "w2": "L1_ffn_w2", "b2": "L1_ffn_b2",
}


def kernel(**inputs):
    import concourse.bacc as bacc
    import numpy as np
    from concourse.bass_utils import run_bass_kernel_spmd

    nc = bacc.Bacc("TRN2", target_bir_lowering=False, num_devices=1)
    arrays = {k: np.ascontiguousarray(inputs[v]) for k, v in NAMES.items()} | constants()
    ins = {k: nc.dram_tensor(f"in_{k}", a.shape, mybir.dt.from_np(a.dtype), kind="ExternalInput").ap() for k, a in arrays.items()}
    out = nc.dram_tensor("out", (SEQS, S, D), F32, kind="ExternalOutput").ap()
    build(nc, ins, out)
    r = run_bass_kernel_spmd(nc, [{f"in_{k}": a for k, a in arrays.items()}], core_ids=[0])
    return r.results[0]["out"]
```

```python
from contextlib import ExitStack

import concourse.bass as bass
from concourse import mybir

F32 = mybir.dt.float32
BF16 = mybir.dt.bfloat16
ALU = mybir.AluOpType
ACT = mybir.ActivationFunctionType
AX = mybir.AxisListType.X

P = 128
SEQS, S, D = 8, 512, 128
T = S // P
H, HD = 16, 8
PAIRS, QUADS = H // 2, H // 4
SLOTS = 64
INTER = 352
ICH = [(0, 128), (128, 128), (256, 96)]
FB = 16
LAYERS, LH, LD = 2, 8, 64
WIN = 64
BAND = P + WIN
HID = 341
HCH = [(0, 128), (128, 128), (256, 85)]
EPS = 1e-5
Q_PART = [0, 0, 1, 1, 0, 2]
K_PART = [0, 1, 0, 1, 2, 0]
M_SLOT = 8 * len(Q_PART)
B_SLOT = M_SLOT + 3
ROWS = [B_SLOT + 2 * T, B_SLOT]

LOCAL_FRONT = [("qk", 0), ("qk", 1), ("ro", 0), ("rT", 0), ("qk", 2), ("ro", 1), ("rT", 1), ("qk", 3), ("ro", 2), ("rT", 2),
               ("v", 0), ("ro", 3), ("rT", 3), ("v", 1)]


def front_steps():
    steps = []
    for a in range(2):
        steps += [((a, "xT"), 2, True)] + [((a, "qkv", i), 3, True) for i in range(2)]
        steps += [((a, "aug", i), 4, False) for i in range(3)]
        steps += [((a, "qkT", g), 2, True) for g in range(QUADS)]
        steps += [((a, kind) + i, 1.2, True) for kind, i in attention_order()]
        steps += [((a, "aT"), 2, True), ((a, "proj"), 4, True), ((a, "norm"), 2, False)]
        if a == 0:
            steps += [(("f", "q1", i), 2, False) for i in range(3)] + [(("f", "xqT"), 2, True)]
            steps += [(("f", "gu", t), 0 if t else 8, True) for t in range(T)]
            steps += [(("f", "q2", i), 5, False) for i in range(3)]
            steps += [(("f", "hT", c), 2, True) for c in range(3)] + [(("f", "down"), 4, True), (("f", "norm"), 2, False)]
    return steps


def back_steps():
    steps = []
    for l in range(LAYERS):
        steps += [(("l", l, "xT"), 2, True)]
        steps += [(("l", l) + i, 3.5, i[0] != "ro") for i in LOCAL_FRONT]
        steps += [(("l", l, "s1", t, q), 1.5, True) for t in range(T) for q in range(2)]
        steps += [(("l", l, "m"), 2, False), (("l", l, "mT"), 2, True)]
        for t in range(T):
            steps += [(("l", l, "s2", t, q), 1.5, True) for q in range(2)] + [(("l", l, "pv", t), 2, True)]
        steps += [(("l", l, "oT", i), 2, True) for i in range(2)] + [(("l", l, "wo"), 3, True)]
        steps += [(("l", l, "x2T"), 2, True), (("l", l, "hB"), 3, True), (("l", l, "norm"), 2, False), (("l", l, "hT"), 3, True)]
        steps += [(("l", l, "w1", c), 0 if c else 6, True) for c in range(3)] + [(("l", l, "w2"), 3, True)]
    return steps + [(("end", i), 2, False) for i in range(2)]


def merged(*streams):
    timed = []
    for n, steps in enumerate(streams):
        total, at = sum(c for _, c, _ in steps), 0
        for i, (step, cost, fills) in enumerate(steps):
            at += cost
            timed.append((at / total, n, i, step, fills))
    return [(step, fills) for _, _, _, step, fills in sorted(timed, key=lambda t: t[:3])]


class Segment:

    def __init__(self, order, before):
        self.order = [step for step, _ in order]
        items = [step for step, fills in order if fills]
        assert len(items) % 3 == 0 and len(set(items)) == len(items)
        self.index = {name: i for i, name in enumerate(items)}
        self.n, self.before = len(items), before

    def slot(self, name):
        return self.index[name] % 3

    def filled(self, name, turn):
        return turn * self.n + self.before + self.index[name] + 1

    def freed(self, name, turn):
        return turn * (self.n // 3) + self.before // 3 + self.index[name] // 3

    def used(self, name, turn):
        return self.freed(name, turn) + 1

    def needs(self, turn, names, claim=None):
        need = {} if claim is None else {self.slot(claim): self.index[claim] // 3}
        for name in names:
            need[self.slot(name)] = max(need.get(self.slot(name), 0), self.index[name] // 3 + 1)
        return [(slot, turn * (self.n // 3) + self.before // 3 + count) for slot, count in need.items()]


def run_steps(segment, *streams):
    pending = [[g, next(g, None)] for g in streams]
    for step in segment.order:
        for p in pending:
            if p[1] == step:
                p[1] = next(p[0], None)
    assert all(p[1] is None for p in pending), [p[1] for p in pending]


def attention_order():
    units = [(i, pr) for i in range(T) for pr in range(2)]
    out = [("s1", (0,) + u) for u in units]
    for g in range(QUADS):
        ahead = [("s1", (g + 1,) + u) for u in units] if g + 1 < QUADS else []
        out += ahead[:3] + [("mT", (g,))]
        rest = ahead[3:]
        for n, u in enumerate(units):
            out += [("s2", (g,) + u)] + rest[:1]
            rest = rest[1:]
            if n == 2 and g:
                out += [("oT", (g - 1,))]
    out += [("oT", (QUADS - 1,))]
    return out


def build(nc, ins, out, seqs=SEQS):
    ctx = ExitStack()
    with ctx:
        def sb(name, shape, dt=F32):
            return ctx.enter_context(nc.sbuf_tensor(name, shape, dt))

        def sem(name):
            return ctx.enter_context(nc.semaphore(name))

        ring = [ctx.enter_context(nc.psum_tensor(f"ring{i}", [P, 1024], F32)) for i in range(3)]
        pv_bank = [ctx.enter_context(nc.psum_tensor(f"pv_bank{i}", [P, 512], F32)) for i in range(2)]
        PREP = 3
        FRONT, BACK = front_steps(), back_steps()
        n_front, n_back = (sum(f for _, _, f in s) for s in (FRONT, BACK))
        FIRST = Segment(merged(FRONT), PREP)
        BOTH = Segment(merged(FRONT, BACK), PREP + n_front)
        LAST = Segment(merged(BACK), PREP + n_front + (seqs - 1) * (n_front + n_back))

        ident = sb("ident", [P, P])
        identb = sb("identb", [P, P], BF16)
        alibi_xq = sb("alibi_xq", [P, 2, S], BF16)
        alibi_xk = sb("alibi_xk", [P, 2, S], BF16)
        alibi_d = sb("alibi_d", [P, 4 * PAIRS, P], BF16)
        band_q = sb("band_q", [P, BAND], BF16)
        band_k = sb("band_k", [P, BAND], BF16)
        ones_m = sb("ones_m", [P, P], BF16)
        wqkvT = sb("wqkvT", [P, 2, 3 * D])
        woT = sb("woT", [P, 2, D])
        bqkv = sb("bqkv", [P, 2, 3 * D])
        bo = sb("bo", [P, 2, D])
        wguT = sb("wguT", [P, 2, INTER])
        wdT = sb("wdT", [P, 3, D])
        wl_qkv = sb("wl_qkv", [P, LAYERS, 3 * LH * LD])
        wl_o = sb("wl_o", [P, LAYERS, 4, D])
        w1 = sb("w1", [P, LAYERS, 2 * HID])
        w2 = sb("w2", [P, LAYERS, 3, D])
        b1 = sb("b1", [P, LAYERS, 2, 3])
        b2 = sb("b2", [P, LAYERS, D])
        ln_g = sb("ln_g", [P, LAYERS])
        ln_b = sb("ln_b", [P, LAYERS])
        rot_c = sb("rot_c", [P, LAYERS, T, 2, LD])
        rot_s = sb("rot_s", [P, LAYERS, T, 2, LD])
        neg_half = sb("neg_half", [P, 16])
        zeros = sb("zeros", [P, 64])

        x_next = sb("x_next", [P, T, D])
        x = sb("x", [P, T, D])
        y = sb("y", [P, T, D])
        xT = sb("xT", [P, S])
        stats = [sb(f"stats{i}", [P, T, 6]) for i in range(2)]
        mv = [sb(f"mv{i}", [P, T, 2]) for i in range(2)]
        rstd = [sb(f"rstd{i}", [P, T]) for i in range(2)]
        fbig = sb("fbig", [P, 10 * 1024])
        qk = fbig[:, 0:1024].rearrange("p (t s c) -> p t s c", t=T, s=2)
        part0 = sb("part0", [P, T, 2, D], BF16)
        part1, part2 = (fbig[:, 6144 + 512 * i:6656 + 512 * i].bitcast(BF16).rearrange("p (t s c) -> p t s c", t=T, s=2)
                        for i in range(2))
        aug = sb("aug", [P, 2, T, H, SLOTS], BF16)
        v_aug = sb("v_aug", [P, T, H, 32])
        qkT = fbig[:, 1024:5120].bitcast(BF16).rearrange("p (g b c s) -> p g b c s", g=QUADS, b=2, c=2)
        qmT = fbig[:, 5120:6144].bitcast(BF16).rearrange("p (g b s) -> p g b s", g=2, b=2)
        neg_max = sb("neg_max", [P, QUADS, T, 4])
        max_r1 = sb("max_r1", [P, T, 4])
        prob = fbig[:, 6144:10240].rearrange("p (n m s) -> p n m s", n=4, m=2)
        oT = sb("oT", [P, 2, S])
        rsum = sb("rsum", [P, T * 4])
        att = sb("att", [P, T, D])
        attT = xT
        n4 = T * INTER
        h4 = fbig[:, 0:n4]
        a4 = fbig[:, n4:2 * n4]
        s4 = fbig[:, 2 * n4:3 * n4]
        c4 = fbig[:, 3 * n4:4 * n4]
        d4 = fbig[:, 4 * n4:5 * n4]
        hqT = fbig[:, 5 * n4:5 * n4 + 3 * S].rearrange("p (c s) -> p c s", c=3)
        silu = fbig[:, 5 * n4 + 3 * S:5 * n4 + 3 * S + 2 * INTER].rearrange("p (c s) -> p c s", c=2)
        amax = sb("amax", [P, n4 // FB])
        fscale = sb("fscale", [P, n4 // FB])
        finv = sb("finv", [P, n4 // FB])

        xb = sb("xb", [P, T, D])
        yb = sb("yb", [P, T, D])
        res = sb("res", [P, T, D])
        xTb = sb("xTb", [P, S])
        bbig = sb("bbig", [P, 10 * 1024])
        lqk = bbig[:, 0:2048].rearrange("p (b s h d) -> p b s h d", b=2, s=2, h=LH)
        lsq = bbig[:, 2048:4096].rearrange("p (b s h d) -> p b s h d", b=2, s=2, h=LH)
        lrs = bbig[:, 4096:6144].rearrange("p (b s h d) -> p b s h d", b=2, s=2, h=LH)
        lqkT = bbig[:, 6144:10240].rearrange("p (c s) -> p c s", c=8)
        lprob = bbig[:, 0:4096].rearrange("p (b h q) -> p b h q", b=2, h=LH)
        lo = bbig[:, 4096:6144].rearrange("p (t c) -> p t c", t=T)
        loT = bbig[:, 6144:8192].rearrange("p (c s) -> p c s", c=4)
        gel = bbig[:, 0:1536].rearrange("p (c s) -> p c s", c=3)
        hid = bbig[:, 1536:3072].rearrange("p (c s) -> p c s", c=3)
        hn = bbig[:, 3072:3584].rearrange("p (t c) -> p t c", t=T)
        lv = sb("lv", [P, T, LH, LD + 1])
        lss = sb("lss", [P, T, 16])
        lrn = sb("lrn", [P, T, 16])
        lneg = sb("lneg", [P, T, LH])
        lm_r1 = sb("lm_r1", [P, T * LH])
        lm = sb("lm", [P, T, LH, SLOTS], BF16)
        lmT = sb("lmT", [P, 4, S], BF16)
        lrsum = sb("lrsum", [P, T, LH])

        w_attn = sem("w_attn")
        w_rest = sem("w_rest")
        x_in = sem("x_in")
        out_done = sem("out_done")
        filled = sem("filled")
        freed = [sem(f"freed{i}") for i in range(3)]
        prep_v = sem("prep_v")
        prep_a = sem("prep_a")
        prep_g = sem("prep_g")
        qkv_ready = sem("qkv_ready")
        hi_ready = sem("hi_ready")
        r1_ready = sem("r1_ready")
        mid_ready = sem("mid_ready")
        aug_a = sem("aug_a")
        aug_g = sem("aug_g")
        maxq_ready = sem("maxq_ready")
        pv_done = sem("pv_done")
        oT_ready = sem("oT_ready")
        x_ready = sem("x_ready")
        fq_x = sem("fq_x")
        fq_s = sem("fq_s")
        fq_g = sem("fq_g")
        fq_q = sem("fq_q")
        hqT_ready = sem("hqT_ready")
        silu_ready = sem("silu_ready")
        var_ready = [sem("var_front"), sem("var_back")]
        rstd_ready = [sem("rstd_front"), sem("rstd_back")]
        xTb_ready = sem("xTb_ready")
        lraw_ready = sem("lraw_ready")
        lss_ready = sem("lss_ready")
        lrn_ready = sem("lrn_ready")
        lsin_ready = sem("lsin_ready")
        lrot_ready = sem("lrot_ready")
        lv_ready = sem("lv_ready")
        lm_ready = sem("lm_ready")
        lo_ready = sem("lo_ready")
        loT_ready = sem("loT_ready")
        h_back = sem("h_back")
        gel_ready = sem("gel_ready")
        hid_ready = sem("hid_ready")
        out_ready = sem("out_ready")

        block = ctx.enter_context(nc.Block())
        N_ATTN = 11
        N_REST = 46
        NW = (6 * 8 + 22) * FB
        NBW = NW // FB

        def program(eng, front, back):
            run_steps(FIRST, front(FIRST, 0, 0))
            with eng.Fori(0, seqs - 1) as r:
                run_steps(BOTH, front(BOTH, r, r + 1), back(BOTH, r, r))
            run_steps(LAST, back(LAST, 0, seqs - 1))

        @block.sync
        def _(sp):
            count = {"a": 0, "r": 0}

            def load_a(dst, src):
                sp.dma_start(dst, src).then_inc(w_attn, 16)
                count["a"] += 1

            def load(dst, src):
                sp.dma_start(dst, src).then_inc(w_rest, 16)
                count["r"] += 1

            rows = lambda n: ins["x"][n].rearrange("o (t p) d -> p (o t) d", p=P)
            load_a(ident[:], ins["ident"])
            load_a(y[:, 0:3, :], ins["wqkv0"].rearrange("(c p) d -> p c d", p=P))
            load_a(yb[:, 0:3, :], ins["wqkv1"].rearrange("(c p) d -> p c d", p=P))
            load_a(y[:, 3, :], ins["wo0"])
            load_a(yb[:, 3, :], ins["wo1"])
            sp.dma_start(x_next[:], rows(slice(0, 1))).then_inc(x_in, 16)
            for a in range(2):
                load_a(bqkv[:, a, :], ins[f"bqkv{a}"].rearrange("(o n) -> o n", o=1).broadcast_to([P, 3 * D]))
                load_a(bo[:, a, :], ins[f"bo{a}"].rearrange("(o n) -> o n", o=1).broadcast_to([P, D]))
            load_a(identb[:], ins["identb"])
            load_a(part0[:].rearrange("p t s c -> p (t s c)"), ins["alibi_b"])
            load(alibi_d[:], ins["alibi_d"])
            load(alibi_xq[:], ins["alibi_xq"])
            load(alibi_xk[:], ins["alibi_xk"])
            load(band_q[:], ins["band_q"])
            load(band_k[:], ins["band_k"])
            load(ones_m[:], ins["ones_m"])
            for l in range(LAYERS):
                load(rot_c[:, l], ins["rot_c"])
                load(rot_s[:, l], ins["rot_s"])
            load(wl_qkv[:], ins["wl_qkv"].rearrange("l d n -> d l n"))
            for l in range(LAYERS):
                load(wl_o[:, l], ins["wl_o"][l].rearrange("(c p) n -> p c n", p=P))
            assert count == {"a": N_ATTN, "r": 13}
            sp.wait_ge(x_ready, 1)
            sp.dma_start(x_next[:], rows(slice(1, 2))).then_inc(x_in, 16)
            with sp.Fori(0, seqs - 2) as i:
                sp.wait_ge(x_ready, 3 * (i + 1) + 1)
                sp.dma_start(x_next[:], rows(bass.ds(i + 2, 1))).then_inc(x_in, 16)
                sp.wait_ge(out_ready, i + 1)
                sp.dma_start(out[bass.ds(i, 1)].rearrange("o (t p) d -> p (o t) d", p=P), res[:]).then_inc(out_done, 16)
            for i in range(seqs - 2, seqs):
                sp.wait_ge(out_ready, i + 1)
                sp.dma_start(out[i:i + 1].rearrange("o (t p) d -> p (o t) d", p=P), res[:]).then_inc(out_done, 16)
            sp.wait_ge(out_done, 16 * (seqs + 1))

        @block.gpsimd
        def _(pool):
            G = nc.gpsimd
            G.memset(aug[:], 0.0)
            G.memset(v_aug[:], 0.0)
            G.memset(neg_half[:], -0.5)
            G.memset(zeros[:], 0.0)
            pool.drain()
            G.memset(aug[:, 1, :, :, M_SLOT:M_SLOT + 3], 1.0)
            G.memset(v_aug[:, :, :, HD:HD + 1], 1.0)
            pool.wait_ge(w_attn, 16 * N_ATTN)
            for side in range(2):
                G.tensor_copy(aug[:, side, :, :, B_SLOT:B_SLOT + 2 * T].rearrange("p t h s -> p (t h) s"),
                              part0[:].rearrange("p t s c -> p (t s c)")[:, side * 512:(side + 1) * 512].rearrange("p (n s) -> p n s", s=2 * T))
            pool.drain().then_inc(prep_g, 1)
            G.memset(lm[:], 0.0)
            G.memset(lv[:], 1.0)
            s4b = s4[:, 0:NW].rearrange("p (b f) -> p b f", f=FB)
            pool.wait_ge(fq_s, 1)
            G.tensor_tensor(s4b, s4b, fscale[:, 0:NBW].unsqueeze(2).broadcast_to([P, NBW, FB]), ALU.mult).then_inc(fq_g, 1)

            def rsqrt(side, value):
                pool.wait_ge(var_ready[side], value)
                G.tensor_tensor(rstd[side][:], mv[side][:, :, 1], neg_half[:, 0:T], ALU.pow).then_inc(rstd_ready[side], 1)

            def front(seg, turn, n):
                def maxima(*names):
                    for slot, count in seg.needs(turn, names):
                        pool.wait_ge(freed[slot], count)

                def fp4_scale(k, cols):
                    nb = cols // FB
                    s = s4[:, 0:cols].rearrange("p (b f) -> p b f", f=FB)
                    pool.wait_ge(fq_s, n * 2 + 1 + k)
                    G.tensor_tensor(s, s, fscale[:, 0:nb].unsqueeze(2).broadcast_to([P, nb, FB]), ALU.mult).then_inc(fq_g, 1)

                def attention(a):
                    flat = lambda t: t.rearrange("p t s c -> p (t s c)")
                    yield (a, "aug", 1)
                    pool.wait_ge(hi_ready, n * 2 + a + 1)
                    G.tensor_tensor(flat(qk), flat(qk), flat(part0[:]), ALU.subtract).then_inc(r1_ready, 1)
                    yield (a, "aug", 2)
                    pool.wait_ge(mid_ready, n * 2 + a + 1)
                    G.tensor_tensor(flat(part2), flat(qk), flat(part1), ALU.subtract)
                    pool.drain()
                    for side, parts in ((0, Q_PART), (1, K_PART)):
                        for k, part in enumerate(parts):
                            if part:
                                G.tensor_copy(aug[:, side, :, :, 8 * k:8 * k + 8],
                                              (part1, part2)[part - 1][:, :, side, :].rearrange("p t (h d) -> p t h d", d=HD))
                    pool.drain().then_inc(aug_g, 1)
                    for g in range(QUADS):
                        yield (a, "mT", g)
                        maxima(*((a, "s1", g, t, pr) for t in range(T) for pr in range(2)))
                        part = lambda k: aug[:, 0, :, 4 * g:4 * g + 4, M_SLOT + k]
                        zero = zeros[:, 0:16].rearrange("p (t h) -> p t h", t=T)
                        G.tensor_tensor(part(0), neg_max[:, g], zero, ALU.add)
                        pool.drain()
                        G.tensor_tensor(max_r1[:], neg_max[:, g], part(0), ALU.subtract)
                        pool.drain()
                        G.tensor_copy(part(1), max_r1[:])
                        pool.drain()
                        G.tensor_tensor(part(2), max_r1[:], part(1), ALU.subtract)
                        pool.drain().then_inc(maxq_ready, 1)
                    yield (a, "proj")
                    pool.wait_ge(filled, seg.filled((a, "mT", QUADS - 1), turn))
                    zero = zeros[:].rearrange("p (t h) -> p t h", t=T)
                    for k in range(3):
                        G.tensor_tensor(aug[:, 0, :, :, M_SLOT + k], zero, zero, ALU.add)
                    pool.drain()
                    rsqrt(0, n * 3 + 1 + 2 * a)

                yield from attention(0)
                yield ("f", "q1", 1)
                fp4_scale(1, T * D)
                yield ("f", "q2", 1)
                fp4_scale(2, n4)
                yield ("f", "down")
                rsqrt(0, n * 3 + 2)
                yield from attention(1)

            def back(seg, turn, n):
                for l in range(LAYERS):
                    for kind, t in LOCAL_FRONT:
                        if kind != "qk":
                            continue
                        yield ("l", l, "qk", t)
                        pool.wait_ge(lraw_ready, n * 8 + l * 4 + t + 1)
                        pool.wait_ge(lss_ready, n * 8 + l * 4 + t + 1)
                        G.tensor_tensor(lrn[:, t, :], lss[:, t, :], neg_half[:, 0:16], ALU.pow).then_inc(lrn_ready, 1)
                        for half in range(2):
                            for side in range(2):
                                last = G.tensor_tensor(
                                    lsq[:, t % 2, side, :, 32 * half:32 * half + 32],
                                    lqk[:, t % 2, side, :, 32 - 32 * half:64 - 32 * half],
                                    rot_s[:, l, t, side, 32 * half:32 * half + 32].unsqueeze(1).broadcast_to([P, LH, 32]),
                                    ALU.mult)
                        pool.drain().then_inc(lsin_ready, 1)
                    yield ("l", l, "m")
                    for slot, count in seg.needs(turn, [("l", l, "s1", t, q) for t in range(T) for q in range(2)]):
                        pool.wait_ge(freed[slot], count)
                    lmf = lm[:].rearrange("p t h s -> p (t h) s")
                    lnf = lneg[:].rearrange("p t h -> p (t h)")
                    G.tensor_tensor(lmf[:, :, 0], lnf, zeros[:, 0:T * LH], ALU.add)
                    G.memset(lprob[:, :, :, BAND:256], 0.0)
                    pool.drain()
                    G.tensor_tensor(lm_r1[:], lnf, lmf[:, :, 0], ALU.subtract)
                    pool.drain()
                    G.tensor_copy(lmf[:, :, 1], lm_r1[:])
                    pool.drain()
                    G.tensor_tensor(lmf[:, :, 2], lm_r1[:], lmf[:, :, 1], ALU.subtract)
                    pool.drain().then_inc(lm_ready, 1)
                    yield ("l", l, "hB")
                    rsqrt(1, n * 3 + 1 + l)
                yield ("end", 0)
                rsqrt(1, n * 3 + 3)

            program(pool, front, back)

        @block.scalar
        def _(act):
            count = [0]

            def load(dst, src, **k):
                act.dma_start(dst, src, **k).then_inc(w_rest, 16)
                count[0] += 1

            load(h4[:, 0:256].rearrange("p (c d) -> p c d", c=2), ins["wgate"][0:256, :].rearrange("(c p) d -> p c d", p=P))
            load(h4[0:96, 256:384], ins["wgate"][256:352, :])
            load(h4[:, 384:640].rearrange("p (c d) -> p c d", c=2), ins["wup"][0:256, :].rearrange("(c p) d -> p c d", p=P))
            load(h4[0:96, 640:768], ins["wup"][256:352, :])
            load(h4[:, 768:768 + INTER], ins["wdown"])
            load(w1[:], ins["w1"].rearrange("l d n -> d l n"))
            for c, (c0, cw) in enumerate(HCH):
                load(w2[0:cw, :, c, :], ins["w2"][:, c0:c0 + cw, :].rearrange("l p n -> p l n"))
                for side in range(2):
                    load(b1[0:cw, :, side, c], ins["b1"][:, side * HID + c0:side * HID + c0 + cw].rearrange("l p -> p l"),
                         allow_slow_non_contiguous=True)
            for l in range(LAYERS):
                load(b2[:, l, :], ins["b2"][l:l + 1, :].broadcast_to([P, D]))
                load(ln_g[:, l:l + 1], ins["ln_g"][l:l + 1, :].rearrange("l p -> p l"), allow_slow_non_contiguous=True)
                load(ln_b[:, l:l + 1], ins["ln_b"][l:l + 1, :].rearrange("l p -> p l"), allow_slow_non_contiguous=True)
            for l in range(LAYERS):
                for side, name in ((0, "q_scale"), (1, "k_scale")):
                    load(c4[:, (2 * l + side) * LD:(2 * l + side + 1) * LD], ins[name][l:l + 1, :].broadcast_to([P, LD]))
                    for half in range(2):
                        o = 4 * LD + (2 * l + side) * LD + 32 * half
                        load(c4[:, o:o + 32], ins[name][l:l + 1, 32 - 32 * half:64 - 32 * half].broadcast_to([P, 32]))
            assert count[0] + 13 == N_REST, count

            def copy(dst, src, func=ACT.Copy, **k):
                return nc.scalar.activation(dst, src, func, **k)

            act.wait_ge(filled, 1)
            copy(wqkvT[:, 0, :], ring[0][:, 0:384])
            copy(wqkvT[:, 1, :], ring[0][:, 384:768])
            copy(woT[:].rearrange("p a d -> p (a d)"), ring[0][:, 768:1024]).then_inc(freed[0], 1)
            act.wait_ge(fq_x, 1)
            copy(s4[:, 0:NW], a4[:, 0:NW], ACT.Sign)
            act.drain()
            copy(a4[:, 0:NW], a4[:, 0:NW], ACT.Abs).then_inc(fq_s, 1)
            act.wait_ge(filled, 2)
            copy(wguT[:, 0, :], ring[1][:, 0:INTER])
            copy(wguT[:, 1, :], ring[1][:, 512:512 + INTER]).then_inc(freed[1], 1)
            act.wait_ge(filled, 3)
            copy(wdT[:, 0:2, :].rearrange("p c d -> p (c d)"), ring[2][:, 0:256])
            copy(wdT[0:96, 2, :], ring[2][0:96, 256:384]).then_inc(freed[2], 1)
            act.drain().then_inc(prep_a, 1)

            def front(seg, turn, n):
                def take(*name):
                    act.wait_ge(filled, seg.filled(name, turn))
                    return ring[seg.slot(name)]

                def release(ins_, *name):
                    ins_.then_inc(freed[seg.slot(name)], 1)
                    return ins_

                def attention(a):
                    yield (a, "xT")
                    release(copy(xT[:], take(a, "xT")[:, 0:S]), a, "xT")
                    flat = lambda t: t.rearrange("p t s c -> p (t s c)")
                    yield (a, "aug", 0)
                    act.wait_ge(qkv_ready, n * 2 + a + 1)
                    copy(flat(part0[:]), flat(qk)).then_inc(hi_ready, 1)
                    act.drain()
                    for side, parts in ((0, Q_PART), (1, K_PART)):
                        for k, part in enumerate(parts):
                            if part == 0:
                                copy(aug[:, side, :, :, 8 * k:8 * k + 8],
                                     part0[:, :, side, :].rearrange("p t (h d) -> p t h d", d=HD))
                    act.drain().then_inc(aug_a, 1)
                    yield (a, "aug", 1)
                    act.wait_ge(r1_ready, n * 2 + a + 1)
                    copy(flat(part1), flat(qk)).then_inc(mid_ready, 1)
                    for g in range(QUADS):
                        yield (a, "qkT", g)
                        release(copy(qkT[:, g].rearrange("p a b s -> p (a b s)"), take(a, "qkT", g)[:].bitcast(BF16)),
                                a, "qkT", g)
                    k = 0
                    for kind, i in attention_order():
                        if kind == "mT":
                            yield (a, "mT") + i
                            g, = i
                            release(copy(qmT[:, g % 2].rearrange("p b s -> p (b s)"), take(a, "mT", g)[:, 0:512].bitcast(BF16)),
                                    a, "mT", g)
                        elif kind == "s2":
                            yield (a, "s2") + i
                            if k >= 4:
                                act.wait_ge(pv_done, n * 32 + a * 16 + (k - 4) // 2 + 1)
                            release(copy(prob[:, k % 4].rearrange("p m s -> p (m s)"), take(a, "s2", *i)[:], ACT.Exp),
                                    a, "s2", *i)
                            k += 1
                            if i[1:] == (0, 1) and i[0]:
                                pv_out(a, i[0] - 1)
                        elif kind == "oT" and i[0] == QUADS - 1:
                            yield (a, "oT") + i
                            pv_out(a, QUADS - 1)
                    yield (a, "aT")
                    release(copy(attT[:], take(a, "aT")[:, 0:S]), a, "aT")

                def pv_out(a, g):
                    act.wait_ge(pv_done, n * 32 + a * 16 + 4 * g + 4)
                    copy(oT[:, g % 2, :], pv_bank[g % 2][:]).then_inc(oT_ready, 1)

                def fp4_sizes(k, cols):
                    act.wait_ge(fq_x, n * 2 + 1 + k)
                    copy(s4[:, 0:cols], a4[:, 0:cols], ACT.Sign)
                    act.drain()
                    copy(a4[:, 0:cols], a4[:, 0:cols], ACT.Abs).then_inc(fq_s, 1)

                yield from attention(0)
                yield ("f", "q1", 0)
                fp4_sizes(1, T * D)
                yield ("f", "xqT")
                release(copy(xT[:], take("f", "xqT")[:, 0:S]), "f", "xqT")
                for t in range(T):
                    yield ("f", "gu", t)
                    gate = take("f", "gu", t)[:, 0:INTER]
                    if t >= 2:
                        act.wait_ge(freed[seg.slot(("f", "gu", t - 2))], seg.used(("f", "gu", t - 2), turn))
                    copy(silu[:, t % 2, :], gate, ACT.Silu).then_inc(silu_ready, 1)
                yield ("f", "q2", 0)
                fp4_sizes(2, n4)
                for c, (c0, cw) in enumerate(ICH):
                    yield ("f", "hT", c)
                    release(copy(hqT[0:cw, c, :], take("f", "hT", c)[0:cw, 0:S]), "f", "hT", c)
                act.drain().then_inc(hqT_ready, 1)
                yield from attention(1)

            def back(seg, turn, n):
                def take(*name):
                    act.wait_ge(filled, seg.filled(name, turn))
                    return ring[seg.slot(name)]

                def release(ins_, *name):
                    ins_.then_inc(freed[seg.slot(name)], 1)
                    return ins_

                def shifted(src):
                    copy(xTb[64:128, 0:1], ident[64:128, 0:1])
                    copy(xTb[0:64, :], src[0:64, 0:S])
                    return copy(xTb[64:128, 1:S], src[64:128, 0:S - 1])

                for l in range(LAYERS):
                    L = ("l", l)
                    yield (*L, "xT")
                    release(shifted(take(*L, "xT")), *L, "xT")
                    act.drain().then_inc(xTb_ready, 1)
                    for kind, t in LOCAL_FRONT:
                        if kind == "ro":
                            continue
                        yield (*L, kind, t)
                        if kind == "qk":
                            src = take(*L, "qk", t)[:]
                            if t >= 2:
                                act.wait_ge(lrot_ready, n * 8 + l * 4 + t - 1)
                            copy(lqk[:, t % 2].rearrange("p s h d -> p (s h d)"), src)
                            release(copy(lsq[:, t % 2].rearrange("p s h d -> p (s h d)"), src, ACT.Square), *L, "qk", t)
                            act.drain().then_inc(lraw_ready, 1)
                        elif kind == "v":
                            release(copy(lv[:, 2 * t:2 * t + 2, :, 0:LD].rearrange("p t h d -> p (t h) d"),
                                         take(*L, "v", t)[:].rearrange("p (h d) -> p h d", d=LD)), *L, "v", t)
                            if t == 1:
                                act.drain().then_inc(lv_ready, 1)
                        else:
                            release(copy(lqkT[:, :, t * P:(t + 1) * P], take(*L, "rT", t)[:].rearrange("p (c q) -> p c q", c=8)),
                                    *L, "rT", t)
                    yield (*L, "mT")
                    release(copy(lmT[:].rearrange("p c s -> p (c s)"), take(*L, "mT")[:].bitcast(BF16)), *L, "mT")
                    for t in range(T):
                        w = BAND if t < T - 1 else P
                        for q in range(2):
                            yield (*L, "s2", t, q)
                            sl = take(*L, "s2", t, q)[:].rearrange("p (m w) -> p m w", m=2)[:, :, 0:2 * BAND].rearrange("p m (u w) -> p m u w", u=2)
                            dst = lprob[:, t % 2, 4 * q:4 * q + 4, 0:w].rearrange("p (u m) w -> p m u w", m=2)
                            release(copy(dst, sl[:, :, :, 0:w], ACT.Exp), *L, "s2", t, q)
                    for i in range(2):
                        yield (*L, "oT", i)
                        release(copy(loT[:, :, 2 * i * P:(2 * i + 2) * P].rearrange("p c (t q) -> p t c q", t=2),
                                     take(*L, "oT", i)[:].rearrange("p (t c q) -> p t c q", t=2, c=4)), *L, "oT", i)
                    act.drain().then_inc(loT_ready, 1)
                    yield (*L, "x2T")
                    release(shifted(take(*L, "x2T")), *L, "x2T")
                    act.drain().then_inc(xTb_ready, 1)
                    yield (*L, "hT")
                    release(copy(xTb[:], take(*L, "hT")[:, 0:S], ACT.Identity, scale=ln_g[:, l:l + 1], bias=ln_b[:, l:l + 1]),
                            *L, "hT")
                    for c, (c0, cw) in enumerate(HCH):
                        yield (*L, "w1", c)
                        copy(gel[0:cw, c, :], take(*L, "w1", c)[0:cw, 512:1024], ACT.Gelu, bias=b1[0:cw, l, 1, c:c + 1]).then_inc(gel_ready, 1)

            program(act, front, back)

        @block.vector
        def _(dve):
            V = nc.vector

            def fp4_low(cols):
                a, c, d = a4[:, 0:cols], c4[:, 0:cols], d4[:, 0:cols]
                V.tensor_scalar(c, a, 5.0, 2.0, ALU.is_gt, ALU.mult)
                V.tensor_scalar(d, a, 0.25, None, ALU.is_gt)
                dve.drain()
                V.scalar_tensor_tensor(c, a, 3.5, c, ALU.is_gt, ALU.add)
                V.scalar_tensor_tensor(d, a, 0.75, d, ALU.is_gt, ALU.add)
                dve.drain()
                V.scalar_tensor_tensor(c, a, 2.5, c, ALU.is_gt, ALU.add)
                V.scalar_tensor_tensor(d, a, 1.25, d, ALU.is_gt, ALU.add)
                dve.drain()

            def fp4_high(cols):
                a, c, d = a4[:, 0:cols], c4[:, 0:cols], d4[:, 0:cols]
                V.scalar_tensor_tensor(d, a, 1.75, d, ALU.is_gt, ALU.add)
                dve.drain()
                V.scalar_tensor_tensor(d, c, 2.0, d, ALU.mult, ALU.add)
                dve.drain()

            def fp4_norm(src, cols):
                nb = cols // FB
                V.tensor_reduce(amax[:, 0:nb], src.rearrange("p (b f) -> p b f", f=FB), op=ALU.max, axis=AX,
                                apply_absolute_value=True)
                dve.drain()
                V.tensor_scalar(fscale[:, 0:nb], amax[:, 0:nb], 1.0 / 6.0, 1e-12, ALU.mult, ALU.max)
                dve.drain()
                V.reciprocal(finv[:, 0:nb], fscale[:, 0:nb])
                dve.drain()
                V.tensor_tensor(a4[:, 0:cols].rearrange("p (b f) -> p b f", f=FB),
                                src.rearrange("p (b f) -> p b f", f=FB),
                                finv[:, 0:nb].unsqueeze(2).broadcast_to([P, nb, FB]), ALU.mult).then_inc(fq_x, 1)

            def fp4_value(dst, cols):
                V.scalar_tensor_tensor(dst, d4[:, 0:cols], 0.5, s4[:, 0:cols], ALU.mult, ALU.mult).then_inc(fq_q, 1)

            def moments(side, src):
                for t in range(T):
                    V.bn_stats(stats[side][:, t, :], src[:, t, :])
                dve.drain()
                for t in range(T):
                    V.bn_aggr(mv[side][:, t, :], stats[side][:, t, :])
                dve.drain()
                V.tensor_scalar(mv[side][:, :, 1], mv[side][:, :, 1], EPS, None, ALU.add).then_inc(var_ready[side], 1)

            def normalise(side, dst, src, value):
                dve.wait_ge(rstd_ready[side], value)
                for t in range(T):
                    last = V.tensor_scalar(dst[:, t, :], src[:, t, :], mv[side][:, t, 0:1], rstd[side][:, t:t + 1], ALU.subtract, ALU.mult)
                return last

            V.memset(h4[96:128, 256:384], 0.0)
            V.memset(h4[96:128, 640:768], 0.0)
            dve.wait_ge(w_attn, 16 * N_ATTN)
            for a in range(2):
                V.tensor_scalar(bqkv[:, a, 0:D], bqkv[:, a, 0:D], HD ** -0.5, None, ALU.mult)
            dve.wait_ge(w_rest, 16 * N_REST)
            for l in range(LAYERS):
                for side in range(2):
                    for tab, o in ((rot_c, 0), (rot_s, 4 * LD)):
                        o += (2 * l + side) * LD
                        V.tensor_tensor(tab[:, l, :, side, :], tab[:, l, :, side, :],
                                        c4[:, o:o + LD].unsqueeze(1).broadcast_to([P, T, LD]), ALU.mult)
            dve.drain().then_inc(prep_v, 1)
            fp4_norm(h4[:, 0:NW], NW)
            dve.wait_ge(fq_s, 1)
            fp4_low(NW)
            fp4_high(NW)
            dve.wait_ge(fq_g, 1)
            fp4_value(h4[:, 0:NW], NW)
            dve.wait_ge(filled, 1)
            dve.sem_inc(out_done, 16)

            def front(seg, turn, n):
                def take(*name):
                    dve.wait_ge(filled, seg.filled(name, turn))
                    return ring[seg.slot(name)]

                def release(ins_, *name):
                    ins_.then_inc(freed[seg.slot(name)], 1)
                    return ins_

                def close_block(name, was, bias, dst, k):
                    yield name
                    o = take(*name)[:, 0:S].rearrange("p (t d) -> p t d", t=T)
                    release(V.tensor_tensor(y[:], o, was[:], ALU.add), *name)
                    dve.drain()
                    if bias is not None:
                        V.tensor_tensor(y[:], y[:], bias.unsqueeze(1).broadcast_to([P, T, D]), ALU.add)
                        dve.drain()
                    moments(0, y)
                    yield (name[0], "norm")
                    normalise(0, dst, y, n * 3 + k)
                    dve.drain().then_inc(x_ready, 1)

                def attention(a):
                    for i in range(2):
                        yield (a, "qkv", i)
                        o = take(a, "qkv", i)
                        if a == 0 and i == 0:
                            dve.wait_ge(prep_g, 1)
                        for b in range(2):
                            t = 2 * i + b
                            src = o[:, 512 * b:512 * b + 3 * D]
                            V.scalar_tensor_tensor(qk[:, t, 0, :], src[:, 0:D], HD ** -0.5, bqkv[:, a, 0:D], ALU.mult, ALU.add)
                            V.tensor_tensor(qk[:, t, 1, :], src[:, D:2 * D], bqkv[:, a, D:2 * D], ALU.add)
                            last = V.tensor_tensor(v_aug[:, t, :, 0:HD], src[:, 2 * D:3 * D].rearrange("p (h d) -> p h d", d=HD),
                                                   bqkv[:, a, 2 * D:3 * D].rearrange("p (h d) -> p h d", d=HD), ALU.add)
                        release(last, a, "qkv", i)
                    dve.drain().then_inc(qkv_ready, 1)
                    for kind, i in attention_order():
                        if kind == "s1":
                            yield (a, "s1") + i
                            g, t, pr = i
                            release(V.tensor_reduce(neg_max[:, g, t, 2 * pr:2 * pr + 2],
                                                    take(a, "s1", *i)[:].rearrange("p (m s) -> p m s", m=2),
                                                    op=ALU.max, axis=AX, negate=True), a, "s1", *i)
                        elif kind == "oT":
                            yield (a, "oT") + i
                            g, = i
                            o4 = take(a, "oT", g)[:, 0:S].rearrange("p (n c) -> p n c", c=32)
                            V.reciprocal(rsum[:], o4[:, :, HD])
                            dve.drain()
                            release(V.tensor_tensor(att[:, :, 32 * g:32 * g + 32].rearrange("p t (j d) -> p t j d", j=4),
                                                    o4[:, :, 0:HD].rearrange("p (t j) d -> p t j d", t=T),
                                                    rsum[:].rearrange("p (t j) -> p t j", t=T).unsqueeze(3).broadcast_to([P, T, 4, HD]),
                                                    ALU.mult), a, "oT", g)
                    yield from close_block((a, "proj"), (x_next, x)[a], bo[:, a, :], (x, xb)[a], 1 + 2 * a)

                yield from attention(0)
                xf = x[:].rearrange("p t d -> p (t d)")
                yield ("f", "q1", 0)
                fp4_norm(xf, T * D)
                yield ("f", "q1", 1)
                dve.wait_ge(fq_s, n * 2 + 2)
                fp4_low(T * D)
                yield ("f", "q1", 2)
                fp4_high(T * D)
                dve.wait_ge(fq_g, n * 2 + 2)
                fp4_value(h4[:, 0:T * D], T * D)
                for t in range(T):
                    yield ("f", "gu", t)
                    o = take("f", "gu", t)
                    dve.wait_ge(silu_ready, n * T + t + 1)
                    release(V.tensor_tensor(h4[:, t * INTER:(t + 1) * INTER], silu[:, t % 2, :], o[:, 512:512 + INTER], ALU.mult),
                            "f", "gu", t)
                yield ("f", "q2", 0)
                dve.drain()
                fp4_norm(h4, n4)
                yield ("f", "q2", 1)
                dve.wait_ge(fq_s, n * 2 + 3)
                fp4_low(n4)
                yield ("f", "q2", 2)
                fp4_high(n4)
                dve.wait_ge(fq_g, n * 2 + 3)
                fp4_value(h4, n4)
                yield from close_block(("f", "down"), x, None, x, 2)
                yield from attention(1)

            def back(seg, turn, n):
                def take(*name):
                    dve.wait_ge(filled, seg.filled(name, turn))
                    return ring[seg.slot(name)]

                def release(ins_, *name):
                    ins_.then_inc(freed[seg.slot(name)], 1)
                    return ins_

                for l in range(LAYERS):
                    L = ("l", l)
                    for kind, t in LOCAL_FRONT:
                        if kind == "qk":
                            yield (*L, "qk", t)
                            dve.wait_ge(lraw_ready, n * 8 + l * 4 + t + 1)
                            V.tensor_reduce(lss[:, t, :], lsq[:, t % 2].rearrange("p s h d -> p (s h) d"), op=ALU.add, axis=AX)
                            for side in range(2):
                                V.tensor_tensor(lrs[:, t % 2, side], lqk[:, t % 2, side],
                                                rot_c[:, l, t, side, :].unsqueeze(1).broadcast_to([P, LH, LD]), ALU.mult)
                            dve.drain()
                            V.tensor_scalar(lss[:, t, :], lss[:, t, :], 1e-24, None, ALU.max).then_inc(lss_ready, 1)
                        elif kind == "ro":
                            yield (*L, "ro", t)
                            flat = lambda v: v[:, t % 2].rearrange("p s h d -> p (s h d)")
                            heads = lrs[:, t % 2].rearrange("p s h d -> p (s h) d")
                            dve.wait_ge(lsin_ready, n * 8 + l * 4 + t + 1)
                            V.tensor_tensor(flat(lrs), flat(lrs), flat(lsq), ALU.add)
                            dve.drain()
                            dve.wait_ge(lrn_ready, n * 8 + l * 4 + t + 1)
                            V.tensor_tensor(heads, heads, lrn[:, t, :].unsqueeze(2).broadcast_to([P, 16, LD]), ALU.mult).then_inc(lrot_ready, 1)
                    for t in range(T):
                        lo_, w = (0, BAND) if t else (WIN, P)
                        for q in range(2):
                            yield (*L, "s1", t, q)
                            sl = take(*L, "s1", t, q)[:].rearrange("p (m w) -> p m w", m=2)[:, :, 0:2 * BAND].rearrange("p m (u w) -> p m u w", u=2)
                            release(V.tensor_reduce(lneg[:, t, 4 * q:4 * q + 4].rearrange("p (u m) -> p m u", m=2),
                                                    sl[:, :, :, lo_:BAND], op=ALU.max, axis=AX, negate=True), *L, "s1", t, q)
                    for t in range(T):
                        yield (*L, "pv", t)
                        o3 = take(*L, "pv", t)[:].rearrange("p (b c) -> p b c", b=2)[:, :, 0:4 * (LD + 1)].rearrange("p b (h c) -> p b h c", c=LD + 1)
                        V.reciprocal(lrsum[:, t, :].rearrange("p (b h) -> p b h", b=2), o3[:, :, :, LD])
                        dve.drain()
                        release(V.tensor_tensor(lo[:, t, :].rearrange("p (b h d) -> p b h d", b=2, h=4), o3[:, :, :, 0:LD],
                                                lrsum[:, t, :].rearrange("p (b h) -> p b h", b=2).unsqueeze(3).broadcast_to([P, 2, 4, LD]),
                                                ALU.mult), *L, "pv", t)
                    dve.drain().then_inc(lo_ready, 1)
                    yield (*L, "wo")
                    release(V.tensor_tensor(yb[:], take(*L, "wo")[:, 0:S].rearrange("p (t d) -> p t d", t=T), (xb, yb)[l][:], ALU.add),
                            *L, "wo")
                    yield (*L, "hB")
                    release(V.tensor_copy(hn, take(*L, "hB")[:, 0:S].rearrange("p (t d) -> p t d", t=T)), *L, "hB")
                    dve.drain()
                    moments(1, hn)
                    V.tensor_tensor(yb[:], yb[:], b2[:, l, :].unsqueeze(1).broadcast_to([P, T, D]), ALU.add)
                    yield (*L, "norm")
                    normalise(1, hn, hn, n * 3 + 1 + l)
                    dve.drain().then_inc(h_back, 1)
                    for c, (c0, cw) in enumerate(HCH):
                        yield (*L, "w1", c)
                        o = take(*L, "w1", c)
                        dve.wait_ge(gel_ready, n * 6 + l * 3 + c + 1)
                        release(V.scalar_tensor_tensor(hid[0:cw, c, :], o[0:cw, 0:S], b1[0:cw, l, 0, c:c + 1],
                                                       gel[0:cw, c, :], ALU.add, ALU.mult), *L, "w1", c)
                    dve.drain().then_inc(hid_ready, 1)
                    yield (*L, "w2")
                    release(V.tensor_tensor(yb[:], take(*L, "w2")[:, 0:S].rearrange("p (t d) -> p t d", t=T), yb[:], ALU.add),
                            *L, "w2")
                yield ("end", 0)
                dve.drain()
                V.tensor_tensor(yb[:], yb[:], xb[:], ALU.add)
                dve.drain()
                moments(1, yb)
                yield ("end", 1)
                dve.wait_ge(out_done, 16 * n + 16)
                normalise(1, res, yb, n * 3 + 3)
                dve.drain().then_inc(out_ready, 1)

            program(dve, front, back)

        @block.tensor
        def _(pe):
            mm = nc.tensor.matmul

            def transpose(dst, src, idt=None):
                k = src.shape[0]
                idt = ident if idt is None else idt
                return nc.tensor.transpose(dst, src, idt[0:k, 0:k])

            def fill(last):
                last.then_inc(filled, 1)

            pe.wait_ge(w_attn, 16 * N_ATTN)
            for c in range(3):
                transpose(ring[0][:, c * P:(c + 1) * P], y[:, c, :])
                transpose(ring[0][:, (3 + c) * P:(4 + c) * P], yb[:, c, :])
            transpose(ring[0][:, 6 * P:7 * P], y[:, 3, :])
            fill(transpose(ring[0][:, 7 * P:8 * P], yb[:, 3, :]))
            pe.wait_ge(fq_q, 1)
            for s in range(2):
                for c, (c0, cw) in enumerate(ICH):
                    last = transpose(ring[1][:, 512 * s + c0:512 * s + c0 + cw], h4[0:cw, (3 * s + c) * D:(3 * s + c + 1) * D])
            fill(last)
            for c, (c0, cw) in enumerate(ICH):
                last = transpose(ring[2][0:cw, c * P:(c + 1) * P], h4[:, 768 + c0:768 + c0 + cw])
            fill(last)
            pe.wait_ge(prep_a, 1)
            pe.wait_ge(prep_v, 1)
            pe.wait_ge(prep_g, 1)

            def front(seg, turn, n):
                def claim(*name, after=()):
                    for slot, count in seg.needs(turn, after, name):
                        pe.wait_ge(freed[slot], count)
                    return ring[seg.slot(name)]

                def extra(o, m, h, q, k, swap):
                    j, b = (h // 2) % 4, h // 8
                    rows = slice(32 * j, 32 * j + 32)
                    one, two = (alibi_xk[rows, b, k], alibi_xq[rows, b, q])
                    mm(o[:, m * S:(m + 1) * S], one, two, start=False, stop=False)

                def diagonal(o, m, h, t, parts):
                    for k in range(parts):
                        block_ = 4 * (h // 2) + (h % 2) * (1 + k)
                        last = mm(o[:, m * S + t * P:m * S + (t + 1) * P], identb[:], alibi_d[:, block_, :], start=False, stop=k == parts - 1)
                    return last

                def scores1(a, g, t, pr):
                    o = claim(a, "s1", g, t, pr, after=[(a, "qkT", g)] if t == pr == 0 else [])
                    for m in range(2):
                        rows = slice(64 * m, 64 * m + ROWS[a])
                        last = mm(o[:, m * S:(m + 1) * S], qkT[rows, g, pr, 0, t * P:(t + 1) * P],
                                  qkT[rows, g, pr, 1, :], start=True, stop=a == 1)
                    if a == 0:
                        for m in range(2):
                            last = diagonal(o, m, 4 * g + 2 * pr + m, t, 1)
                    fill(last)

                def scores2(a, g, t, pr):
                    o = claim(a, "s2", g, t, pr, after=[(a, "mT", g)] if t == pr == 0 else [])
                    for m in range(2):
                        rows = slice(64 * m, 64 * m + ROWS[a])
                        last = mm(o[:, m * S:(m + 1) * S], qkT[rows, g, pr, 1, t * P:(t + 1) * P], qmT[rows, g % 2, pr, :], start=True, stop=a == 1)
                    if a == 0:
                        h = 4 * g + 2 * pr
                        extra(o, 1, h + 1, slice(0, S), slice(t * P, (t + 1) * P), False)
                        diagonal(o, 0, h, t, 1)
                        last = diagonal(o, 1, h + 1, t, 3)
                    fill(last)

                def weighted(a, g, t):
                    k = 8 * g + 2 * t
                    for slot, count in seg.needs(turn, [(a, "s2", g, t, pr) for pr in range(2)]):
                        pe.wait_ge(freed[slot], count)
                    for j in range(4):
                        last = mm(pv_bank[g % 2][32 * j:32 * j + 32, :], v_aug[:, t, 4 * g + j, :], prob[:, (k + j // 2) % 4, j % 2, :],
                                  start=t == 0, stop=t == T - 1)
                    last.then_inc(pv_done, 1)

                def attention(a):
                    yield (a, "xT")
                    o = claim(a, "xT")
                    src = (x_next, x)[a]
                    if a == 0:
                        pe.wait_ge(x_in, n * 16 + 16)
                    else:
                        pe.wait_ge(x_ready, n * 3 + 2)
                    for t in range(T):
                        last = transpose(o[:, t * P:(t + 1) * P], src[:, t, :])
                    fill(last)
                    for i in range(2):
                        yield (a, "qkv", i)
                        o = claim(a, "qkv", i, after=[(a, "xT")])
                        for b in range(2):
                            t = 2 * i + b
                            last = mm(o[:, 512 * b:512 * b + 3 * D], xT[:, t * P:(t + 1) * P], wqkvT[:, a, :], start=True, stop=True)
                        fill(last)
                    for g in range(QUADS):
                        yield (a, "qkT", g)
                        if g == 0:
                            pe.wait_ge(aug_a, n * 2 + a + 1)
                            pe.wait_ge(aug_g, n * 2 + a + 1)
                        o = claim(a, "qkT", g)[:].bitcast(BF16)
                        for pr in range(2):
                            for side in range(2):
                                for t in range(T):
                                    c = (2 * pr + side) * S + t * P
                                    h0 = 4 * g + 2 * pr
                                    last = transpose(o[:, c:c + P], aug[:, side, t, h0:h0 + 2, :].rearrange("p h s -> p (h s)"), identb)
                        fill(last)
                    late = None
                    for kind, i in attention_order():
                        yield (a, kind) + i
                        if kind == "s1":
                            scores1(a, *i)
                        elif kind == "mT":
                            g, = i
                            o = claim(a, "mT", g)[:, 0:512].bitcast(BF16)
                            pe.wait_ge(maxq_ready, n * 8 + a * 4 + g + 1)
                            for pr in range(2):
                                for t in range(T):
                                    c, h0 = pr * S + t * P, 4 * g + 2 * pr
                                    last = transpose(o[:, c:c + P], aug[:, 0, t, h0:h0 + 2, :].rearrange("p h s -> p (h s)"), identb)
                            fill(last)
                        elif kind == "s2":
                            g, t, pr = i
                            scores2(a, *i)
                            if pr == 0 and late is not None:
                                weighted(a, *late)
                                late = None
                            if pr == 1:
                                late = (g, t)
                        elif kind == "oT":
                            g, = i
                            if g == QUADS - 1:
                                weighted(a, *late)
                            o = claim(a, "oT", g)
                            pe.wait_ge(oT_ready, n * 8 + a * 4 + g + 1)
                            for t in range(T):
                                last = transpose(o[:, t * P:(t + 1) * P], oT[:, g % 2, t * P:(t + 1) * P])
                            fill(last)
                    yield (a, "aT")
                    o = claim(a, "aT", after=[(a, "oT", g) for g in range(QUADS)])
                    for t in range(T):
                        last = transpose(o[:, t * P:(t + 1) * P], att[:, t, :])
                    fill(last)
                    yield (a, "proj")
                    o = claim(a, "proj", after=[(a, "aT")])
                    for t in range(T):
                        last = mm(o[:, t * D:(t + 1) * D], attT[:, t * P:(t + 1) * P], woT[:, a, :], start=True, stop=True)
                    fill(last)

                yield from attention(0)
                yield ("f", "xqT")
                o = claim("f", "xqT")
                pe.wait_ge(fq_q, n * 2 + 2)
                for t in range(T):
                    last = transpose(o[:, t * P:(t + 1) * P], h4[:, t * D:(t + 1) * D])
                fill(last)
                for t in range(T):
                    yield ("f", "gu", t)
                    o = claim("f", "gu", t, after=[("f", "xqT")])
                    for s in range(2):
                        last = mm(o[:, 512 * s:512 * s + INTER], xT[:, t * P:(t + 1) * P], wguT[:, s, :], start=True, stop=True)
                    fill(last)
                for c, (c0, cw) in enumerate(ICH):
                    yield ("f", "hT", c)
                    o = claim("f", "hT", c)
                    pe.wait_ge(fq_q, n * 2 + 3)
                    for t in range(T):
                        last = transpose(o[0:cw, t * P:(t + 1) * P], h4[:, t * INTER + c0:t * INTER + c0 + cw])
                    fill(last)
                yield ("f", "down")
                o = claim("f", "down")
                pe.wait_ge(hqT_ready, n + 1)
                for t in range(T):
                    for c, (c0, cw) in enumerate(ICH):
                        last = mm(o[:, t * D:(t + 1) * D], hqT[0:cw, c, t * P:(t + 1) * P], wdT[0:cw, c, :], start=c == 0, stop=c == 2)
                fill(last)
                yield from attention(1)

            def back(seg, turn, n):
                def claim(*name, after=()):
                    for slot, count in seg.needs(turn, after, name):
                        pe.wait_ge(freed[slot], count)
                    return ring[seg.slot(name)]

                for l in range(LAYERS):
                    L = ("l", l)
                    yield (*L, "xT")
                    o = claim(*L, "xT", after=[("l", 0, "w2")] if l else [])
                    if l == 0:
                        pe.wait_ge(x_ready, n * 3 + 3)
                    for t in range(T):
                        last = transpose(o[:, t * P:(t + 1) * P], (xb, yb)[l][:, t, :])
                    fill(last)
                    for kind, t in LOCAL_FRONT:
                        if kind == "ro":
                            continue
                        yield (*L, kind, t)
                        o = claim(*L, kind, t)
                        pe.wait_ge(xTb_ready, n * 4 + 2 * l + 1)
                        if kind == "qk":
                            for s in range(2):
                                last = mm(o[:, 512 * s:512 * s + 512], xTb[:, t * P:(t + 1) * P], wl_qkv[:, l, 512 * s:512 * s + 512], start=True, stop=True)
                        elif kind == "v":
                            for b in range(2):
                                last = mm(o[:, 512 * b:512 * b + 512], xTb[:, (2 * t + b) * P:(2 * t + b + 1) * P], wl_qkv[:, l, 1024:1536], start=True, stop=True)
                        else:
                            pe.wait_ge(lrot_ready, n * 8 + l * 4 + t + 1)
                            for c in range(8):
                                last = transpose(o[:, c * P:(c + 1) * P], lrs[:, t % 2, c // 4, 2 * (c % 4):2 * (c % 4) + 2, :].rearrange("p h d -> p (h d)"))
                        fill(last)
                    for t in range(T):
                        k0 = t * P - WIN if t else 0
                        c0 = 0 if t else WIN
                        for q in range(2):
                            yield (*L, "s1", t, q)
                            o = claim(*L, "s1", t, q, after=[(*L, "rT", i) for i in range(t + 1)])
                            for u in range(2):
                                part = lambda m: o[:, 512 * m + BAND * u + c0:512 * m + BAND * (u + 1)]
                                for m in range(2):
                                    rows, pr = slice(64 * m, 64 * m + 64), 2 * q + u
                                    mm(part(m), lqkT[rows, pr, t * P:(t + 1) * P], lqkT[rows, 4 + pr, k0:(t + 1) * P], start=True, stop=False)
                                for m in range(2):
                                    last = mm(part(m), identb[:], band_q[:, c0:BAND], start=False, stop=True)
                            fill(last)
                    yield (*L, "mT")
                    o = claim(*L, "mT")[:].bitcast(BF16)
                    pe.wait_ge(lm_ready, n * 2 + l + 1)
                    for c in range(4):
                        for t in range(T):
                            last = transpose(o[:, c * S + t * P:c * S + (t + 1) * P], lm[:, t, 2 * c:2 * c + 2, :].rearrange("p h s -> p (h s)"), identb)
                    fill(last)

                    def sums(t):
                        o = claim(*L, "pv", t, after=[(*L, "s2", t, q) for q in range(2)])
                        pe.wait_ge(lv_ready, n * 2 + l + 1)
                        for h in range(LH):
                            dst = o[:, 512 * (h // 4) + (LD + 1) * (h % 4):512 * (h // 4) + (LD + 1) * (h % 4 + 1)]
                            last = mm(dst, lprob[:, t % 2, h, 0:P], lv[:, t, h, :], start=True, stop=t == 0)
                            if t:
                                last = mm(dst, lprob[WIN:P, (t - 1) % 2, h, P:2 * P], lv[WIN:P, t - 1, h, :], start=False, stop=True)
                        fill(last)

                    for t in range(T):
                        w = BAND if t < T - 1 else P
                        for q in range(2):
                            yield (*L, "s2", t, q)
                            o = claim(*L, "s2", t, q, after=[(*L, "mT")])
                            for u in range(2):
                                part = lambda m: o[:, 512 * m + BAND * u:512 * m + BAND * u + w]
                                for m in range(2):
                                    rows, pr = slice(64 * m, 64 * m + 64), 2 * q + u
                                    mm(part(m), lqkT[rows, 4 + pr, t * P:(t + 1) * P], lqkT[rows, pr, t * P:t * P + w], start=True, stop=False)
                                for m in range(2):
                                    rows, pr = slice(64 * m, 64 * m + 64), 2 * q + u
                                    mm(part(m), ones_m[rows, :], lmT[rows, pr, t * P:t * P + w], start=False, stop=False)
                                for m in range(2):
                                    last = mm(part(m), identb[:], band_k[:, 0:w], start=False, stop=True)
                            fill(last)
                        yield (*L, "pv", t)
                        sums(t)
                    for i in range(2):
                        yield (*L, "oT", i)
                        o = claim(*L, "oT", i)
                        pe.wait_ge(lo_ready, n * 2 + l + 1)
                        for b in range(2):
                            for c in range(4):
                                last = transpose(o[:, (4 * b + c) * P:(4 * b + c + 1) * P], lo[:, 2 * i + b, c * P:(c + 1) * P])
                        fill(last)
                    yield (*L, "wo")
                    o = claim(*L, "wo")
                    pe.wait_ge(loT_ready, n * 2 + l + 1)
                    for t in range(T):
                        for c in range(4):
                            last = mm(o[:, t * D:(t + 1) * D], loT[:, c, t * P:(t + 1) * P], wl_o[:, l, c, :], start=c == 0, stop=c == 3)
                    fill(last)
                    yield (*L, "x2T")
                    o = claim(*L, "x2T", after=[(*L, "wo")])
                    for t in range(T):
                        last = transpose(o[:, t * P:(t + 1) * P], yb[:, t, :])
                    fill(last)
                    yield (*L, "hB")
                    o = claim(*L, "hB")
                    pe.wait_ge(xTb_ready, n * 4 + 2 + 2 * l)
                    for t in range(T):
                        last = transpose(o[:, t * P:(t + 1) * P], xTb[:, t * P:(t + 1) * P])
                    fill(last)
                    yield (*L, "hT")
                    o = claim(*L, "hT")
                    pe.wait_ge(h_back, n * 2 + l + 1)
                    for t in range(T):
                        last = transpose(o[:, t * P:(t + 1) * P], hn[:, t, :])
                    fill(last)
                    for c, (c0, cw) in enumerate(HCH):
                        yield (*L, "w1", c)
                        o = claim(*L, "w1", c, after=[(*L, "hT")])
                        for s in range(2):
                            last = mm(o[0:cw, 512 * s:512 * s + 512], w1[:, l, s * HID + c0:s * HID + c0 + cw], xTb[:], start=True, stop=True)
                        fill(last)
                    yield (*L, "w2")
                    o = claim(*L, "w2")
                    pe.wait_ge(hid_ready, n * 2 + l + 1)
                    for t in range(T):
                        for c, (c0, cw) in enumerate(HCH):
                            last = mm(o[:, t * D:(t + 1) * D], hid[0:cw, c, t * P:(t + 1) * P], w2[0:cw, l, c, :], start=c == 0, stop=c == 2)
                    fill(last)

            program(pe, front, back)


def constants():
    import numpy as np
    bf = mybir.dt.np(BF16)
    f32 = np.float32

    def parts(v):
        v = np.asarray(v, f32)
        out = []
        for _ in range(3):
            p = v.astype(bf)
            out.append(p)
            v = v - p.astype(f32)
        return out

    slopes = (2.0 ** (8.0 * np.arange(0, -H, -1, dtype=f32) / H)).astype(f32)
    pos = np.arange(S)
    tile, centred = pos // P, (pos - S // 2).astype(f32)
    alibi_b = np.zeros((P, 2, T, H, 2 * T), f32)
    alibi_xq, alibi_xk = np.zeros((P, 2, S), f32), np.zeros((P, 2, S), f32)
    alibi_d = np.zeros((P, 4 * PAIRS, P), bf)
    within = np.arange(P)
    dist = np.abs(within[:, None] - within[None, :]).astype(f32)
    rows = lambda v: v.reshape(T, P).T
    for h in range(H):
        for i, s in enumerate(parts(slopes[h])):
            s = float(s)
            for c in range(T):
                sign = np.sign(tile - c).astype(f32)
                here = (tile == c).astype(f32)
                if i == 0:
                    alibi_b[:, 0, :, h, 2 * c], alibi_b[:, 1, :, h, 2 * c] = rows(sign * centred), rows(-s * here)
                    alibi_b[:, 0, :, h, 2 * c + 1], alibi_b[:, 1, :, h, 2 * c + 1] = rows(sign * s), rows(centred * here)
                elif h % 2:
                    row, b = 32 * ((h // 2) % 4) + 4 * c + 2 * (i - 1), h // 8
                    alibi_xq[row, b], alibi_xk[row, b] = sign * centred, -s * here
                    alibi_xq[row + 1, b], alibi_xk[row + 1, b] = sign * s, centred * here
        for i, p in enumerate(parts(-slopes[h] * dist)):
            if h % 2:
                alibi_d[:, 4 * (h // 2) + 1 + i, :] = p
            elif i == 0:
                alibi_d[:, 4 * (h // 2), :] = p
    band = np.arange(BAND)
    gap_q = within[:, None] - (band[None, :] - WIN)
    gap_k = band[None, :] - within[:, None]
    mask = lambda gap: np.where((gap >= 0) & (gap <= WIN), 0.0, -1e30).astype(bf)
    ones_m = np.zeros((P, P), bf)
    for m in range(2):
        ones_m[SLOTS * m:SLOTS * m + 3] = 1
    half = np.arange(0, LD, 2, dtype=f32)
    inv = (1.0 / 10000.0 ** (half / LD)).astype(f32)
    t = np.arange(S, dtype=f32)
    freqs = np.tile(t[:, None] * inv[None, :], (1, 2))
    base = ((half + 0.4 * LD) / (1.4 * LD)).astype(f32)
    scale = np.tile(base[None, :] ** ((t - S // 2) / f32(WIN // 2))[:, None], (1, 2)).astype(f32)
    sign = np.where(np.arange(LD) < LD // 2, -1.0, 1.0).astype(f32)
    lay = lambda q, k: np.ascontiguousarray(np.stack([q, k], 1).reshape(T, P, 2, LD).transpose(1, 0, 2, 3).astype(f32))
    cos, sin = np.cos(freqs).astype(f32), np.sin(freqs).astype(f32)
    return {
        "ident": np.eye(P, dtype=f32), "identb": np.eye(P).astype(bf),
        "alibi_b": alibi_b.reshape(P, -1).astype(bf), "alibi_d": alibi_d,
        "alibi_xq": alibi_xq.astype(bf), "alibi_xk": alibi_xk.astype(bf),
        "band_q": mask(gap_q), "band_k": mask(gap_k), "ones_m": ones_m,
        "rot_c": lay(cos * scale * 8, cos / scale), "rot_s": lay(sign * sin * scale * 8, sign * sin / scale),
    }


NAMES = {
    "x": "L0_attn_x", "wqkv0": "L0_attn_W_qkv", "bqkv0": "L0_attn_b_qkv", "wo0": "L0_attn_W_out", "bo0": "L0_attn_b_out",
    "wgate": "L0_ffn_w_gate", "wup": "L0_ffn_w_up", "wdown": "L0_ffn_w_down",
    "wqkv1": "L1_attn_W_qkv", "bqkv1": "L1_attn_b_qkv", "wo1": "L1_attn_W_proj", "bo1": "L1_attn_b_proj",
    "wl_qkv": "L1_ffn_wqkv", "q_scale": "L1_ffn_q_scale", "k_scale": "L1_ffn_k_scale", "wl_o": "L1_ffn_wo",
    "ln_g": "L1_ffn_ln_g", "ln_b": "L1_ffn_ln_b", "w1": "L1_ffn_w1", "b1": "L1_ffn_b1", "w2": "L1_ffn_w2", "b2": "L1_ffn_b2",
}


def kernel(**inputs):
    import concourse.bacc as bacc
    import numpy as np
    from concourse.bass_utils import run_bass_kernel_spmd

    nc = bacc.Bacc("TRN2", target_bir_lowering=False, num_devices=1)
    arrays = {k: np.ascontiguousarray(inputs[v]) for k, v in NAMES.items()} | constants()
    ins = {k: nc.dram_tensor(f"in_{k}", a.shape, mybir.dt.from_np(a.dtype), kind="ExternalInput").ap() for k, a in arrays.items()}
    out = nc.dram_tensor("out", (SEQS, S, D), F32, kind="ExternalOutput").ap()
    build(nc, ins, out)
    r = run_bass_kernel_spmd(nc, [{f"in_{k}": a for k, a in arrays.items()}], core_ids=[0])
    return r.results[0]["out"]
```

```python
from contextlib import ExitStack

import concourse.bass as bass
from concourse import mybir

F32 = mybir.dt.float32
BF16 = mybir.dt.bfloat16
ALU = mybir.AluOpType
ACT = mybir.ActivationFunctionType
AX = mybir.AxisListType.X

P = 128
SEQS, S, D = 8, 512, 128
T = S // P
H, HD = 16, 8
PAIRS, QUADS = H // 2, H // 4
SLOTS = 64
INTER = 352
ICH = [(0, 128), (128, 128), (256, 96)]
FB = 16
LAYERS, LH, LD = 2, 8, 64
WIN = 64
BAND = P + WIN
HID = 341
HCH = [(0, 128), (128, 128), (256, 85)]
EPS = 1e-5
Q_PART = [0, 0, 1, 1, 0, 2]
K_PART = [0, 1, 0, 1, 2, 0]
M_SLOT = 8 * len(Q_PART)
B_SLOT = M_SLOT + 3
ROWS = [B_SLOT + 2 * T, B_SLOT]

RUNS = [3, 1, 3, 2, 5, 1, 8, 1, 3, 1, 3, 1, 2, 1, 1, 1, 4, 1, 4, 1, 3, 1, 1, 1, 2, 2, 9, 3, 4, 1, 2, 3, 10, 1, 5, 1,
        5, 1, 4, 1, 3, 3, 2, 3, 2, 1, 5, 1, 2, 2, 1, 4, 3, 3, 2, 1, 1, 1, 2, 2, 4, 1, 2, 2, 2, 1, 10, 1, 4, 1,
        2, 1, 6, 1, 4, 2, 3, 1, 1, 1, 1, 2, 3, 3, 4, 1, 1, 3, 4, 1, 4, 1, 2, 3, 4, 1, 2, 1, 3, 2, 3, 1, 3, 1,
        2, 1, 1, 1, 2, 2, 3, 1, 1, 1, 1, 2, 2, 1, 1, 2]

LOCAL_FRONT = [("qk", 0), ("qk", 1), ("ro", 0), ("rT", 0), ("qk", 2), ("ro", 1), ("rT", 1), ("qk", 3), ("ro", 2), ("rT", 2),
               ("v", 0), ("ro", 3), ("rT", 3), ("v", 1)]


def front_steps():
    steps = []
    for a in range(2):
        steps += [((a, "xT"), 2, True)] + [((a, "qkv", i), 3, True) for i in range(2)]
        steps += [((a, "aug", i), 4, False) for i in range(3)]
        steps += [((a, "qkT", g), 2, True) for g in range(QUADS)]
        steps += [((a, kind) + i, 1.2, True) for kind, i in attention_order()]
        steps += [((a, "aT"), 2, True), ((a, "proj"), 4, True), ((a, "norm"), 2, False)]
        if a == 0:
            steps += [(("f", "q1", i), 2, False) for i in range(3)] + [(("f", "xqT"), 2, True)]
            steps += [(("f", "gu", t), 0 if t else 8, True) for t in range(T)]
            steps += [(("f", "q2", i, half), 2.5, False) for i in range(3) for half in range(2)]
            steps += [(("f", "hT", c), 2, True) for c in range(3)] + [(("f", "down"), 4, True), (("f", "norm"), 2, False)]
    return steps


def weight_steps():
    return [(("w", "rot"), 0, False), (("w", "q", 0), 0, False), (("w", "q", 1), 0, False), (("w", "q", 2), 0, False),
            (("w", "guT"), 0, True), (("w", "dT"), 0, True)]


def local_order():
    out = [("s", 0, 0), ("s", 0, 1)]
    for t in range(T):
        ahead = [("s", t + 1, q) for q in range(2)] if t + 1 < T else []
        out += ahead[:1] + [("own", t)] + ahead[1:]
        out += [("prev", t)] if t else []
        out += [("pv", t)]
    return out


def head_steps(l):
    return [(("l", l, "xT"), 2, True)] + [(("l", l) + i, 3.5, i[0] != "ro") for i in LOCAL_FRONT]


def tail_steps(l):
    steps = [(("l", l) + i, 1.5, True) for i in local_order()]
    steps += [(("l", l, "wo", i), 3, True) for i in range(2)]
    steps += [(("l", l, "x2T"), 2, True), (("l", l, "hB"), 3, True), (("l", l, "norm"), 2, False), (("l", l, "hT"), 3, True)]
    return steps + [(("l", l, "w1", c), 0 if c else 6, True) for c in range(3)] + [(("l", l, "w2"), 3, True)]


def back_steps():
    return head_steps(0) + tail_steps(0) + head_steps(1) + tail_steps(1) + [(("end", i), 2, False) for i in range(2)]


def interleaved(first, second, runs):
    streams, order = [iter(first), iter(second)], []
    for i, n in enumerate(runs):
        order += [next(streams[i % 2]) for _ in range(n)]
    assert len(order) == len(first) + len(second)
    return [(step, fills) for step, _, fills in order]


class Segment:

    def __init__(self, order, before):
        self.order = [step for step, _ in order]
        items = [step for step, fills in order if fills]
        assert len(set(items)) == len(items)
        self.index = {name: before + i for i, name in enumerate(items)}
        self.n = len(items)

    def slot(self, name):
        return self.index[name] % 3

    def filled(self, name, turn):
        return turn * self.n + self.index[name] + 1

    def needs(self, turn, names, claim=None):
        need = {} if claim is None else {self.slot(claim): self.index[claim] // 3}
        for name in names:
            need[self.slot(name)] = max(need.get(self.slot(name), 0), self.index[name] // 3 + 1)
        return [(slot, turn * (self.n // 3) + count) for slot, count in need.items()]


def run_steps(segment, *streams):
    pending = [[g, next(g, None)] for g in streams]
    for step in segment.order:
        for p in pending:
            if p[1] == step:
                p[1] = next(p[0], None)
    assert all(p[1] is None for p in pending), [p[1] for p in pending]


def attention_order():
    units = [(i, pr) for i in range(T) for pr in range(2)]
    out = [("s1", (0,) + u) for u in units]
    for g in range(QUADS):
        ahead = [("s1", (g + 1,) + u) for u in units] if g + 1 < QUADS else []
        out += ahead[:3] + [("mT", (g,))]
        rest = ahead[3:]
        for n, u in enumerate(units):
            out += [("s2", (g,) + u)] + rest[:1]
            rest = rest[1:]
            if n == 2 and g:
                out += [("oT", (g - 1,))]
    out += [("oT", (QUADS - 1,))]
    return out


def build(nc, ins, out, seqs=SEQS):
    ctx = ExitStack()
    with ctx:
        def sb(name, shape, dt=F32):
            return ctx.enter_context(nc.sbuf_tensor(name, shape, dt))

        def sem(name):
            return ctx.enter_context(nc.semaphore(name))

        ring = [ctx.enter_context(nc.psum_tensor(f"ring{i}", [P, 1024], F32)) for i in range(3)]
        pv_bank = [ctx.enter_context(nc.psum_tensor(f"pv_bank{i}", [P, 512], F32)) for i in range(2)]
        PREP = 1
        FRONT, BACK = front_steps(), back_steps()
        WEIGHTS = weight_steps()
        FIRST = Segment(interleaved(FRONT, WEIGHTS, [26, 1, 4, 1, 6, 1, 6, 1, 6, 1, 2, 1, len(FRONT) - 50]), PREP)
        done = PREP + FIRST.n
        BOTH = Segment(interleaved(FRONT, BACK, RUNS), done)
        LAST = Segment(interleaved([], BACK, [0, len(BACK)]), done + (seqs - 1) * BOTH.n)
        assert BOTH.n % 3 == 0
        assert BOTH.order.index(("l", 0, "xT")) < BOTH.order.index((0, "proj"))

        ident = sb("ident", [P, P])
        identb = sb("identb", [P, P], BF16)
        alibi_xq = sb("alibi_xq", [P, 2, S], BF16)
        alibi_xk = sb("alibi_xk", [P, 2, S], BF16)
        alibi_d = sb("alibi_d", [P, 4 * PAIRS, P], BF16)
        band_q = sb("band_q", [P, BAND], BF16)
        wqkvT = sb("wqkvT", [P, 2, 3 * D])
        woT = sb("woT", [P, 2, D])
        bqkv = sb("bqkv", [P, 2, 3 * D])
        bo = sb("bo", [P, 2, D])
        wguT = sb("wguT", [P, 2, INTER])
        wdT = sb("wdT", [P, 3, D])
        wl_qkv = sb("wl_qkv", [P, LAYERS, 3 * LH * LD])
        wl_o = sb("wl_o", [P, LAYERS, 4, D])
        w1 = sb("w1", [P, LAYERS, 2 * HID])
        w2 = sb("w2", [P, LAYERS, 3, D])
        b1 = sb("b1", [P, LAYERS, 2, 3])
        b2 = sb("b2", [P, LAYERS, D])
        ln_g = sb("ln_g", [P, LAYERS])
        ln_b = sb("ln_b", [P, LAYERS])
        rot_c = sb("rot_c", [P, LAYERS, T, 2, LD])
        rot_s = sb("rot_s", [P, LAYERS, T, 2, LD])
        neg_half = sb("neg_half", [P, 16])
        neg_one = sb("neg_one", [P, LH // 2])
        zeros = sb("zeros", [P, 64])

        x_next = sb("x_next", [P, T, D])
        x = sb("x", [P, T, D])
        y = sb("y", [P, T, D])
        xT = sb("xT", [P, S])
        stats = [sb(f"stats{i}", [P, T, 6]) for i in range(2)]
        mv = [sb(f"mv{i}", [P, T, 2]) for i in range(2)]
        rstd = [sb(f"rstd{i}", [P, T]) for i in range(2)]
        fbig = sb("fbig", [P, 10 * 1024])
        qk = fbig[:, 0:1024].rearrange("p (t s c) -> p t s c", t=T, s=2)
        part0 = sb("part0", [P, T, 2, D], BF16)
        part1 = fbig[:, 6144:6656].bitcast(BF16).rearrange("p (t s c) -> p t s c", t=T, s=2)
        aug = sb("aug", [P, 2, T, H, SLOTS], BF16)
        v_aug = sb("v_aug", [P, T, H, 32])
        qkT = fbig[:, 1024:5120].bitcast(BF16).rearrange("p (g b c s) -> p g b c s", g=QUADS, b=2, c=2)
        qmT = fbig[:, 5120:6144].bitcast(BF16).rearrange("p (g b s) -> p g b s", g=2, b=2)
        neg_max = sb("neg_max", [P, QUADS, T, 4])
        max_r1 = sb("max_r1", [P, T, 4])
        prob = fbig[:, 6144:10240].rearrange("p (n m s) -> p n m s", n=4, m=2)
        oT = sb("oT", [P, 2, S])
        rsum = sb("rsum", [P, T * 4])
        att = sb("att", [P, T, D])
        attT = xT
        n4 = T * INTER
        h4 = fbig[:, 0:n4]
        a4 = fbig[:, n4:2 * n4]
        s4 = fbig[:, 2 * n4:3 * n4]
        c4 = fbig[:, 3 * n4:4 * n4]
        d4 = fbig[:, 4 * n4:5 * n4]
        hqT = fbig[:, 5 * n4:5 * n4 + 3 * S].rearrange("p (c s) -> p c s", c=3)
        silu = fbig[:, 5 * n4 + 3 * S:5 * n4 + 3 * S + 2 * INTER].rearrange("p (c s) -> p c s", c=2)
        fp4_x = (a4, s4, c4, d4)
        amax = sb("amax", [P, n4 // FB])
        fscale = sb("fscale", [P, n4 // FB])
        finv = sb("finv", [P, n4 // FB])

        xb = sb("xb", [P, T, D])
        yb = sb("yb", [P, T, D])
        res = sb("res", [P, T, D])
        xTb = sb("xTb", [P, S])
        bbig = sb("bbig", [P, 10 * 1024])
        lqk = bbig[:, 0:2048].rearrange("p (b s h d) -> p b s h d", b=2, s=2, h=LH)
        lsq = bbig[:, 2048:4096].rearrange("p (b s h d) -> p b s h d", b=2, s=2, h=LH)
        lrs = bbig[:, 4096:6144].rearrange("p (b s h d) -> p b s h d", b=2, s=2, h=LH)
        lqkT = bbig[:, 6144:10240].rearrange("p (c s) -> p c s", c=8)
        lprob = bbig[:, 0:3072].rearrange("p (b h k) -> p b h k", b=2, h=LH)
        lown = bbig[:, 3072:4096].rearrange("p (h q) -> p h q", h=LH)
        lprev = bbig[:, 4096:5120].rearrange("p (h q) -> p h q", h=LH)
        gel = bbig[:, 0:1536].rearrange("p (c s) -> p c s", c=3)
        hid = bbig[:, 1536:3072].rearrange("p (c s) -> p c s", c=3)
        hn = bbig[:, 3072:3584].rearrange("p (t c) -> p t c", t=T)
        NW = (6 * 8 + 22) * FB
        NBW = NW // FB
        hw, *fp4_w = (bbig[:, i * NW:(i + 1) * NW] for i in range(5))
        rot_w = bbig[:, 5 * NW:5 * NW + 8 * LD]
        lv = sb("lv", [P, T, LH, LD])
        lss = sb("lss", [P, T, 16])
        lrn = sb("lrn", [P, T, 16])
        lneg = sb("lneg", [P, T, LH])
        loT = sb("loT", [P, 4, S])
        lsum = sb("lsum", [P, T, LH])
        lrsum = sb("lrsum", [P, T, LH])

        w_attn = sem("w_attn")
        w_alibi = sem("w_alibi")
        w_rest = sem("w_rest")
        x_in = sem("x_in")
        out_done = sem("out_done")
        filled = sem("filled")
        freed = [sem(f"freed{i}") for i in range(3)]
        prep_v = sem("prep_v")
        prep_a = sem("prep_a")
        prep_g = sem("prep_g")
        wT_ready = sem("wT_ready")
        qkv_ready = sem("qkv_ready")
        hi_ready = sem("hi_ready")
        aug_a = sem("aug_a")
        aug_v = sem("aug_v")
        maxq_ready = sem("maxq_ready")
        pv_done = sem("pv_done")
        oT_ready = sem("oT_ready")
        x_ready = sem("x_ready")
        fq_x = sem("fq_x")
        fq_s = sem("fq_s")
        fq_g = sem("fq_g")
        fq_q = sem("fq_q")
        hqT_ready = sem("hqT_ready")
        silu_ready = sem("silu_ready")
        var_ready = [sem("var_front"), sem("var_back")]
        rstd_ready = [sem("rstd_front"), sem("rstd_back")]
        xTb_ready = sem("xTb_ready")
        lraw_ready = sem("lraw_ready")
        lss_ready = sem("lss_ready")
        lrn_ready = sem("lrn_ready")
        lsin_ready = sem("lsin_ready")
        lrot_ready = sem("lrot_ready")
        lhead_ready = sem("lhead_ready")
        lnorm_ready = sem("lnorm_ready")
        lneg_ready = sem("lneg_ready")
        h_back = sem("h_back")
        gel_ready = sem("gel_ready")
        hid_ready = sem("hid_ready")
        out_ready = sem("out_ready")

        def flat(v):
            return v.rearrange("p t s c -> p (t s c)")

        def slots(copy, side, part):
            for k, which in enumerate((Q_PART, K_PART)[side]):
                if which == part:
                    copy(aug[:, side, :, :, 8 * k:8 * k + 8],
                         (part0, part1)[part][:, :, side, :].rearrange("p t (h d) -> p t h d", d=HD))

        block = ctx.enter_context(nc.Block())
        N_ATTN = 11
        N_REST = 41
        HALF = [(0, n4 // 2), (n4 // 2, n4)]

        def program(eng, weights, front, head, tail, end):
            def back(seg, turn, n):
                for l in range(LAYERS):
                    yield from head(seg, turn, n, l)
                    yield from tail(seg, turn, n, l)
                yield from end(seg, turn, n)

            run_steps(FIRST, front(FIRST, 0, 0), weights())
            with eng.Fori(0, seqs - 1) as r:
                run_steps(BOTH, front(BOTH, r, r + 1), back(BOTH, r, r))
            run_steps(LAST, back(LAST, 0, seqs - 1))

        @block.sync
        def _(sp):
            count = {"a": 0, "r": 0}

            def load_a(dst, src):
                sp.dma_start(dst, src).then_inc(w_attn, 16)
                count["a"] += 1

            def load(dst, src, **k):
                sp.dma_start(dst, src, **k).then_inc(w_rest, 16)
                count["r"] += 1

            rows = lambda n: ins["x"][n].rearrange("o (t p) d -> p (o t) d", p=P)
            load_a(ident[:], ins["ident"])
            load_a(y[:, 0:3, :], ins["wqkv0"].rearrange("(c p) d -> p c d", p=P))
            load_a(yb[:, 0:3, :], ins["wqkv1"].rearrange("(c p) d -> p c d", p=P))
            load_a(y[:, 3, :], ins["wo0"])
            load_a(yb[:, 3, :], ins["wo1"])
            sp.dma_start(x_next[:], rows(slice(0, 1))).then_inc(x_in, 16)
            for a in range(2):
                load_a(bqkv[:, a, :], ins[f"bqkv{a}"].rearrange("(o n) -> o n", o=1).broadcast_to([P, 3 * D]))
                load_a(bo[:, a, :], ins[f"bo{a}"].rearrange("(o n) -> o n", o=1).broadcast_to([P, D]))
            load_a(identb[:], ins["identb"])
            load_a(part0[:].rearrange("p t s c -> p (t s c)"), ins["alibi_b"])
            for dst, name in ((alibi_d, "alibi_d"), (alibi_xq, "alibi_xq"), (alibi_xk, "alibi_xk")):
                sp.dma_start(dst[:], ins[name]).then_inc(w_alibi, 16)
            load(band_q[:], ins["band_q"])
            for l in range(LAYERS):
                load(rot_c[:, l], ins["rot_c"])
                load(rot_s[:, l], ins["rot_s"])
            load(wl_qkv[:], ins["wl_qkv"].rearrange("l d n -> d l n"))
            for l in range(LAYERS):
                load(wl_o[:, l], ins["wl_o"][l].rearrange("(c p) n -> p c n", p=P))
            load(hw[:, 0:256].rearrange("p (c d) -> p c d", c=2), ins["wgate"][0:256, :].rearrange("(c p) d -> p c d", p=P))
            load(hw[0:96, 256:384], ins["wgate"][256:352, :])
            load(hw[:, 384:640].rearrange("p (c d) -> p c d", c=2), ins["wup"][0:256, :].rearrange("(c p) d -> p c d", p=P))
            load(hw[0:96, 640:768], ins["wup"][256:352, :])
            load(hw[:, 768:768 + INTER], ins["wdown"])
            load(w1[:], ins["w1"].rearrange("l d n -> d l n"))
            for c, (c0, cw) in enumerate(HCH):
                load(w2[0:cw, :, c, :], ins["w2"][:, c0:c0 + cw, :].rearrange("l p n -> p l n"))
                for side in range(2):
                    load(b1[0:cw, :, side, c], ins["b1"][:, side * HID + c0:side * HID + c0 + cw].rearrange("l p -> p l"),
                         allow_slow_non_contiguous=True)
            for l in range(LAYERS):
                load(b2[:, l, :], ins["b2"][l:l + 1, :].broadcast_to([P, D]))
                load(ln_g[:, l:l + 1], ins["ln_g"][l:l + 1, :].rearrange("l p -> p l"), allow_slow_non_contiguous=True)
                load(ln_b[:, l:l + 1], ins["ln_b"][l:l + 1, :].rearrange("l p -> p l"), allow_slow_non_contiguous=True)
            for l in range(LAYERS):
                for side, name in ((0, "q_scale"), (1, "k_scale")):
                    load(rot_w[:, (2 * l + side) * LD:(2 * l + side + 1) * LD], ins[name][l:l + 1, :].broadcast_to([P, LD]))
                    for half in range(2):
                        o = 4 * LD + (2 * l + side) * LD + 32 * half
                        load(rot_w[:, o:o + 32], ins[name][l:l + 1, 32 - 32 * half:64 - 32 * half].broadcast_to([P, 32]))
            assert count == {"a": N_ATTN, "r": N_REST}
            sp.wait_ge(x_ready, 1)
            sp.dma_start(x_next[:], rows(slice(1, 2))).then_inc(x_in, 16)
            with sp.Fori(0, seqs - 2) as i:
                sp.wait_ge(x_ready, 3 * (i + 1) + 1)
                sp.dma_start(x_next[:], rows(bass.ds(i + 2, 1))).then_inc(x_in, 16)
                sp.wait_ge(out_ready, i + 1)
                sp.dma_start(out[bass.ds(i, 1)].rearrange("o (t p) d -> p (o t) d", p=P), res[:]).then_inc(out_done, 16)
            for i in range(seqs - 2, seqs):
                sp.wait_ge(out_ready, i + 1)
                sp.dma_start(out[i:i + 1].rearrange("o (t p) d -> p (o t) d", p=P), res[:]).then_inc(out_done, 16)
            sp.wait_ge(out_done, 16 * (seqs + 1))

        @block.gpsimd
        def _(pool):
            G = nc.gpsimd
            G.memset(aug[:, 0], 0.0)
            G.memset(neg_half[:], -0.5)
            G.memset(neg_one[:], -1.0)
            G.memset(zeros[:], 0.0)
            pool.drain()
            pool.wait_ge(w_attn, 16 * N_ATTN)
            for side in range(2):
                G.tensor_copy(aug[:, side, :, :, B_SLOT:B_SLOT + 2 * T].rearrange("p t h s -> p (t h) s"),
                              part0[:].rearrange("p t s c -> p (t s c)")[:, side * 512:(side + 1) * 512].rearrange("p (n s) -> p n s", s=2 * T))
            pool.drain().then_inc(prep_g, 1)

            def weights():
                yield ("w", "rot")
                pool.wait_ge(prep_v, 1)
                yield ("w", "q", 1)
                signs = fp4_w[1].rearrange("p (b f) -> p b f", f=FB)
                pool.wait_ge(fq_s, 1)
                G.tensor_tensor(signs, signs, fscale[:, 0:NBW].unsqueeze(2).broadcast_to([P, NBW, FB]), ALU.mult).then_inc(fq_g, 1)

            def rsqrt(side, value):
                pool.wait_ge(var_ready[side], value)
                G.tensor_tensor(rstd[side][:], mv[side][:, :, 1], neg_half[:, 0:T], ALU.pow).then_inc(rstd_ready[side], 1)

            def front(seg, turn, n):
                def maxima(*names):
                    for slot, count in seg.needs(turn, names):
                        pool.wait_ge(freed[slot], count)

                def fp4_scale(k, lo_, hi):
                    s = s4[:, lo_:hi].rearrange("p (b f) -> p b f", f=FB)
                    pool.wait_ge(fq_s, n * 3 + 1 + k)
                    G.tensor_tensor(s, s, fscale[:, lo_ // FB:hi // FB].unsqueeze(2).broadcast_to([P, (hi - lo_) // FB, FB]), ALU.mult).then_inc(fq_g, 1)

                def attention(a):
                    for g in range(QUADS):
                        yield (a, "mT", g)
                        maxima(*((a, "s1", g, t, pr) for t in range(T) for pr in range(2)))
                        part = lambda k: aug[:, 0, :, 4 * g:4 * g + 4, M_SLOT + k]
                        zero = zeros[:, 0:16].rearrange("p (t h) -> p t h", t=T)
                        G.tensor_tensor(part(0), neg_max[:, g], zero, ALU.add)
                        pool.drain()
                        G.tensor_tensor(max_r1[:], neg_max[:, g], part(0), ALU.subtract)
                        pool.drain()
                        G.tensor_copy(part(1), max_r1[:])
                        pool.drain()
                        G.tensor_tensor(part(2), max_r1[:], part(1), ALU.subtract)
                        pool.drain().then_inc(maxq_ready, 1)
                    yield (a, "proj")
                    pool.wait_ge(filled, seg.filled((a, "mT", QUADS - 1), turn))
                    zero = zeros[:].rearrange("p (t h) -> p t h", t=T)
                    for k in range(3):
                        G.tensor_tensor(aug[:, 0, :, :, M_SLOT + k], zero, zero, ALU.add)
                    pool.drain()
                    rsqrt(0, n * 3 + 1 + 2 * a)

                yield from attention(0)
                yield ("f", "q1", 1)
                fp4_scale(1, 0, T * D)
                for half in range(2):
                    yield ("f", "q2", 1, half)
                    fp4_scale(2 + half, *HALF[half])
                yield ("f", "down")
                rsqrt(0, n * 3 + 2)
                yield from attention(1)

            def head(seg, turn, n, l):
                for kind, t in LOCAL_FRONT:
                    if kind != "qk":
                        continue
                    yield ("l", l, "qk", t)
                    pool.wait_ge(lraw_ready, n * 8 + l * 4 + t + 1)
                    pool.wait_ge(lss_ready, n * 8 + l * 4 + t + 1)
                    G.tensor_tensor(lrn[:, t, :], lss[:, t, :], neg_half[:, 0:16], ALU.pow).then_inc(lrn_ready, 1)
                    for half in range(2):
                        for side in range(2):
                            G.tensor_tensor(
                                lsq[:, t % 2, side, :, 32 * half:32 * half + 32],
                                lqk[:, t % 2, side, :, 32 - 32 * half:64 - 32 * half],
                                rot_s[:, l, t, side, 32 * half:32 * half + 32].unsqueeze(1).broadcast_to([P, LH, 32]),
                                ALU.mult)
                    pool.drain().then_inc(lsin_ready, 1)

            def tail(seg, turn, n, l):
                for kind, t, *q in local_order():
                    if kind != "s":
                        continue
                    yield ("l", l, kind, t, *q)
                    heads, w = slice(4 * q[0], 4 * q[0] + 4), BAND if t else P
                    for slot, count in seg.needs(turn, [("l", l, "s", t, *q)]):
                        pool.wait_ge(freed[slot], count)
                    G.tensor_tensor(lrsum[:, t, heads], lsum[:, t, heads], neg_one[:], ALU.pow)
                    pool.drain()
                    p_ = lprob[:, t % 2, heads, 0:w]
                    G.tensor_tensor(p_, p_, lrsum[:, t, heads].unsqueeze(2).broadcast_to([P, 4, w]), ALU.mult).then_inc(lnorm_ready, 1)
                yield ("l", l, "hB")
                rsqrt(1, n * 3 + 1 + l)

            def end(seg, turn, n):
                yield ("end", 0)
                rsqrt(1, n * 3 + 3)

            program(pool, weights, front, head, tail, end)

        @block.scalar
        def _(act):
            def copy(dst, src, func=ACT.Copy, **k):
                return nc.scalar.activation(dst, src, func, **k)

            act.wait_ge(filled, 1)
            copy(wqkvT[:, 0, :], ring[0][:, 0:384])
            copy(wqkvT[:, 1, :], ring[0][:, 384:768])
            copy(woT[:].rearrange("p a d -> p (a d)"), ring[0][:, 768:1024]).then_inc(freed[0], 1)
            act.drain().then_inc(prep_a, 1)

            def weights():
                yield ("w", "q", 0)
                act.wait_ge(fq_x, 1)
                copy(fp4_w[1], fp4_w[0], ACT.Sign)
                act.drain()
                copy(fp4_w[0], fp4_w[0], ACT.Abs).then_inc(fq_s, 1)
                yield ("w", "guT")
                i = FIRST.slot(("w", "guT"))
                act.wait_ge(filled, FIRST.filled(("w", "guT"), 0))
                copy(wguT[:, 0, :], ring[i][:, 0:INTER])
                copy(wguT[:, 1, :], ring[i][:, 512:512 + INTER]).then_inc(freed[i], 1)
                yield ("w", "dT")
                i = FIRST.slot(("w", "dT"))
                act.wait_ge(filled, FIRST.filled(("w", "dT"), 0))
                copy(wdT[0:96, 2, :], ring[i][0:96, 256:384])
                copy(wdT[:, 0:2, :].rearrange("p c d -> p (c d)"), ring[i][:, 0:256]).then_inc(freed[i], 1)
                act.drain().then_inc(wT_ready, 1)

            def front(seg, turn, n):
                def take(*name):
                    act.wait_ge(filled, seg.filled(name, turn))
                    return ring[seg.slot(name)]

                def release(ins_, *name):
                    ins_.then_inc(freed[seg.slot(name)], 1)
                    return ins_

                def attention(a):
                    yield (a, "xT")
                    release(copy(xT[:], take(a, "xT")[:, 0:S]), a, "xT")
                    yield (a, "aug", 0)
                    act.wait_ge(qkv_ready, n * 2 + a + 1)
                    copy(flat(part0[:]), flat(qk)).then_inc(hi_ready, 1)
                    act.drain()
                    slots(copy, 0, 0)
                    act.drain().then_inc(aug_a, 1)
                    for g in range(QUADS):
                        yield (a, "qkT", g)
                        release(copy(qkT[:, g].rearrange("p a b s -> p (a b s)"), take(a, "qkT", g)[:].bitcast(BF16)),
                                a, "qkT", g)
                    k = 0
                    for kind, i in attention_order():
                        if kind == "mT":
                            yield (a, "mT") + i
                            g, = i
                            release(copy(qmT[:, g % 2].rearrange("p b s -> p (b s)"), take(a, "mT", g)[:, 0:512].bitcast(BF16)),
                                    a, "mT", g)
                        elif kind == "s2":
                            yield (a, "s2") + i
                            if k >= 4:
                                act.wait_ge(pv_done, n * 32 + a * 16 + (k - 4) // 2 + 1)
                            release(copy(prob[:, k % 4].rearrange("p m s -> p (m s)"), take(a, "s2", *i)[:], ACT.Exp),
                                    a, "s2", *i)
                            k += 1
                            if i[1:] == (0, 1) and i[0]:
                                pv_out(a, i[0] - 1)
                        elif kind == "oT" and i[0] == QUADS - 1:
                            yield (a, "oT") + i
                            pv_out(a, QUADS - 1)
                    yield (a, "aT")
                    release(copy(attT[:], take(a, "aT")[:, 0:S]), a, "aT")

                def pv_out(a, g):
                    act.wait_ge(pv_done, n * 32 + a * 16 + 4 * g + 4)
                    copy(oT[:, g % 2, :], pv_bank[g % 2][:]).then_inc(oT_ready, 1)

                def fp4_sizes(k, lo_, hi):
                    act.wait_ge(fq_x, n * 3 + 1 + k)
                    copy(s4[:, lo_:hi], a4[:, lo_:hi], ACT.Sign)
                    act.drain()
                    copy(a4[:, lo_:hi], a4[:, lo_:hi], ACT.Abs).then_inc(fq_s, 1)

                yield from attention(0)
                yield ("f", "q1", 0)
                fp4_sizes(1, 0, T * D)
                yield ("f", "xqT")
                release(copy(xT[:], take("f", "xqT")[:, 0:S]), "f", "xqT")
                for t in range(T):
                    yield ("f", "gu", t)
                    gate = take("f", "gu", t)[:, 0:INTER]
                    if t >= 2:
                        for slot, count in seg.needs(turn, [("f", "gu", t - 2)]):
                            act.wait_ge(freed[slot], count)
                    copy(silu[:, t % 2, :], gate, ACT.Silu).then_inc(silu_ready, 1)
                for half in range(2):
                    yield ("f", "q2", 0, half)
                    fp4_sizes(2 + half, *HALF[half])
                for c, (c0, cw) in enumerate(ICH):
                    yield ("f", "hT", c)
                    release(copy(hqT[0:cw, c, :], take("f", "hT", c)[0:cw, 0:S]), "f", "hT", c)
                act.drain().then_inc(hqT_ready, 1)
                yield from attention(1)

            def taking(seg, turn):
                def take(*name):
                    act.wait_ge(filled, seg.filled(name, turn))
                    return ring[seg.slot(name)]

                def release(ins_, *name):
                    ins_.then_inc(freed[seg.slot(name)], 1)
                    return ins_
                return take, release

            def shifted(src):
                copy(xTb[64:128, 0:1], ident[64:128, 0:1])
                copy(xTb[0:64, :], src[0:64, 0:S])
                return copy(xTb[64:128, 1:S], src[64:128, 0:S - 1])

            def head(seg, turn, n, l):
                take, release = taking(seg, turn)
                L = ("l", l)
                yield (*L, "xT")
                release(shifted(take(*L, "xT")), *L, "xT")
                act.drain().then_inc(xTb_ready, 1)
                for kind, t in LOCAL_FRONT:
                    if kind == "ro":
                        continue
                    yield (*L, kind, t)
                    if kind == "qk":
                        src = take(*L, "qk", t)[:]
                        if t >= 2:
                            act.wait_ge(lrot_ready, n * 8 + l * 4 + t - 1)
                        copy(lqk[:, t % 2].rearrange("p s h d -> p (s h d)"), src)
                        release(copy(lsq[:, t % 2].rearrange("p s h d -> p (s h d)"), src, ACT.Square), *L, "qk", t)
                        act.drain().then_inc(lraw_ready, 1)
                    elif kind == "v":
                        release(copy(lv[:, 2 * t:2 * t + 2].rearrange("p t h d -> p (t h) d"),
                                     take(*L, "v", t)[:].rearrange("p (h d) -> p h d", d=LD)), *L, "v", t)
                    else:
                        release(copy(lqkT[:, :, t * P:(t + 1) * P], take(*L, "rT", t)[:].rearrange("p (c q) -> p c q", c=8)),
                                *L, "rT", t)
                act.drain().then_inc(lhead_ready, 1)

            def tail(seg, turn, n, l):
                take, release = taking(seg, turn)
                L = ("l", l)
                for kind, t, *q in local_order():
                    if kind == "prev":
                        continue
                    yield (*L, kind, t, *q)
                    if kind == "s":
                        q, w = q[0], BAND if t else P
                        o = take(*L, "s", t, q)
                        act.wait_ge(lneg_ready, n * 16 + l * 8 + 2 * t + q + 1)
                        for m in range(2):
                            for u in range(2):
                                c = 512 * m + BAND * u
                                h = 4 * q + 2 * u + m
                                last = copy(lprob[:, t % 2, h, 0:w], o[:, c:c + w], ACT.Exp,
                                            bias=lneg[:, t, 4 * q + 2 * m + u:4 * q + 2 * m + u + 1], accum_out=lsum[:, t, h:h + 1])
                        release(last, *L, "s", t, q)
                    elif kind == "own":
                        release(copy(lown.rearrange("p h q -> p (h q)"), take(*L, "own", t)[:]), *L, "own", t)
                    else:
                        release(copy(loT[:, :, t * P:(t + 1) * P], take(*L, "pv", t)[:, 0:S].rearrange("p (c q) -> p c q", c=4)),
                                *L, "pv", t)
                yield (*L, "x2T")
                release(shifted(take(*L, "x2T")), *L, "x2T")
                act.drain().then_inc(xTb_ready, 1)
                yield (*L, "hT")
                release(copy(xTb[:], take(*L, "hT")[:, 0:S], ACT.Identity, scale=ln_g[:, l:l + 1], bias=ln_b[:, l:l + 1]),
                        *L, "hT")
                for c, (c0, cw) in enumerate(HCH):
                    yield (*L, "w1", c)
                    copy(gel[0:cw, c, :], take(*L, "w1", c)[0:cw, 512:1024], ACT.Gelu, bias=b1[0:cw, l, 1, c:c + 1]).then_inc(gel_ready, 1)

            def end(seg, turn, n):
                yield from ()

            program(act, weights, front, head, tail, end)

        @block.vector
        def _(dve):
            V = nc.vector

            def fp4_low(lo_, hi, bufs=fp4_x):
                a, _, c, d = (v[:, lo_:hi] for v in bufs)
                V.tensor_scalar(c, a, 5.0, 2.0, ALU.is_gt, ALU.mult)
                V.tensor_scalar(d, a, 0.25, None, ALU.is_gt)
                dve.drain()
                V.scalar_tensor_tensor(c, a, 3.5, c, ALU.is_gt, ALU.add)
                V.scalar_tensor_tensor(d, a, 0.75, d, ALU.is_gt, ALU.add)
                dve.drain()
                V.scalar_tensor_tensor(c, a, 2.5, c, ALU.is_gt, ALU.add)
                V.scalar_tensor_tensor(d, a, 1.25, d, ALU.is_gt, ALU.add)
                dve.drain()

            def fp4_high(lo_, hi, bufs=fp4_x):
                a, _, c, d = (v[:, lo_:hi] for v in bufs)
                V.scalar_tensor_tensor(d, a, 1.75, d, ALU.is_gt, ALU.add)
                dve.drain()
                V.scalar_tensor_tensor(d, c, 2.0, d, ALU.mult, ALU.add)
                dve.drain()

            def fp4_norm(src, lo_, hi, bufs=fp4_x):
                b0, nb = lo_ // FB, (hi - lo_) // FB
                blocks = slice(b0, b0 + nb)
                src = src[:, lo_:hi]
                V.tensor_reduce(amax[:, blocks], src.rearrange("p (b f) -> p b f", f=FB), op=ALU.max, axis=AX,
                                apply_absolute_value=True)
                dve.drain()
                V.tensor_scalar(fscale[:, blocks], amax[:, blocks], 1.0 / 6.0, 1e-12, ALU.mult, ALU.max)
                dve.drain()
                V.reciprocal(finv[:, blocks], fscale[:, blocks])
                dve.drain()
                V.tensor_tensor(bufs[0][:, lo_:hi].rearrange("p (b f) -> p b f", f=FB),
                                src.rearrange("p (b f) -> p b f", f=FB),
                                finv[:, blocks].unsqueeze(2).broadcast_to([P, nb, FB]), ALU.mult).then_inc(fq_x, 1)

            def fp4_value(dst, lo_, hi, bufs=fp4_x):
                V.scalar_tensor_tensor(dst[:, lo_:hi], bufs[3][:, lo_:hi], 0.5, bufs[1][:, lo_:hi], ALU.mult, ALU.mult).then_inc(fq_q, 1)

            def moments(side, src):
                for t in range(T):
                    V.bn_stats(stats[side][:, t, :], src[:, t, :])
                dve.drain()
                for t in range(T):
                    V.bn_aggr(mv[side][:, t, :], stats[side][:, t, :])
                dve.drain()
                V.tensor_scalar(mv[side][:, :, 1], mv[side][:, :, 1], EPS, None, ALU.add).then_inc(var_ready[side], 1)

            def normalise(side, dst, src, value):
                dve.wait_ge(rstd_ready[side], value)
                for t in range(T):
                    last = V.tensor_scalar(dst[:, t, :], src[:, t, :], mv[side][:, t, 0:1], rstd[side][:, t:t + 1], ALU.subtract, ALU.mult)
                return last

            V.memset(hw[96:128, 256:384], 0.0)
            V.memset(hw[96:128, 640:768], 0.0)
            V.memset(v_aug[:], 0.0)
            V.memset(aug[:, 1, :, :, 0:B_SLOT], 0.0)
            V.memset(aug[:, 1, :, :, B_SLOT + 2 * T:SLOTS], 0.0)
            dve.drain()
            V.memset(aug[:, 1, :, :, M_SLOT:M_SLOT + 3], 1.0)
            V.memset(v_aug[:, :, :, HD:HD + 1], 1.0)
            dve.wait_ge(w_attn, 16 * N_ATTN)
            for a in range(2):
                V.tensor_scalar(bqkv[:, a, 0:D], bqkv[:, a, 0:D], HD ** -0.5, None, ALU.mult)
            dve.drain()
            dve.sem_inc(out_done, 16)

            def weights():
                yield ("w", "rot")
                dve.wait_ge(w_rest, 16 * N_REST)
                for l in range(LAYERS):
                    for side in range(2):
                        for tab, o in ((rot_c, 0), (rot_s, 4 * LD)):
                            o += (2 * l + side) * LD
                            V.tensor_tensor(tab[:, l, :, side, :], tab[:, l, :, side, :],
                                            rot_w[:, o:o + LD].unsqueeze(1).broadcast_to([P, T, LD]), ALU.mult)
                dve.drain().then_inc(prep_v, 1)
                yield ("w", "q", 0)
                fp4_norm(hw, 0, NW, fp4_w)
                yield ("w", "q", 1)
                dve.wait_ge(fq_s, 1)
                fp4_low(0, NW, fp4_w)
                yield ("w", "q", 2)
                fp4_high(0, NW, fp4_w)
                dve.wait_ge(fq_g, 1)
                fp4_value(hw, 0, NW, fp4_w)

            def front(seg, turn, n):
                def take(*name):
                    dve.wait_ge(filled, seg.filled(name, turn))
                    return ring[seg.slot(name)]

                def release(ins_, *name):
                    ins_.then_inc(freed[seg.slot(name)], 1)
                    return ins_

                def close_block(name, was, bias, dst, k):
                    yield name
                    o = take(*name)[:, 0:S].rearrange("p (t d) -> p t d", t=T)
                    release(V.tensor_tensor(y[:], o, was[:], ALU.add), *name)
                    dve.drain()
                    if bias is not None:
                        V.tensor_tensor(y[:], y[:], bias.unsqueeze(1).broadcast_to([P, T, D]), ALU.add)
                        dve.drain()
                    moments(0, y)
                    yield (name[0], "norm")
                    normalise(0, dst, y, n * 3 + k)
                    dve.drain().then_inc(x_ready, 1)

                def attention(a):
                    for i in range(2):
                        yield (a, "qkv", i)
                        o = take(a, "qkv", i)
                        for b in range(2):
                            t = 2 * i + b
                            src = o[:, 512 * b:512 * b + 3 * D]
                            V.scalar_tensor_tensor(qk[:, t, 0, :], src[:, 0:D], HD ** -0.5, bqkv[:, a, 0:D], ALU.mult, ALU.add)
                            V.tensor_tensor(qk[:, t, 1, :], src[:, D:2 * D], bqkv[:, a, D:2 * D], ALU.add)
                            last = V.tensor_tensor(v_aug[:, t, :, 0:HD], src[:, 2 * D:3 * D].rearrange("p (h d) -> p h d", d=HD),
                                                   bqkv[:, a, 2 * D:3 * D].rearrange("p (h d) -> p h d", d=HD), ALU.add)
                        release(last, a, "qkv", i)
                    dve.drain()
                    if a == 0:
                        dve.wait_ge(prep_g, 1)
                    dve.sem_inc(qkv_ready, 1)
                    yield (a, "aug", 1)
                    dve.wait_ge(hi_ready, n * 2 + a + 1)
                    V.tensor_tensor(flat(qk), flat(qk), flat(part0[:]), ALU.subtract)
                    dve.drain()
                    V.tensor_copy(flat(part1), flat(qk))
                    dve.drain()
                    for side, parts in ((0, Q_PART), (1, K_PART)):
                        k, = (k for k, part in enumerate(parts) if part == 2)
                        heads = lambda v: v[:, :, side, :].rearrange("p t (h d) -> p t h d", d=HD)
                        V.tensor_tensor(aug[:, side, :, :, 8 * k:8 * k + 8], heads(qk), heads(part1), ALU.subtract)
                    yield (a, "aug", 2)
                    slots(V.tensor_copy, 0, 1)
                    slots(V.tensor_copy, 1, 1)
                    slots(V.tensor_copy, 1, 0)
                    dve.drain().then_inc(aug_v, 1)
                    for kind, i in attention_order():
                        if kind == "s1":
                            yield (a, "s1") + i
                            g, t, pr = i
                            release(V.tensor_reduce(neg_max[:, g, t, 2 * pr:2 * pr + 2],
                                                    take(a, "s1", *i)[:].rearrange("p (m s) -> p m s", m=2),
                                                    op=ALU.max, axis=AX, negate=True), a, "s1", *i)
                        elif kind == "oT":
                            yield (a, "oT") + i
                            g, = i
                            o4 = take(a, "oT", g)[:, 0:S].rearrange("p (n c) -> p n c", c=32)
                            V.reciprocal(rsum[:], o4[:, :, HD])
                            dve.drain()
                            release(V.tensor_tensor(att[:, :, 32 * g:32 * g + 32].rearrange("p t (j d) -> p t j d", j=4),
                                                    o4[:, :, 0:HD].rearrange("p (t j) d -> p t j d", t=T),
                                                    rsum[:].rearrange("p (t j) -> p t j", t=T).unsqueeze(3).broadcast_to([P, T, 4, HD]),
                                                    ALU.mult), a, "oT", g)
                    yield from close_block((a, "proj"), (x_next, x)[a], bo[:, a, :], x, 1 + 2 * a)

                yield from attention(0)
                xf = x[:].rearrange("p t d -> p (t d)")
                yield ("f", "q1", 0)
                fp4_norm(xf, 0, T * D)
                yield ("f", "q1", 1)
                dve.wait_ge(fq_s, n * 3 + 2)
                fp4_low(0, T * D)
                yield ("f", "q1", 2)
                fp4_high(0, T * D)
                dve.wait_ge(fq_g, n * 3 + 2)
                fp4_value(h4, 0, T * D)
                for t in range(T):
                    yield ("f", "gu", t)
                    o = take("f", "gu", t)
                    dve.wait_ge(silu_ready, n * T + t + 1)
                    release(V.tensor_tensor(h4[:, t * INTER:(t + 1) * INTER], silu[:, t % 2, :], o[:, 512:512 + INTER], ALU.mult),
                            "f", "gu", t)
                for half in range(2):
                    yield ("f", "q2", 0, half)
                    if half == 0:
                        dve.drain()
                    fp4_norm(h4, *HALF[half])
                for half in range(2):
                    yield ("f", "q2", 1, half)
                    dve.wait_ge(fq_s, n * 3 + 3 + half)
                    fp4_low(*HALF[half])
                for half in range(2):
                    yield ("f", "q2", 2, half)
                    fp4_high(*HALF[half])
                    dve.wait_ge(fq_g, n * 3 + 3 + half)
                    fp4_value(h4, *HALF[half])
                yield from close_block(("f", "down"), x, None, x, 2)
                yield from attention(1)

            def taking(seg, turn):
                def take(*name):
                    dve.wait_ge(filled, seg.filled(name, turn))
                    return ring[seg.slot(name)]

                def release(ins_, *name):
                    ins_.then_inc(freed[seg.slot(name)], 1)
                    return ins_
                return take, release

            def head(seg, turn, n, l):
                take, release = taking(seg, turn)
                L = ("l", l)
                yield (*L, "xT")
                if l == 0:
                    V.tensor_copy(xb[:], x[:])
                for kind, t in LOCAL_FRONT:
                    if kind == "qk":
                        yield (*L, "qk", t)
                        dve.wait_ge(lraw_ready, n * 8 + l * 4 + t + 1)
                        V.tensor_reduce(lss[:, t, :], lsq[:, t % 2].rearrange("p s h d -> p (s h) d"), op=ALU.add, axis=AX)
                        for side in range(2):
                            V.tensor_tensor(lrs[:, t % 2, side], lqk[:, t % 2, side],
                                            rot_c[:, l, t, side, :].unsqueeze(1).broadcast_to([P, LH, LD]), ALU.mult)
                        dve.drain()
                        V.tensor_scalar(lss[:, t, :], lss[:, t, :], 1e-24, None, ALU.max).then_inc(lss_ready, 1)
                    elif kind == "ro":
                        yield (*L, "ro", t)
                        flat = lambda v: v[:, t % 2].rearrange("p s h d -> p (s h d)")
                        heads = lrs[:, t % 2].rearrange("p s h d -> p (s h) d")
                        dve.wait_ge(lsin_ready, n * 8 + l * 4 + t + 1)
                        V.tensor_tensor(flat(lrs), flat(lrs), flat(lsq), ALU.add)
                        dve.drain()
                        dve.wait_ge(lrn_ready, n * 8 + l * 4 + t + 1)
                        V.tensor_tensor(heads, heads, lrn[:, t, :].unsqueeze(2).broadcast_to([P, 16, LD]), ALU.mult).then_inc(lrot_ready, 1)

            def tail(seg, turn, n, l):
                take, release = taking(seg, turn)
                L = ("l", l)
                for kind, t, *q in local_order():
                    if kind not in ("s", "prev"):
                        continue
                    yield (*L, kind, t, *q)
                    o = take(*L, kind, t, *q)[:]
                    if kind == "s":
                        q, w = q[0], BAND if t else P
                        heads = lambda v: v[:, :, 0:2 * BAND].rearrange("p m (u w) -> p m u w", u=2)[:, :, :, 0:w]
                        sc = heads(o.rearrange("p (m w) -> p m w", m=2))
                        neg = lneg[:, t, 4 * q:4 * q + 4].rearrange("p (m u) -> p m u", m=2)
                        V.tensor_reduce(neg, sc, op=ALU.max, axis=AX, negate=True).then_inc(lneg_ready, 1)
                    elif kind == "prev":
                        release(V.tensor_copy(lprev[WIN:P].rearrange("p h q -> p (h q)"), o[WIN:P, :]), *L, "prev", t)
                for i in range(2):
                    yield (*L, "wo", i)
                    tiles = slice(2 * i, 2 * i + 2)
                    release(V.tensor_tensor(yb[:, tiles], take(*L, "wo", i)[:, 0:2 * D].rearrange("p (t d) -> p t d", t=2),
                                            (xb, yb)[l][:, tiles], ALU.add), *L, "wo", i)
                yield (*L, "hB")
                release(V.tensor_copy(hn, take(*L, "hB")[:, 0:S].rearrange("p (t d) -> p t d", t=T)), *L, "hB")
                dve.drain()
                moments(1, hn)
                V.tensor_tensor(yb[:], yb[:], b2[:, l, :].unsqueeze(1).broadcast_to([P, T, D]), ALU.add)
                yield (*L, "norm")
                normalise(1, hn, hn, n * 3 + 1 + l)
                dve.drain().then_inc(h_back, 1)
                for c, (c0, cw) in enumerate(HCH):
                    yield (*L, "w1", c)
                    o = take(*L, "w1", c)
                    dve.wait_ge(gel_ready, n * 6 + l * 3 + c + 1)
                    release(V.scalar_tensor_tensor(hid[0:cw, c, :], o[0:cw, 0:S], b1[0:cw, l, 0, c:c + 1],
                                                   gel[0:cw, c, :], ALU.add, ALU.mult), *L, "w1", c)
                dve.drain().then_inc(hid_ready, 1)
                yield (*L, "w2")
                release(V.tensor_tensor(yb[:], take(*L, "w2")[:, 0:S].rearrange("p (t d) -> p t d", t=T), yb[:], ALU.add),
                        *L, "w2")

            def end(seg, turn, n):
                yield ("end", 0)
                dve.drain()
                V.tensor_tensor(yb[:], yb[:], xb[:], ALU.add)
                dve.drain()
                moments(1, yb)
                yield ("end", 1)
                dve.wait_ge(out_done, 16 * n + 16)
                normalise(1, res, yb, n * 3 + 3)
                dve.drain().then_inc(out_ready, 1)

            program(dve, weights, front, head, tail, end)

        @block.tensor
        def _(pe):
            mm = nc.tensor.matmul

            def transpose(dst, src, idt=None):
                k = src.shape[0]
                idt = ident if idt is None else idt
                return nc.tensor.transpose(dst, src, idt[0:k, 0:k])

            def fill(last):
                last.then_inc(filled, 1)

            pe.wait_ge(w_attn, 16 * N_ATTN)
            for c in range(3):
                transpose(ring[0][:, c * P:(c + 1) * P], y[:, c, :])
                transpose(ring[0][:, (3 + c) * P:(4 + c) * P], yb[:, c, :])
            transpose(ring[0][:, 6 * P:7 * P], y[:, 3, :])
            fill(transpose(ring[0][:, 7 * P:8 * P], yb[:, 3, :]))
            pe.wait_ge(prep_a, 1)

            def weights():
                yield ("w", "guT")
                i = FIRST.slot(("w", "guT"))
                for slot, count in FIRST.needs(0, [], ("w", "guT")):
                    pe.wait_ge(freed[slot], count)
                pe.wait_ge(w_rest, 16 * N_REST)
                pe.wait_ge(fq_q, 1)
                for s in range(2):
                    for c, (c0, cw) in enumerate(ICH):
                        last = transpose(ring[i][:, 512 * s + c0:512 * s + c0 + cw], hw[0:cw, (3 * s + c) * D:(3 * s + c + 1) * D])
                fill(last)
                yield ("w", "dT")
                i = FIRST.slot(("w", "dT"))
                for slot, count in FIRST.needs(0, [], ("w", "dT")):
                    pe.wait_ge(freed[slot], count)
                for c, (c0, cw) in enumerate(ICH):
                    last = transpose(ring[i][0:cw, c * P:(c + 1) * P], hw[:, 768 + c0:768 + c0 + cw])
                fill(last)

            def front(seg, turn, n):
                def claim(*name, after=()):
                    for slot, count in seg.needs(turn, after, name):
                        pe.wait_ge(freed[slot], count)
                    return ring[seg.slot(name)]

                def extra(o, m, h, q, k, swap):
                    j, b = (h // 2) % 4, h // 8
                    rows = slice(32 * j, 32 * j + 32)
                    one, two = (alibi_xk[rows, b, k], alibi_xq[rows, b, q])
                    mm(o[:, m * S:(m + 1) * S], one, two, start=False, stop=False)

                def diagonal(o, m, h, t, parts):
                    for k in range(parts):
                        block_ = 4 * (h // 2) + (h % 2) * (1 + k)
                        last = mm(o[:, m * S + t * P:m * S + (t + 1) * P], identb[:], alibi_d[:, block_, :], start=False, stop=k == parts - 1)
                    return last

                def scores1(a, g, t, pr):
                    o = claim(a, "s1", g, t, pr, after=[(a, "qkT", g)] if t == pr == 0 else [])
                    for m in range(2):
                        rows = slice(64 * m, 64 * m + ROWS[a])
                        last = mm(o[:, m * S:(m + 1) * S], qkT[rows, g, pr, 0, t * P:(t + 1) * P],
                                  qkT[rows, g, pr, 1, :], start=True, stop=a == 1)
                    if a == 0:
                        for m in range(2):
                            last = diagonal(o, m, 4 * g + 2 * pr + m, t, 1)
                    fill(last)

                def scores2(a, g, t, pr):
                    o = claim(a, "s2", g, t, pr, after=[(a, "mT", g)] if t == pr == 0 else [])
                    for m in range(2):
                        rows = slice(64 * m, 64 * m + ROWS[a])
                        last = mm(o[:, m * S:(m + 1) * S], qkT[rows, g, pr, 1, t * P:(t + 1) * P], qmT[rows, g % 2, pr, :], start=True, stop=a == 1)
                    if a == 0:
                        h = 4 * g + 2 * pr
                        extra(o, 1, h + 1, slice(0, S), slice(t * P, (t + 1) * P), False)
                        diagonal(o, 0, h, t, 1)
                        last = diagonal(o, 1, h + 1, t, 3)
                    fill(last)

                def weighted(a, g, t):
                    k = 8 * g + 2 * t
                    for slot, count in seg.needs(turn, [(a, "s2", g, t, pr) for pr in range(2)]):
                        pe.wait_ge(freed[slot], count)
                    for j in range(4):
                        last = mm(pv_bank[g % 2][32 * j:32 * j + 32, :], v_aug[:, t, 4 * g + j, :], prob[:, (k + j // 2) % 4, j % 2, :],
                                  start=t == 0, stop=t == T - 1)
                    last.then_inc(pv_done, 1)

                def attention(a):
                    yield (a, "xT")
                    o = claim(a, "xT")
                    src = (x_next, x)[a]
                    if a == 0:
                        pe.wait_ge(x_in, n * 16 + 16)
                    else:
                        pe.wait_ge(x_ready, n * 3 + 2)
                    for t in range(T):
                        last = transpose(o[:, t * P:(t + 1) * P], src[:, t, :])
                    fill(last)
                    for i in range(2):
                        yield (a, "qkv", i)
                        o = claim(a, "qkv", i, after=[(a, "xT")])
                        for b in range(2):
                            t = 2 * i + b
                            last = mm(o[:, 512 * b:512 * b + 3 * D], xT[:, t * P:(t + 1) * P], wqkvT[:, a, :], start=True, stop=True)
                        fill(last)
                    for g in range(QUADS):
                        yield (a, "qkT", g)
                        if g == 0:
                            pe.wait_ge(aug_a, n * 2 + a + 1)
                            pe.wait_ge(aug_v, n * 2 + a + 1)
                            if seg is FIRST and a == 0:
                                pe.wait_ge(w_alibi, 16 * 3)
                        o = claim(a, "qkT", g)[:].bitcast(BF16)
                        for pr in range(2):
                            for side in range(2):
                                for t in range(T):
                                    c = (2 * pr + side) * S + t * P
                                    h0 = 4 * g + 2 * pr
                                    last = transpose(o[:, c:c + P], aug[:, side, t, h0:h0 + 2, :].rearrange("p h s -> p (h s)"), identb)
                        fill(last)
                    late = None
                    for kind, i in attention_order():
                        yield (a, kind) + i
                        if kind == "s1":
                            scores1(a, *i)
                        elif kind == "mT":
                            g, = i
                            o = claim(a, "mT", g)[:, 0:512].bitcast(BF16)
                            pe.wait_ge(maxq_ready, n * 8 + a * 4 + g + 1)
                            for pr in range(2):
                                for t in range(T):
                                    c, h0 = pr * S + t * P, 4 * g + 2 * pr
                                    last = transpose(o[:, c:c + P], aug[:, 0, t, h0:h0 + 2, :].rearrange("p h s -> p (h s)"), identb)
                            fill(last)
                        elif kind == "s2":
                            g, t, pr = i
                            scores2(a, *i)
                            if pr == 0 and late is not None:
                                weighted(a, *late)
                                late = None
                            if pr == 1:
                                late = (g, t)
                        elif kind == "oT":
                            g, = i
                            if g == QUADS - 1:
                                weighted(a, *late)
                            o = claim(a, "oT", g)
                            pe.wait_ge(oT_ready, n * 8 + a * 4 + g + 1)
                            for t in range(T):
                                last = transpose(o[:, t * P:(t + 1) * P], oT[:, g % 2, t * P:(t + 1) * P])
                            fill(last)
                    yield (a, "aT")
                    o = claim(a, "aT", after=[(a, "oT", g) for g in range(QUADS)])
                    for t in range(T):
                        last = transpose(o[:, t * P:(t + 1) * P], att[:, t, :])
                    fill(last)
                    yield (a, "proj")
                    o = claim(a, "proj", after=[(a, "aT")])
                    for t in range(T):
                        last = mm(o[:, t * D:(t + 1) * D], attT[:, t * P:(t + 1) * P], woT[:, a, :], start=True, stop=True)
                    fill(last)

                yield from attention(0)
                yield ("f", "xqT")
                o = claim("f", "xqT")
                pe.wait_ge(wT_ready, 1)
                pe.wait_ge(fq_q, n * 3 + 2)
                for t in range(T):
                    last = transpose(o[:, t * P:(t + 1) * P], h4[:, t * D:(t + 1) * D])
                fill(last)
                for t in range(T):
                    yield ("f", "gu", t)
                    o = claim("f", "gu", t, after=[("f", "xqT")])
                    for s in range(2):
                        last = mm(o[:, 512 * s:512 * s + INTER], xT[:, t * P:(t + 1) * P], wguT[:, s, :], start=True, stop=True)
                    fill(last)
                for c, (c0, cw) in enumerate(ICH):
                    yield ("f", "hT", c)
                    o = claim("f", "hT", c)
                    pe.wait_ge(fq_q, n * 3 + 4)
                    for t in range(T):
                        last = transpose(o[0:cw, t * P:(t + 1) * P], h4[:, t * INTER + c0:t * INTER + c0 + cw])
                    fill(last)
                yield ("f", "down")
                o = claim("f", "down")
                pe.wait_ge(hqT_ready, n + 1)
                for t in range(T):
                    for c, (c0, cw) in enumerate(ICH):
                        last = mm(o[:, t * D:(t + 1) * D], hqT[0:cw, c, t * P:(t + 1) * P], wdT[0:cw, c, :], start=c == 0, stop=c == 2)
                fill(last)
                yield from attention(1)

            def claiming(seg, turn):
                def claim(*name, after=()):
                    for slot, count in seg.needs(turn, after, name):
                        pe.wait_ge(freed[slot], count)
                    return ring[seg.slot(name)]
                return claim

            def head(seg, turn, n, l):
                claim = claiming(seg, turn)
                L = ("l", l)
                yield (*L, "xT")
                o = claim(*L, "xT", after=[("l", 0, "w2")] if l else [])
                if l == 0:
                    pe.wait_ge(x_ready, n * 3 + 3)
                for t in range(T):
                    last = transpose(o[:, t * P:(t + 1) * P], (x, yb)[l][:, t, :])
                fill(last)
                for kind, t in LOCAL_FRONT:
                    if kind == "ro":
                        continue
                    yield (*L, kind, t)
                    o = claim(*L, kind, t)
                    pe.wait_ge(xTb_ready, n * 4 + 2 * l + 1)
                    if kind == "qk":
                        for s in range(2):
                            last = mm(o[:, 512 * s:512 * s + 512], xTb[:, t * P:(t + 1) * P], wl_qkv[:, l, 512 * s:512 * s + 512], start=True, stop=True)
                    elif kind == "v":
                        for b in range(2):
                            last = mm(o[:, 512 * b:512 * b + 512], xTb[:, (2 * t + b) * P:(2 * t + b + 1) * P], wl_qkv[:, l, 1024:1536], start=True, stop=True)
                    else:
                        pe.wait_ge(lrot_ready, n * 8 + l * 4 + t + 1)
                        for c in range(8):
                            last = transpose(o[:, c * P:(c + 1) * P], lrs[:, t % 2, c // 4, 2 * (c % 4):2 * (c % 4) + 2, :].rearrange("p h d -> p (h d)"))
                    fill(last)

            def tail(seg, turn, n, l):
                claim = claiming(seg, turn)
                L = ("l", l)
                for kind, t, *q in local_order():
                    yield (*L, kind, t, *q)
                    if kind == "s":
                        q, w = q[0], BAND if t else P
                        if t == q == 0:
                            pe.wait_ge(lhead_ready, n * 2 + l + 1)
                        o = claim(*L, "s", t, q)
                        for u in range(2):
                            part = lambda m, c0, c1: o[:, 512 * m + BAND * u + c0:512 * m + BAND * u + c1]
                            for m in range(2):
                                mm(part(m, 0, w), identb[:], band_q[:, 0:w], start=True, stop=False)
                            for m in range(2):
                                rows, pr = slice(64 * m, 64 * m + 64), 2 * q + u
                                queries = lqkT[rows, pr, t * P:(t + 1) * P]
                                last = mm(part(m, 0, P), queries, lqkT[rows, 4 + pr, t * P:(t + 1) * P], start=False, stop=t == 0)
                                if t:
                                    last = mm(part(m, P, BAND), queries, lqkT[rows, 4 + pr, t * P - WIN:t * P], start=False, stop=True)
                    elif kind == "own":
                        o = claim(*L, "own", t)
                        pe.wait_ge(lnorm_ready, n * 16 + l * 8 + 2 * t + 2)
                        for h in range(LH):
                            last = transpose(o[:, h * P:(h + 1) * P], lprob[:, t % 2, h, 0:P])
                    elif kind == "prev":
                        o = claim(*L, "prev", t)
                        for h in range(LH):
                            last = transpose(o[:, h * P:(h + 1) * P], lprob[:, t % 2, h, BAND - P:BAND])
                    else:
                        o = claim(*L, "pv", t, after=[(*L, "own", t)] + [(*L, "prev", t)][:t])
                        for c in range(4):
                            for m in range(2):
                                last = mm(o[64 * m:64 * m + 64, c * P:(c + 1) * P], lv[:, t, 2 * c + m, :], lown[:, 2 * c + m, :],
                                          start=True, stop=t == 0)
                            for m in range(2 if t else 0):
                                last = mm(o[64 * m:64 * m + 64, c * P:(c + 1) * P], lv[WIN:P, t - 1, 2 * c + m, :], lprev[WIN:P, 2 * c + m, :],
                                          start=False, stop=True)
                    fill(last)
                for i in range(2):
                    yield (*L, "wo", i)
                    o = claim(*L, "wo", i, after=[(*L, "pv", t) for t in range(2 * i + 2)])
                    for b in range(2):
                        t = 2 * i + b
                        for c in range(4):
                            last = mm(o[:, b * D:(b + 1) * D], loT[:, c, t * P:(t + 1) * P], wl_o[:, l, c, :], start=c == 0, stop=c == 3)
                    fill(last)
                yield (*L, "x2T")
                o = claim(*L, "x2T", after=[(*L, "wo", i) for i in range(2)])
                for t in range(T):
                    last = transpose(o[:, t * P:(t + 1) * P], yb[:, t, :])
                fill(last)
                yield (*L, "hB")
                o = claim(*L, "hB")
                pe.wait_ge(xTb_ready, n * 4 + 2 + 2 * l)
                for t in range(T):
                    last = transpose(o[:, t * P:(t + 1) * P], xTb[:, t * P:(t + 1) * P])
                fill(last)
                yield (*L, "hT")
                o = claim(*L, "hT")
                pe.wait_ge(h_back, n * 2 + l + 1)
                for t in range(T):
                    last = transpose(o[:, t * P:(t + 1) * P], hn[:, t, :])
                fill(last)
                for c, (c0, cw) in enumerate(HCH):
                    yield (*L, "w1", c)
                    o = claim(*L, "w1", c, after=[(*L, "hT")])
                    for s in range(2):
                        last = mm(o[0:cw, 512 * s:512 * s + 512], w1[:, l, s * HID + c0:s * HID + c0 + cw], xTb[:], start=True, stop=True)
                    fill(last)
                yield (*L, "w2")
                o = claim(*L, "w2")
                pe.wait_ge(hid_ready, n * 2 + l + 1)
                for t in range(T):
                    for c, (c0, cw) in enumerate(HCH):
                        last = mm(o[:, t * D:(t + 1) * D], hid[0:cw, c, t * P:(t + 1) * P], w2[0:cw, l, c, :], start=c == 0, stop=c == 2)
                fill(last)

            def end(seg, turn, n):
                yield from ()

            program(pe, weights, front, head, tail, end)


def constants():
    import numpy as np
    bf = mybir.dt.np(BF16)
    f32 = np.float32

    def parts(v):
        v = np.asarray(v, f32)
        out = []
        for _ in range(3):
            p = v.astype(bf)
            out.append(p)
            v = v - p.astype(f32)
        return out

    slopes = (2.0 ** (8.0 * np.arange(0, -H, -1, dtype=f32) / H)).astype(f32)
    pos = np.arange(S)
    tile, centred = pos // P, (pos - S // 2).astype(f32)
    alibi_b = np.zeros((P, 2, T, H, 2 * T), f32)
    alibi_xq, alibi_xk = np.zeros((P, 2, S), f32), np.zeros((P, 2, S), f32)
    alibi_d = np.zeros((P, 4 * PAIRS, P), bf)
    within = np.arange(P)
    dist = np.abs(within[:, None] - within[None, :]).astype(f32)
    rows = lambda v: v.reshape(T, P).T
    for h in range(H):
        for i, s in enumerate(parts(slopes[h])):
            s = float(s)
            for c in range(T):
                sign = np.sign(tile - c).astype(f32)
                here = (tile == c).astype(f32)
                if i == 0:
                    alibi_b[:, 0, :, h, 2 * c], alibi_b[:, 1, :, h, 2 * c] = rows(sign * centred), rows(-s * here)
                    alibi_b[:, 0, :, h, 2 * c + 1], alibi_b[:, 1, :, h, 2 * c + 1] = rows(sign * s), rows(centred * here)
                elif h % 2:
                    row, b = 32 * ((h // 2) % 4) + 4 * c + 2 * (i - 1), h // 8
                    alibi_xq[row, b], alibi_xk[row, b] = sign * centred, -s * here
                    alibi_xq[row + 1, b], alibi_xk[row + 1, b] = sign * s, centred * here
        for i, p in enumerate(parts(-slopes[h] * dist)):
            if h % 2:
                alibi_d[:, 4 * (h // 2) + 1 + i, :] = p
            elif i == 0:
                alibi_d[:, 4 * (h // 2), :] = p
    band = np.arange(BAND)
    key = np.where(band < P, band, band - BAND)
    gap_q = within[:, None] - key[None, :]
    mask = lambda gap: np.where((gap >= 0) & (gap <= WIN), 0.0, -1e30).astype(bf)
    half = np.arange(0, LD, 2, dtype=f32)
    inv = (1.0 / 10000.0 ** (half / LD)).astype(f32)
    t = np.arange(S, dtype=f32)
    freqs = np.tile(t[:, None] * inv[None, :], (1, 2))
    base = ((half + 0.4 * LD) / (1.4 * LD)).astype(f32)
    scale = np.tile(base[None, :] ** ((t - S // 2) / f32(WIN // 2))[:, None], (1, 2)).astype(f32)
    sign = np.where(np.arange(LD) < LD // 2, -1.0, 1.0).astype(f32)
    lay = lambda q, k: np.ascontiguousarray(np.stack([q, k], 1).reshape(T, P, 2, LD).transpose(1, 0, 2, 3).astype(f32))
    cos, sin = np.cos(freqs).astype(f32), np.sin(freqs).astype(f32)
    return {
        "ident": np.eye(P, dtype=f32), "identb": np.eye(P).astype(bf),
        "alibi_b": alibi_b.reshape(P, -1).astype(bf), "alibi_d": alibi_d,
        "alibi_xq": alibi_xq.astype(bf), "alibi_xk": alibi_xk.astype(bf),
        "band_q": mask(gap_q),
        "rot_c": lay(cos * scale * 8, cos / scale), "rot_s": lay(sign * sin * scale * 8, sign * sin / scale),
    }


NAMES = {
    "x": "L0_attn_x", "wqkv0": "L0_attn_W_qkv", "bqkv0": "L0_attn_b_qkv", "wo0": "L0_attn_W_out", "bo0": "L0_attn_b_out",
    "wgate": "L0_ffn_w_gate", "wup": "L0_ffn_w_up", "wdown": "L0_ffn_w_down",
    "wqkv1": "L1_attn_W_qkv", "bqkv1": "L1_attn_b_qkv", "wo1": "L1_attn_W_proj", "bo1": "L1_attn_b_proj",
    "wl_qkv": "L1_ffn_wqkv", "q_scale": "L1_ffn_q_scale", "k_scale": "L1_ffn_k_scale", "wl_o": "L1_ffn_wo",
    "ln_g": "L1_ffn_ln_g", "ln_b": "L1_ffn_ln_b", "w1": "L1_ffn_w1", "b1": "L1_ffn_b1", "w2": "L1_ffn_w2", "b2": "L1_ffn_b2",
}


def kernel(**inputs):
    import concourse.bacc as bacc
    import numpy as np
    from concourse.bass_utils import run_bass_kernel_spmd

    nc = bacc.Bacc("TRN2", target_bir_lowering=False, num_devices=1)
    arrays = {k: np.ascontiguousarray(inputs[v]) for k, v in NAMES.items()} | constants()
    ins = {k: nc.dram_tensor(f"in_{k}", a.shape, mybir.dt.from_np(a.dtype), kind="ExternalInput").ap() for k, a in arrays.items()}
    out = nc.dram_tensor("out", (SEQS, S, D), F32, kind="ExternalOutput").ap()
    build(nc, ins, out)
    r = run_bass_kernel_spmd(nc, [{f"in_{k}": a for k, a in arrays.items()}], core_ids=[0])
    return r.results[0]["out"]
```
